# Optimizing a Trainium2 kernel written in Bass

```python
import numpy as np
import jax
import jax.numpy as jnp

def _softmax(x, axis=-1):
    return jax.nn.softmax(x, axis=axis)

def _gelu(x):
    return jax.nn.gelu(x, approximate=True)

def _silu(x):
    return jax.nn.silu(x)

def _sigmoid(x):
    return jax.nn.sigmoid(x)

def _layernorm(x, axis=-1, eps=1e-05):
    m = jnp.mean(x, axis=axis, keepdims=True)
    v = jnp.var(x, axis=axis, keepdims=True)
    return (x - m) / jnp.sqrt(v + eps)

def _scatter_add(tgt, idx, src, axis=0):
    return tgt.at[idx].add(src)

def _segment_sum(src, seg, n):
    return jax.ops.segment_sum(src, seg, n)
kernel_name = 'mk_gnn_resnorm_d4_gnn_r32_875133'

def setup_inputs(seed: int=0):
    np.random.seed(seed)
    _w = jnp.asarray

    def _rec_inputs():
        import jax
        import jax.numpy as jnp
        _gk = jax.random.key(seed)
        x = -0.000202 + 1 * jax.random.normal(jax.random.fold_in(_gk, 1), (3125, 128), jnp.float32)
        src = jax.random.randint(jax.random.fold_in(_gk, 2), (50000,), 0, 3125, jnp.int32)
        dst = jnp.minimum((3125 * jax.random.uniform(jax.random.fold_in(_gk, 3), (50000,)) ** 2.0).astype(jnp.int32), 99999)
        _o = jnp.argsort(dst, stable=True)
        src = src[_o]
        dst = dst[_o]
        edge_attr3_1x32 = jax.random.uniform(jax.random.fold_in(_gk, 12), (50000, 1, 32), jnp.float32, 0.0, 1)
        edge_type_3 = jax.random.randint(jax.random.fold_in(_gk, 14), (50000,), 0, 3, jnp.int32)
        edge_weight = jax.random.uniform(jax.random.fold_in(_gk, 15), (50000,), jnp.float32, 0.0, 0.999998)
        edge_weight1 = jax.random.uniform(jax.random.fold_in(_gk, 16), (50000, 1), jnp.float32, 0.0, 1)
        return (x, src, dst, edge_attr3_1x32, edge_type_3, edge_weight, edge_weight1)
    x, src, dst, edge_attr3_1x32, edge_type_3, edge_weight, edge_weight1 = _rec_inputs()

    def _L0_gnn_setup():
        import jax, jax.numpy as jnp
        import numpy as np
        N_NODES = 50000
        N_EDGES = 25000
        IN_FEATS = 128
        OUT_FEATS = 128
        N_REL = 3
        key = jax.random.key(seed)
        k1, k2, k3, k4, k5, k6 = jax.random.split(key, 6)
        feature = jax.random.normal(k1, (N_NODES, IN_FEATS), dtype=jnp.float32)
        bound = float(np.sqrt(6.0 / IN_FEATS))
        weight = jax.random.uniform(k2, (N_REL, IN_FEATS, OUT_FEATS), dtype=jnp.float32, minval=-bound, maxval=bound)
        norm = jax.random.uniform(k3, (N_EDGES,), dtype=jnp.float32)
        src = jax.random.randint(k4, (N_EDGES,), 0, N_NODES)
        dst = jax.random.randint(k5, (N_EDGES,), 0, N_NODES)
        rel_type = jax.random.randint(k6, (N_EDGES,), 0, N_REL)
        return {'feature': feature, 'weight': weight, 'norm': norm, 'src': src, 'dst': dst, 'rel_type': rel_type}
    _L0_gnn_all = _L0_gnn_setup()
    _L0_gnn_in = {k: v for k, v in _L0_gnn_all.items() if k in ('weight',)}
    del _L0_gnn_all

    def _L1_gnn_setup():
        import jax, jax.numpy as jnp
        import numpy as np
        import math
        N_NODES, N_EDGES, DIM, N_HEADS = (50000, 25000, 128, 8)
        D_K = DIM // N_HEADS
        key = jax.random.key(seed)
        ks = jax.random.split(key, 12)
        f32 = jnp.float32
        s = 1.0 / math.sqrt(DIM)
        return {'x': jax.random.normal(ks[0], (N_NODES, DIM), f32), 'src': jax.random.randint(ks[1], (N_EDGES,), 0, N_NODES), 'dst': jax.random.randint(ks[2], (N_EDGES,), 0, N_NODES), 'edge_weight': jax.random.normal(ks[3], (N_EDGES,), f32), 'Wk': jax.random.normal(ks[4], (DIM, DIM), f32) * s, 'bk': jax.random.normal(ks[5], (DIM,), f32) * 0.01, 'Wq': jax.random.normal(ks[6], (DIM, DIM), f32) * s, 'bq': jax.random.normal(ks[7], (DIM,), f32) * 0.01, 'Wv': jax.random.normal(ks[8], (DIM, DIM), f32) * s, 'bv': jax.random.normal(ks[9], (DIM,), f32) * 0.01, 'rel_att': jax.random.normal(ks[10], (N_HEADS, D_K), f32) * 0.1, 'rel_msg': jax.random.normal(ks[11], (N_HEADS, D_K, D_K), f32) / math.sqrt(D_K)}
    _L1_gnn_all = _L1_gnn_setup()
    _L1_gnn_in = {k: v for k, v in _L1_gnn_all.items() if k in ('Wk', 'bk', 'Wq', 'bq', 'Wv', 'bv', 'rel_att', 'rel_msg')}
    del _L1_gnn_all

    def _L2_gnn_setup():
        import jax, jax.numpy as jnp
        import numpy as np
        LOG2 = 0.6931471805599453

        def ssp(x):
            return jax.nn.softplus(x) - LOG2
        N_ATOMS = 3125
        N_PAIRS = 50000
        F_ATOM = 128
        F_FILT = 128
        N_RBF = 32
        key = jax.random.key(seed)
        ks = jax.random.split(key, 12)
        s = lambda k, fan_in, shape: jax.random.normal(k, shape, dtype=jnp.float32) / np.sqrt(fan_in)
        return {'x': jax.random.normal(ks[0], (N_ATOMS, F_ATOM), dtype=jnp.float32), 'pairlist': jax.random.randint(ks[1], (2, N_PAIRS), 0, N_ATOMS), 'f_ij': jax.random.uniform(ks[2], (N_PAIRS, 1, N_RBF), dtype=jnp.float32), 'f_ij_cutoff': jax.random.uniform(ks[3], (N_PAIRS, 1), dtype=jnp.float32), 'W_in': s(ks[4], F_ATOM, (F_ATOM, F_FILT)), 'Wf1': s(ks[5], N_RBF, (N_RBF, F_FILT)), 'bf1': jnp.zeros((F_FILT,), dtype=jnp.float32), 'Wf2': s(ks[6], F_FILT, (F_FILT, F_FILT)), 'bf2': jnp.zeros((F_FILT,), dtype=jnp.float32), 'Wo1': s(ks[7], F_FILT, (F_FILT, F_ATOM)), 'bo1': jnp.zeros((F_ATOM,), dtype=jnp.float32), 'Wo2': s(ks[8], F_ATOM, (F_ATOM, F_ATOM)), 'bo2': jnp.zeros((F_ATOM,), dtype=jnp.float32)}
    _L2_gnn_all = _L2_gnn_setup()
    _L2_gnn_in = {k: v for k, v in _L2_gnn_all.items() if k in ('W_in', 'Wf1', 'bf1', 'Wf2', 'bf2', 'Wo1', 'bo1', 'Wo2', 'bo2')}
    del _L2_gnn_all

    def _L3_gnn_setup():
        import jax, jax.numpy as jnp
        import numpy as np
        N = 1250
        E = 20000
        IN_DIM = 128
        OUT_DIM = 128
        HEADS = 4
        NEG_SLOPE = 0.01

        def lrelu(x):
            return jnp.where(x >= 0, x, NEG_SLOPE * x)

        def gat_layer(h, fc_W, attn_W, edge_w, m_w, src, dst, pd):
            n = h.shape[0]
            z = lrelu(h @ fc_W.T)
            d = z.shape[1]
            a_src = z @ attn_W[0, :d]
            a_dst = z @ attn_W[0, d:]
            a = a_src[src] + a_dst[dst]
            ev = pd[:, 0] * edge_w[0, 0]
            e = lrelu(a * ev)
            ne = e * m_w[0, 0]
            m = jax.ops.segment_max(ne, dst, num_segments=n)
            m = jnp.where(jnp.isfinite(m), m, 0.0)
            ex = jnp.exp(ne - m[dst])
            s = jax.ops.segment_sum(ex, dst, num_segments=n)
            denom = jnp.where(s > 0, s, 1.0)
            alpha = ex / denom[dst]
            return jax.ops.segment_sum(alpha[:, None] * z[src], dst, num_segments=n)

        def gru_cell(x, hprev, Wih, Whh, bih, bhh):
            gi = x @ Wih.T + bih
            gh = hprev @ Whh.T + bhh
            ir, iz, in_ = jnp.split(gi, 3, axis=1)
            hr, hz, hn = jnp.split(gh, 3, axis=1)
            r = jax.nn.sigmoid(ir + hr)
            zg = jax.nn.sigmoid(iz + hz)
            ng = jnp.tanh(in_ + r * hn)
            return (1.0 - zg) * ng + zg * hprev
        key = jax.random.key(seed)
        ks = jax.random.split(key, 16)
        sc = 0.05
        inp = {'h': jax.random.normal(ks[0], (N, IN_DIM), jnp.float32), 'pd': jax.random.uniform(ks[1], (E, 1), jnp.float32), 'src': jax.random.randint(ks[2], (E,), 0, N, jnp.int32), 'dst': jax.random.randint(ks[3], (E,), 0, N, jnp.int32), 'fc_W': jax.random.normal(ks[4], (HEADS, OUT_DIM, IN_DIM), jnp.float32) * sc, 'attn_W': jax.random.normal(ks[5], (HEADS, 1, 2 * OUT_DIM), jnp.float32) * sc, 'edge_w': jax.random.normal(ks[6], (HEADS, 1, 1), jnp.float32) * sc + 1.0, 'm_w': jax.random.normal(ks[7], (HEADS, 1, 1), jnp.float32) * sc + 1.0, 'out_fc_W': jax.random.normal(ks[8], (OUT_DIM, HEADS * OUT_DIM), jnp.float32) * sc, 'out_attn_W': jax.random.normal(ks[9], (1, 2 * OUT_DIM), jnp.float32) * sc, 'out_edge_w': jax.random.normal(ks[10], (1, 1), jnp.float32) * sc + 1.0, 'out_m_w': jax.random.normal(ks[11], (1, 1), jnp.float32) * sc + 1.0, 'gru_Wih': jax.random.normal(ks[12], (3 * OUT_DIM, OUT_DIM), jnp.float32) * sc, 'gru_Whh': jax.random.normal(ks[13], (3 * OUT_DIM, OUT_DIM), jnp.float32) * sc, 'gru_bih': jax.random.normal(ks[14], (3 * OUT_DIM,), jnp.float32) * sc, 'gru_bhh': jax.random.normal(ks[15], (3 * OUT_DIM,), jnp.float32) * sc}
        return inp
    _L3_gnn_all = _L3_gnn_setup()
    _L3_gnn_in = {k: v for k, v in _L3_gnn_all.items() if k in ('fc_W', 'attn_W', 'edge_w', 'm_w', 'out_fc_W', 'out_attn_W', 'out_edge_w', 'out_m_w', 'gru_Wih', 'gru_Whh', 'gru_bih', 'gru_bhh')}
    del _L3_gnn_all
    return {'x': x, 'src': src, 'dst': dst, 'edge_attr3_1x32': edge_attr3_1x32, 'edge_type_3': edge_type_3, 'edge_weight': edge_weight, 'edge_weight1': edge_weight1, 'L0_gnn_weight': _L0_gnn_in['weight'], 'L1_gnn_Wk': _L1_gnn_in['Wk'], 'L1_gnn_bk': _L1_gnn_in['bk'], 'L1_gnn_Wq': _L1_gnn_in['Wq'], 'L1_gnn_bq': _L1_gnn_in['bq'], 'L1_gnn_Wv': _L1_gnn_in['Wv'], 'L1_gnn_bv': _L1_gnn_in['bv'], 'L1_gnn_rel_att': _L1_gnn_in['rel_att'], 'L1_gnn_rel_msg': _L1_gnn_in['rel_msg'], 'L2_gnn_W_in': _L2_gnn_in['W_in'], 'L2_gnn_Wf1': _L2_gnn_in['Wf1'], 'L2_gnn_bf1': _L2_gnn_in['bf1'], 'L2_gnn_Wf2': _L2_gnn_in['Wf2'], 'L2_gnn_bf2': _L2_gnn_in['bf2'], 'L2_gnn_Wo1': _L2_gnn_in['Wo1'], 'L2_gnn_bo1': _L2_gnn_in['bo1'], 'L2_gnn_Wo2': _L2_gnn_in['Wo2'], 'L2_gnn_bo2': _L2_gnn_in['bo2'], 'L3_gnn_fc_W': _L3_gnn_in['fc_W'], 'L3_gnn_attn_W': _L3_gnn_in['attn_W'], 'L3_gnn_edge_w': _L3_gnn_in['edge_w'], 'L3_gnn_m_w': _L3_gnn_in['m_w'], 'L3_gnn_out_fc_W': _L3_gnn_in['out_fc_W'], 'L3_gnn_out_attn_W': _L3_gnn_in['out_attn_W'], 'L3_gnn_out_edge_w': _L3_gnn_in['out_edge_w'], 'L3_gnn_out_m_w': _L3_gnn_in['out_m_w'], 'L3_gnn_gru_Wih': _L3_gnn_in['gru_Wih'], 'L3_gnn_gru_Whh': _L3_gnn_in['gru_Whh'], 'L3_gnn_gru_bih': _L3_gnn_in['gru_bih'], 'L3_gnn_gru_bhh': _L3_gnn_in['gru_bhh']}

def reference(x, src, dst, edge_attr3_1x32, edge_type_3, edge_weight, edge_weight1, L0_gnn_weight, L1_gnn_Wk, L1_gnn_bk, L1_gnn_Wq, L1_gnn_bq, L1_gnn_Wv, L1_gnn_bv, L1_gnn_rel_att, L1_gnn_rel_msg, L2_gnn_W_in, L2_gnn_Wf1, L2_gnn_bf1, L2_gnn_Wf2, L2_gnn_bf2, L2_gnn_Wo1, L2_gnn_bo1, L2_gnn_Wo2, L2_gnn_bo2, L3_gnn_fc_W, L3_gnn_attn_W, L3_gnn_edge_w, L3_gnn_m_w, L3_gnn_out_fc_W, L3_gnn_out_attn_W, L3_gnn_out_edge_w, L3_gnn_out_m_w, L3_gnn_gru_Wih, L3_gnn_gru_Whh, L3_gnn_gru_bih, L3_gnn_gru_bhh):
    import jax
    import jax.numpy as jnp

    def _L0_gnn_ref(feature, weight, norm, src, dst, rel_type):
        import jax, jax.numpy as jnp
        import numpy as np
        N_NODES = 50000
        N_EDGES = 25000
        IN_FEATS = 128
        OUT_FEATS = 128
        N_REL = 3
        hr = jnp.einsum('ni,rio->rno', feature, weight)
        msg = hr[rel_type, src] * norm[:, None]
        h = jax.ops.segment_sum(msg, dst, num_segments=feature.shape[0])
        return jax.nn.relu(h)

    def _L1_gnn_ref(x, src, dst, edge_weight, Wk, bk, Wq, bq, Wv, bv, rel_att, rel_msg):
        import jax, jax.numpy as jnp
        import numpy as np
        import math
        N_NODES, N_EDGES, DIM, N_HEADS = (50000, 25000, 128, 8)
        D_K = DIM // N_HEADS
        N, D = x.shape
        H, dk = rel_att.shape
        inv_sqrt_dk = jnp.asarray(1.0 / math.sqrt(dk), x.dtype)
        k = (x @ Wk.T + bk).reshape(N, H, dk)
        q = (x @ Wq.T + bq).reshape(N, H, dk)
        v = (x @ Wv.T + bv).reshape(N, H, dk)
        qp = edge_weight[:, None, None] * rel_att[None]
        att = ((q[dst] + qp) * k[src]).sum(-1) * inv_sqrt_dk
        val = jnp.einsum('ehd,hdk->ehk', v[src], rel_msg)
        m = jax.ops.segment_max(att, dst, num_segments=N)
        e = jnp.exp(att - m[dst])
        s = jax.ops.segment_sum(e, dst, num_segments=N)
        w = e / s[dst]
        h = jax.ops.segment_sum(w[..., None] * val, dst, num_segments=N)
        return jax.nn.relu(h.reshape(N, D))

    def _L2_gnn_ref(x, pairlist, f_ij, f_ij_cutoff, W_in, Wf1, bf1, Wf2, bf2, Wo1, bo1, Wo2, bo2):
        import jax, jax.numpy as jnp
        import numpy as np
        LOG2 = 0.6931471805599453

        def ssp(x):
            return jax.nn.softplus(x) - LOG2
        N_ATOMS = 3125
        N_PAIRS = 50000
        F_ATOM = 128
        F_FILT = 128
        N_RBF = 32
        idx_i, idx_j = (pairlist[0], pairlist[1])
        h = x @ W_in
        W_ij = ssp(f_ij[:, 0, :] @ Wf1 + bf1) @ Wf2 + bf2
        W_ij = W_ij * f_ij_cutoff
        x_ij = h[idx_j] * W_ij
        out = jax.ops.segment_sum(x_ij, idx_i, num_segments=x.shape[0])
        return ssp(out @ Wo1 + bo1) @ Wo2 + bo2

    def _L3_gnn_ref(h, pd, fc_W, attn_W, edge_w, m_w, out_fc_W, out_attn_W, out_edge_w, out_m_w, gru_Wih, gru_Whh, gru_bih, gru_bhh, src, dst):
        import jax, jax.numpy as jnp
        import numpy as np
        N = 1250
        E = 20000
        IN_DIM = 128
        OUT_DIM = 128
        HEADS = 4
        NEG_SLOPE = 0.01

        def lrelu(x):
            return jnp.where(x >= 0, x, NEG_SLOPE * x)

        def gat_layer(h, fc_W, attn_W, edge_w, m_w, src, dst, pd):
            n = h.shape[0]
            z = lrelu(h @ fc_W.T)
            d = z.shape[1]
            a_src = z @ attn_W[0, :d]
            a_dst = z @ attn_W[0, d:]
            a = a_src[src] + a_dst[dst]
            ev = pd[:, 0] * edge_w[0, 0]
            e = lrelu(a * ev)
            ne = e * m_w[0, 0]
            m = jax.ops.segment_max(ne, dst, num_segments=n)
            m = jnp.where(jnp.isfinite(m), m, 0.0)
            ex = jnp.exp(ne - m[dst])
            s = jax.ops.segment_sum(ex, dst, num_segments=n)
            denom = jnp.where(s > 0, s, 1.0)
            alpha = ex / denom[dst]
            return jax.ops.segment_sum(alpha[:, None] * z[src], dst, num_segments=n)

        def gru_cell(x, hprev, Wih, Whh, bih, bhh):
            gi = x @ Wih.T + bih
            gh = hprev @ Whh.T + bhh
            ir, iz, in_ = jnp.split(gi, 3, axis=1)
            hr, hz, hn = jnp.split(gh, 3, axis=1)
            r = jax.nn.sigmoid(ir + hr)
            zg = jax.nn.sigmoid(iz + hz)
            ng = jnp.tanh(in_ + r * hn)
            return (1.0 - zg) * ng + zg * hprev
        gru_in = h
        heads = [gat_layer(h, fc_W[i], attn_W[i], edge_w[i], m_w[i], src, dst, pd) for i in range(HEADS)]
        x = lrelu(jnp.concatenate(heads, axis=1))
        x = lrelu(gat_layer(x, out_fc_W, out_attn_W, out_edge_w, out_m_w, src, dst, pd))
        x = lrelu(gru_cell(x, gru_in, gru_Wih, gru_Whh, gru_bih, gru_bhh))
        return x
    edge_index = jnp.stack([src, dst])
    x = _layernorm(x + _L0_gnn_ref(x, L0_gnn_weight, edge_weight, src, dst, edge_type_3), axis=-1)
    x = _layernorm(x + _L1_gnn_ref(x, src, dst, edge_weight, L1_gnn_Wk, L1_gnn_bk, L1_gnn_Wq, L1_gnn_bq, L1_gnn_Wv, L1_gnn_bv, L1_gnn_rel_att, L1_gnn_rel_msg), axis=-1)
    x = _layernorm(x + _L2_gnn_ref(x, edge_index, edge_attr3_1x32, edge_weight1, L2_gnn_W_in, L2_gnn_Wf1, L2_gnn_bf1, L2_gnn_Wf2, L2_gnn_bf2, L2_gnn_Wo1, L2_gnn_bo1, L2_gnn_Wo2, L2_gnn_bo2), axis=-1)
    x = _layernorm(x + _L3_gnn_ref(x, edge_weight1, L3_gnn_fc_W, L3_gnn_attn_W, L3_gnn_edge_w, L3_gnn_m_w, L3_gnn_out_fc_W, L3_gnn_out_attn_W, L3_gnn_out_edge_w, L3_gnn_out_m_w, L3_gnn_gru_Wih, L3_gnn_gru_Whh, L3_gnn_gru_bih, L3_gnn_gru_bhh, src, dst), axis=-1)
    return x

_drawn_inputs = setup_inputs


def setup_inputs(seed=0):
    import zlib

    import numpy as np

    out = dict(_drawn_inputs(seed))
    spreads = {'L2_gnn_bf1': (0.0, 0.1),
     'L2_gnn_bf2': (0.0, 0.1),
     'L2_gnn_bo1': (0.0, 0.1),
     'L2_gnn_bo2': (0.0, 0.1)}
    factors = {'L1_gnn_bk': 64.0,
     'L1_gnn_bq': 8.0,
     'L1_gnn_bv': 6.394,
     'L1_gnn_rel_att': 4.116,
     'L3_gnn_fc_W': 8.0,
     'L3_gnn_attn_W': 8.0,
     'L3_gnn_edge_w': 64.0,
     'L3_gnn_m_w': 64.0,
     'L3_gnn_out_attn_W': 8.0,
     'L3_gnn_gru_bih': 4.145,
     'L3_gnn_gru_bhh': 5.394}
    for name, (base, spread) in spreads.items():
        noise = np.random.default_rng([zlib.crc32(name.encode()), seed]).standard_normal(out[name].shape)
        drawn = base * np.exp(spread * noise) if base else spread * noise
        out[name] = jnp.asarray(drawn.astype(out[name].dtype))
    for name, factor in factors.items():
        out[name] = (out[name] * factor).astype(out[name].dtype)
    return out
```

```python
import concourse.bass as bass
from concourse import mybir
from contextlib import ExitStack, contextmanager

F32 = mybir.dt.float32
BF16 = mybir.dt.bfloat16
I32 = mybir.dt.int32
ALU = mybir.AluOpType
ACT = mybir.ActivationFunctionType
AX = mybir.AxisListType

P = 128
N_NODES, N_EDGES, D = 3125, 50000, 128
NB = -(-N_NODES // P)
NP = NB * P
TR = -(-N_EDGES // P)
LAST = N_EDGES - (TR - 1) * P
T = TR + NB
G = 8
STEPS = T // (2 * G)
H1, DK = 8, 16
H3 = 4
ZW = D + 1
CH = 16
CT = T // CH
SC = CT * P
FR = 36
BIG = 1.0e30
LOG2 = 0.6931471805599453
EPS = 1e-5
NBU, NBI = 5, 5
assert STEPS * 2 * G == T and NBU * NBI == NB and CH * CT == T and NP == NB * P


def gnn_program(nc, a, out):
    top = ExitStack()

    def dram(name, shape):
        return nc.dram_tensor(name, shape, F32, kind="Internal").ap()

    rec_d = dram("rec_d", (P * T, 8))
    rec_s = dram("rec_s", (P * T, FR))
    rec_tmp = dram("rec_tmp", (P * TR, 8))
    t_hr = dram("t_hr", (3 * NP, D))
    t_k = dram("t_k", (NP, D + H1))
    t_v = dram("t_v", (NP, D))
    t_h = dram("t_h", (NP, D))
    t_z = dram("t_z", (NP, H3 * ZW))
    t_as = dram("t_as", (NP, H3))
    t_zo = dram("t_zo", (NP, ZW))
    t_ao = dram("t_ao", (NP, H3))

    with top:
        def SB(stack, name, shape, dt=F32):
            return stack.enter_context(nc.sbuf_tensor(name, shape, dt))

        def PS(stack, name, shape, dt=F32):
            return stack.enter_context(nc.psum_tensor(name, shape, dt))

        phase_sems = []

        def sem(name):
            phase_sems.append(nc.alloc_semaphore(name))
            return phase_sems[-1]

        def end_phase():
            nc.clear_and_free_semaphores(list(phase_sems))
            phase_sems.clear()
            nc.all_engine_barrier()

        @contextmanager
        def phase():
            with nc.Block() as block:
                yield block
            end_phase()

        def move(dve, out_, in_):
            return dve.tensor_scalar(out_, in_, 1.0, None, ALU.mult)

        class Chain:

            def __init__(self, eng, name):
                self.eng, self.done, self.n, self.base = eng, sem(name), 0, 0

            def link(self, ins):
                self.n += 1
                ins.then_inc(self.done, 1)
                self.eng.wait_ge(self.done, self.base + self.n)

            @contextmanager
            def loop(self, lo, hi, per):
                before, self.n = self.n, 0
                with self.eng.Fori(lo, hi) as i:
                    self.base = (i - lo) * per + before
                    yield i
                    assert self.n == per, self.n
                self.base, self.n = 0, before + (hi - lo) * per

        def sb(name, shape, dt=F32):
            return SB(top, name, shape, dt)

        X = sb("X", [P, NB, D])
        iota_f = sb("iota_f", [P, P])
        iota_i = sb("iota_i", [P, P], I32)
        pid_i = sb("pid_i", [P, 1], I32)
        pid = sb("pid", [P, 3])
        ident = sb("ident", [P, P])
        below = sb("below", [P, P])
        above = sb("above", [P, P])
        tri_m1 = sb("tri_m1", [P, P], BF16)
        ones_bf = sb("ones_bf", [P, P], BF16)
        ones = sb("ones", [P, P])
        src_i = sb("src_i", [P, T], I32)
        hr_i = sb("hr_i", [P, T], I32)
        blk_i = sb("blk_i", [P, T], I32)
        dloc = sb("dloc", [P, T])
        ew = sb("ew", [P, T])
        ew1 = sb("ew1", [P, T])
        rs4 = sb("rs4", [P, T, 4])
        dst2_i = sb("dst2_i", [P, T], I32)
        sblk_i = sb("sblk_i", [P, T], I32)
        unsorted_i = sb("unsorted_i", [P, 1], I32)
        reset = sb("reset", [P, SC + 1])
        att = sb("att", [P, T, 8])

        def rank_vector(dve, c, s, key, place, align):
            link = c.link
            link(dve.memset(s["zero"][:], 0.0))
            link(dve.memset(s["base"][:], 0.0))
            link(dve.memset(place[:], 0.0))
            with c.loop(0, NB, 9 if align else 7) as b:
                link(dve.tensor_scalar(s["hit"][:], key[:], 0.0, None, ALU.is_equal))
                dve.sem_inc(s["hit_ready"], 1)
                link(dve.tensor_scalar(key[:], key[:], -1.0, None, ALU.add))
                dve.wait_ge(s["counted"], b + 1)
                link(dve.tensor_tensor_scan(s["run"][:], s["ps_tot"][:, 0:TR], s["zero"][:], s["base"][:, 0:1],
                                       ALU.add, ALU.add))
                link(dve.tensor_tensor(s["spot"][:], s["run"][:], s["ps_pre"][:, 0:TR], ALU.add))
                link(dve.tensor_tensor(s["spot"][:], s["spot"][:], s["hit"][:], ALU.mult))
                link(dve.tensor_tensor(place[:], place[:], s["spot"][:], ALU.add))
                if align:
                    link(dve.tensor_scalar(s["base_i"][:], s["run"][:, TR - 1:TR], float(P - 1), None, ALU.add))
                    link(dve.tensor_scalar(s["base_i"][:], s["base_i"][:], -P, None, ALU.bitwise_and))
                    link(dve.tensor_copy(s["base"][:], s["base_i"][:]))
                else:
                    link(dve.tensor_copy(s["base"][:], s["run"][:, TR - 1:TR]))

        def rank_tensor(pe, s):
            with pe.Fori(0, NB) as b:
                pe.wait_ge(s["hit_ready"], b + 1)
                pe.matmul(s["ps_pre"][:, 0:TR], lhsT=tri_m1[:], rhs=s["hit"][:], start=True, stop=True)
                pe.matmul(s["ps_tot"][:, 0:TR], lhsT=ones_bf[:], rhs=s["hit"][:],
                          start=True, stop=True).then_inc(s["counted"], 1)

        def place_to_row(dve, link, s, place, row, final):
            link(dve.tensor_copy(s["pl_i"][:], place[:]))
            link(dve.tensor_scalar(s["lo_i"][:], s["pl_i"][:], P - 1, None, ALU.bitwise_and))
            link(dve.tensor_scalar(s["pl_i"][:], s["pl_i"][:], 7, None, ALU.arith_shift_right))
            link(dve.tensor_copy(s["run"][:], s["lo_i"][:]))
            link(dve.tensor_copy(s["spot"][:], s["pl_i"][:]))
            if final:
                link(dve.memset(s["zero"][:], 0.0))
                for k in range(1, CH):
                    link(dve.scalar_tensor_tensor(s["zero"][:], s["spot"][:], float(CT * k), s["zero"][:],
                                             ALU.is_ge, ALU.add))
                link(dve.tensor_scalar(s["spot"][:], s["spot"][:], float(CH), None, ALU.mult))
                link(dve.scalar_tensor_tensor(s["spot"][:], s["zero"][:], float(1 - CH * CT), s["spot"][:],
                                         ALU.mult, ALU.add))
            link(dve.scalar_tensor_tensor(s["run"][:], s["run"][:], float(T if final else TR), s["spot"][:],
                                     ALU.mult, ALU.add))
            link(dve.tensor_copy(row[:], s["run"][:]))

        def rank_scratch(st, name):
            s = {"zero": SB(st, name + "_zero", [P, TR]), "base": SB(st, name + "_base", [P, 1]),
                 "base_i": SB(st, name + "_base_i", [P, 1], I32), "hit": SB(st, name + "_hit", [P, TR], BF16),
                 "run": SB(st, name + "_run", [P, TR]), "spot": SB(st, name + "_spot", [P, TR]),
                 "pl_i": SB(st, name + "_pl_i", [P, TR], I32), "lo_i": SB(st, name + "_lo_i", [P, TR], I32),
                 "ps_pre": PS(st, name + "_ps_pre", [P, 512]), "ps_tot": PS(st, name + "_ps_tot", [P, 512]),
                 "hit_ready": sem(name + "_hit_ready"), "counted": sem(name + "_counted")}
            return s

        SG = 13

        def scatter_pool(pool, s, rows, records, table):
            def half(i, h):
                pool.tensor_copy(s["idx"][:, h, :], rows[:, bass.ds(i * 2 * SG + h * SG, SG)])\
                    .then_inc(s["idx_ready"], 1)
                pool.tensor_copy(s["out"][:, h, :, :], records[:, bass.ds(i * 2 * SG + h * SG, SG), :])\
                    .then_inc(s["idx_ready"], 1)
                pool.wait_ge(s["idx_ready"], i * 4 + 2 * h + 2)
                pool.nop(nofuse=True)
                for u in range(SG):
                    pool.indirect_dma_start(
                        out=table, out_offset=bass.IndirectOffsetOnAxis(ap=s["idx"][:, h, u:u + 1], axis=0),
                        in_=s["out"][:, h, u, :],
                        in_offset=None).then_inc(s["written"][h], 16)
            for h in range(2):
                half(0, h)
            with pool.Fori(1, (TR - 1) // (2 * SG)) as i:
                for h in range(2):
                    pool.wait_ge(s["written"][h], i * (16 * SG))
                    half(i, h)
            for h in range(2):
                pool.wait_ge(s["written"][h], (TR - 1) // 2 * 16)
            pool.tensor_copy(s["idx"][:, 0, 0:1], rows[:, TR - 1:TR]).then_inc(s["idx_ready"], 1)
            pool.wait_ge(s["idx_ready"], (TR - 1) // SG * 2 + 1)
            pool.indirect_dma_start(
                out=table, out_offset=bass.IndirectOffsetOnAxis(ap=s["idx"][0:LAST, 0, 0:1], axis=0),
                in_=records[0:LAST, TR - 1, :], in_offset=None).then_inc(s["written"][0], 16)
            pool.wait_ge(s["written"][0], (TR - 1) // 2 * 16 + 16)

        def scatter_scratch(st, name, width):
            return {"out": SB(st, name + "_out", [P, 2, SG, width]), "idx": SB(st, name + "_idx", [P, 2, SG], I32), "idx_ready": sem(name + "_idx_ready"),
                    "written": [sem(name + f"_written{h}") for h in range(2)]}
        assert (TR - 1) % (2 * SG) == 0

        with ExitStack() as st:
            recs = SB(st, "recs", [P, TR, FR])
            recd = SB(st, "recd", [P, TR, 8])
            key_s = SB(st, "key_s", [P, TR])
            place_s = SB(st, "place_s", [P, TR])
            row_s = SB(st, "row_s", [P, TR], I32)
            key_d = SB(st, "key_d", [P, TR])
            place_d = SB(st, "place_d", [P, TR])
            row_d = SB(st, "row_d", [P, TR], I32)
            c_ready = sem("consts_ready")
            loaded = sem("edges_loaded")
            filled = sem("tables_filled")
            fill_ready = sem("fill_ready")
            with ExitStack() as s2:
                e_src = SB(s2, "e_src", [P, TR], I32)
                e_dst = SB(s2, "e_dst", [P, TR], I32)
                e_typ = SB(s2, "e_typ", [P, TR], I32)
                e_tmp = SB(s2, "e_tmp", [P, TR], I32)
                e_tf = SB(s2, "e_tf", [P, TR])
                e_w = SB(s2, "e_w", [P, 2, TR])
                d_line = SB(s2, "d_line", [P, TR + 1], I32)
                d_viol = SB(s2, "d_viol", [P, TR])
                viol = SB(s2, "viol", [P, 1])
                fill_d = SB(s2, "fill_d", [P, 8])
                fill_s = SB(s2, "fill_s", [P, FR])
                fill_dt = SB(s2, "fill_dt", [P, T, 8])
                fill_st = SB(s2, "fill_st", [P, 2 * G, FR])
                ps_v = PS(s2, "ps_v", [P, 512])
                viol_ready = sem("viol_ready")
                viol_sum = sem("viol_sum")
                with phase() as block:
                    @block.sync
                    def _(sp):
                        sp.dma_start(e_src[:], a["src"]).then_inc(loaded, 16)
                        sp.dma_start(e_dst[:], a["dst"]).then_inc(loaded, 16)
                        sp.dma_start(e_typ[:], a["typ"]).then_inc(loaded, 16)
                        sp.dma_start(e_w[:, 0, :], a["w"]).then_inc(loaded, 16)
                        sp.dma_start(e_w[:, 1, :], a["w1"]).then_inc(loaded, 16)
                        sp.dma_start(d_line[:], a["dst_line"]).then_inc(loaded, 16)
                        sp.dma_start(X[:], a["x"].rearrange("(b p) d -> p b d", p=P)).then_inc(loaded, 16)
                        sp.dma_start(recs[:, :, 0:32], a["f"]).then_inc(loaded, 16)
                        sp.wait_ge(fill_ready, 1)
                        sp.dma_start(rec_d.rearrange("(p t) f -> p (t f)", p=P),
                                     fill_dt[:].rearrange("p t f -> p (t f)")).then_inc(filled, 16)
                        for c in range(STEPS):
                            sp.dma_start(rec_s.rearrange("(p c t) f -> p c (t f)", p=P, c=STEPS)[:, c, :],
                                         fill_st[:].rearrange("p t f -> p (t f)")).then_inc(filled, 16)
                        sp.dma_start(rec_tmp.rearrange("(p t) f -> p (t f)", p=P),
                                     fill_dt[:, 0:TR, :].rearrange("p t f -> p (t f)")).then_inc(filled, 16)
                        sp.wait_ge(filled, 16 * (STEPS + 2))
                        sp.wait_ge(loaded, 16 * 8)

                    @block.gpsimd
                    def _(pool):
                        pool.iota(iota_i[:], pattern=[[1, P]], base=0, channel_multiplier=0).then_inc(c_ready, 1)
                        pool.iota(pid_i[:], pattern=[[0, 1]], base=0, channel_multiplier=1).then_inc(c_ready, 1)

                    @block.tensor
                    def _(pe):
                        pe.wait_ge(viol_ready, 1)
                        pe.matmul(ps_v[:, 0:1], lhsT=ones[:], rhs=viol[:], start=True, stop=True)\
                            .then_inc(viol_sum, 1)

                    @block.vector
                    def _(dve):
                        link = Chain(dve, "setup_step").link
                        link(dve.memset(fill_d[:], 0.0))
                        link(dve.memset(fill_d[:, 1:2], -1.0))
                        link(dve.memset(fill_d[:, 5:6], -1.0))
                        link(dve.memset(fill_s[:], 0.0))
                        link(dve.memset(fill_s[:, 34:35], -1.0))
                        link(dve.tensor_copy(fill_dt[:], fill_d[:].unsqueeze(1).to_broadcast([P, T, 8])))
                        link(dve.tensor_copy(fill_st[:], fill_s[:].unsqueeze(1).to_broadcast([P, 2 * G, FR])))
                        dve.sem_inc(fill_ready, 1)
                        dve.wait_ge(c_ready, 2)
                        link(dve.tensor_copy(iota_f[:], iota_i[:]))
                        link(dve.tensor_copy(pid[:, 0:1], pid_i[:]))
                        link(dve.tensor_scalar(pid[:, 1:2], pid[:, 0:1], 8.0, None, ALU.add))
                        link(dve.tensor_scalar(pid[:, 2:3], pid[:, 0:1], -8.0, None, ALU.add))
                        link(dve.tensor_scalar(ident[:], iota_f[:], pid[:, 0:1], None, ALU.is_equal))
                        link(dve.tensor_scalar(below[:], iota_f[:], pid[:, 1:2], None, ALU.is_equal))
                        link(dve.tensor_scalar(above[:], iota_f[:], pid[:, 2:3], None, ALU.is_equal))
                        link(dve.tensor_scalar(tri_m1[:], iota_f[:], pid[:, 0:1], -1.0, ALU.is_le, ALU.mult))
                        link(dve.memset(ones_bf[:], 1.0))
                        link(dve.memset(ones[:], 1.0))
                        dve.wait_ge(loaded, 16 * 8)
                        link(dve.tensor_tensor(d_viol[:], d_line[:, 1:TR + 1], d_line[:, 0:TR], ALU.is_lt))
                        link(dve.tensor_reduce(viol[:], d_viol[:], AX.X, ALU.add))
                        dve.sem_inc(viol_ready, 1)
                        link(dve.tensor_copy(recs[:, :, 32], e_w[:, 1, :]))
                        link(dve.tensor_copy(recs[:, :, 33], e_dst[:]))
                        link(dve.tensor_scalar(e_tmp[:], e_src[:], P - 1, None, ALU.bitwise_and))
                        link(dve.tensor_copy(recs[:, :, 34], e_tmp[:]))
                        link(dve.tensor_scalar(e_tmp[:], e_src[:], 7, None, ALU.arith_shift_right))
                        link(dve.tensor_copy(recs[:, :, 35], e_tmp[:]))
                        link(dve.tensor_copy(key_s[:], e_tmp[:]))
                        link(dve.memset(recd[:], 0.0))
                        link(dve.tensor_copy(recd[:, :, 0], e_src[:]))
                        link(dve.tensor_copy(recd[:, :, 1], e_dst[:]))
                        link(dve.tensor_copy(e_tf[:], e_typ[:]))
                        link(dve.scalar_tensor_tensor(recd[:, :, 2], e_tf[:], float(NP), recd[:, :, 0],
                                                 ALU.mult, ALU.add))
                        link(dve.tensor_copy(recd[:, :, 3], e_w[:, 0, :]))
                        link(dve.tensor_copy(recd[:, :, 4], e_w[:, 1, :]))
                        link(dve.tensor_scalar(e_tmp[:], e_dst[:], P - 1, None, ALU.bitwise_and))
                        link(dve.tensor_copy(recd[:, :, 5], e_tmp[:]))
                        link(dve.tensor_scalar(e_tmp[:], e_dst[:], 7, None, ALU.arith_shift_right))
                        link(dve.tensor_copy(recd[:, :, 6], e_tmp[:]))
                        dve.wait_ge(viol_sum, 1)
                        link(dve.tensor_copy(unsorted_i[:], ps_v[:, 0:1]))

            def bucket_key(dve, link, key, digit, t):
                link(dve.tensor_scalar(t[:], recd[:, :, 1], 0.0, None, ALU.is_ge))
                link(dve.scalar_tensor_tensor(key[:], digit, 1.0, t[:], ALU.add, ALU.mult))
                link(dve.tensor_scalar(key[:], key[:], -1.0, None, ALU.add))

            with ExitStack() as s2:
                rt = [rank_scratch(s2, "rank_t0")]
                sct = [scatter_scratch(s2, "scat_t0", 8)]
                rt.append(dict(rt[0], hit_ready=sem("rank_t1_hit_ready"), counted=sem("rank_t1_counted")))
                sct.append(dict(sct[0], idx_ready=sem("scat_t1_idx_ready"),
                                written=[sem(f"scat_t1_written{h}") for h in range(2)]))
                placed, passed, reloaded = sem("pass_placed"), sem("pass_scattered"), sem("pass_reloaded")

                def out_of_order(eng):
                    return eng.If(eng.value_load(unsorted_i[0:1, 0:1], min_val=0, max_val=P * (TR + 1)))

                with phase() as block:
                    @block.vector
                    def _(dve):
                        c = Chain(dve, "pass_step")
                        with out_of_order(dve):
                            for k in range(2):
                                r = rt[k]
                                if k:
                                    dve.wait_ge(reloaded, 16 * k)
                                c.link(dve.tensor_copy(r["lo_i"][:], recd[:, :, 5]))
                                if k == 0:
                                    c.link(dve.tensor_scalar(r["lo_i"][:], r["lo_i"][:], 15, None, ALU.bitwise_and))
                                else:
                                    c.link(dve.tensor_scalar(r["lo_i"][:], r["lo_i"][:], 4, None,
                                                             ALU.arith_shift_right))
                                c.link(dve.tensor_copy(r["spot"][:], r["lo_i"][:]))
                                bucket_key(dve, c.link, key_d, r["spot"][:], r["run"])
                                rank_vector(dve, c, r, key_d, place_d, False)
                                place_to_row(dve, c.link, r, place_d, row_d, False)
                                dve.sem_inc(placed, 1)

                    @block.tensor
                    def _(pe):
                        with out_of_order(pe):
                            for k in range(2):
                                rank_tensor(pe, rt[k])

                    @block.gpsimd
                    def _(pool):
                        with out_of_order(pool):
                            for k in range(2):
                                pool.wait_ge(placed, k + 1)
                                scatter_pool(pool, sct[k], row_d, recd, rec_tmp)
                                pool.sem_inc(passed, 1)

                    @block.sync
                    def _(sp):
                        with out_of_order(sp):
                            for k in range(2):
                                sp.wait_ge(passed, k + 1)
                                sp.dma_start(recd[:].rearrange("p t f -> p (t f)"),
                                             rec_tmp.rearrange("(p t) f -> p (t f)", p=P)).then_inc(reloaded, 16)
                                sp.wait_ge(reloaded, 16 * (k + 1))

            with ExitStack() as s2:
                rs = rank_scratch(s2, "rank_s")
                with phase() as block:
                    @block.vector
                    def _(dve):
                        c = Chain(dve, "rank_s_step")
                        rank_vector(dve, c, rs, key_s, place_s, True)
                        place_to_row(dve, c.link, rs, place_s, row_s, True)

                    @block.tensor
                    def _(pe):
                        rank_tensor(pe, rs)

            with ExitStack() as s2:
                ss = scatter_scratch(s2, "scat_s", FR)
                rd = rank_scratch(s2, "rank_d")
                with phase() as block:
                    @block.gpsimd
                    def _(pool):
                        scatter_pool(pool, ss, row_s, recs, rec_s)

                    @block.vector
                    def _(dve):
                        c = Chain(dve, "rank_d_step")
                        link = c.link
                        bucket_key(dve, link, key_d, recd[:, :, 6], rd["run"])
                        rank_vector(dve, c, rd, key_d, place_d, True)
                        place_to_row(dve, c.link, rd, place_d, row_d, True)

                    @block.tensor
                    def _(pe):
                        rank_tensor(pe, rd)

            with ExitStack() as s2:
                sd = scatter_scratch(s2, "scat_d", 8)
                with phase() as block:
                    @block.gpsimd
                    def _(pool):
                        scatter_pool(pool, sd, row_d, recd, rec_d)

                    @block.tensor
                    def _(pe):
                        pe.nop()

        def to_scan_tensor(pe, s, data):
            v = data[:].rearrange("p (a c) h -> p a (c h)", c=CH)
            for t in range(CT):
                q, r = divmod(t, 4)
                if r == 0 and q >= 2:
                    pe.wait_ge(s["scan_copied"], q - 1)
                pe.transpose(s["ps_scan"][:, q % 2, r * P:(r + 1) * P], v[:, t, :], ident[:])\
                    .then_inc(s["scan_turned"], 1)

        def to_scan_scalar(act, s, dest):
            for q in range(-(-CT // 4)):
                n = min(4, CT - 4 * q)
                act.wait_ge(s["scan_turned"], 4 * q + n)
                act.copy(dest[:, q * 4 * P:q * 4 * P + n * P], s["ps_scan"][:, q % 2, 0:n * P])\
                    .then_inc(s["scan_copied"], 1)

        with ExitStack() as st:
            rec2 = SB(st, "rec2", [P, T, 8])
            dst8 = SB(st, "dst8", [P, T, 8])
            dscan = SB(st, "dscan", [P, SC + 1])
            s = {"ps_scan": PS(st, "r_ps_scan", [P, 2, 512]), "scan_copied": sem("r_copied"),
                 "scan_turned": sem("r_turned")}
            ps_n = PS(st, "r_ps_n", [P, 512])
            r_loaded = sem("r_loaded")
            r_dst8 = sem("r_dst8")
            r_col = sem("r_col")
            r_shift = sem("r_shift")
            with phase() as block:
                @block.sync
                def _(sp):
                    sp.dma_start(rec2[:].rearrange("p t f -> p (t f)"),
                                 rec_d.rearrange("(p t) f -> p (t f)", p=P)).then_inc(r_loaded, 16)
                    sp.dma_start(rs4[:], rec_s.rearrange("(p t) f -> p t f", p=P)[:, :, 32:36]).then_inc(r_loaded, 16)
                    sp.wait_ge(r_loaded, 32)

                @block.tensor
                def _(pe):
                    pe.wait_ge(r_dst8, 1)
                    to_scan_tensor(pe, s, dst8)
                    pe.wait_ge(s["scan_copied"], -(-CT // 4))
                    pe.matmul(ps_n[:, 0:1], lhsT=below[:], rhs=dscan[:, SC:SC + 1], start=True, stop=True)\
                        .then_inc(r_shift, 1)
                    pe.wait_ge(r_col, 1)
                    pe.matmul(ps_n[:, 1:2], lhsT=above[:], rhs=reset[:, 0:1], start=True, stop=True)\
                        .then_inc(r_shift, 1)

                @block.scalar
                def _(act):
                    to_scan_scalar(act, s, dscan[:, 1:SC + 1])

                @block.vector
                def _(dve):
                    link = Chain(dve, "reload_step").link
                    dve.wait_ge(r_loaded, 32)
                    link(dve.tensor_copy(dst8[:], rec2[:, :, 1:2].to_broadcast([P, T, 8])))
                    dve.sem_inc(r_dst8, 1)
                    link(dve.tensor_copy(src_i[:], rec2[:, :, 0]))
                    link(dve.tensor_copy(hr_i[:], rec2[:, :, 2]))
                    link(dve.tensor_copy(ew[:], rec2[:, :, 3]))
                    link(dve.tensor_copy(ew1[:], rec2[:, :, 4]))
                    link(dve.tensor_copy(dloc[:], rec2[:, :, 5]))
                    link(dve.tensor_copy(blk_i[:], rec2[:, :, 6]))
                    link(dve.tensor_copy(dst2_i[:], rs4[:, :, 1]))
                    link(dve.tensor_copy(sblk_i[:], rs4[:, :, 3]))
                    dve.wait_ge(r_shift, 1)
                    link(dve.tensor_copy(dscan[:, 0:1], ps_n[:, 0:1]))
                    link(dve.tensor_tensor(reset[:, 0:SC], dscan[:, 1:SC + 1], dscan[:, 0:SC], ALU.not_equal))
                    link(dve.tensor_scalar(reset[:, 0:SC], reset[:, 0:SC], -BIG, None, ALU.mult))
                    dve.sem_inc(r_col, 1)
                    dve.wait_ge(r_shift, 2)
                    link(dve.tensor_copy(reset[:, SC:SC + 1], ps_n[:, 1:2]))

        def segment_exp(name):
            with ExitStack() as st:
                sc = SB(st, name + "_sc", [P, SC])
                fw = SB(st, name + "_fw", [P, SC])
                col = SB(st, name + "_col", [P, 4])
                rowb = SB(st, name + "_row", [1, 4, P])
                s = {"ps_scan": PS(st, name + "_ps_scan", [P, 2, 512]), "scan_copied": sem(name + "_copied"),
                     "scan_turned": sem(name + "_turned")}
                ps_b = PS(st, name + "_ps_b", [P, 2, 512])
                ps_r = PS(st, name + "_ps_r", [P, 512])
                ps_c = PS(st, name + "_ps_c", [P, 512])
                c_ends, c_rows, c_carry, c_col = (sem(name + n) for n in ("_ends", "_rows", "_carry", "_col"))
                m_ready, m_back, m_used = (sem(name + n) for n in ("_max", "_back", "_used"))
                e_done = sem(name + "_exp")
                vb = att[:].rearrange("p (a c) h -> p (a c h)", c=CH)
                with phase() as block:
                    @block.tensor
                    def _(pe):
                        to_scan_tensor(pe, s, att)
                        for k in range(2):
                            pe.wait_ge(c_ends, k + 1)
                            pe.matmul(ps_r[0:1, 0:P], lhsT=col[:, 2 * k:2 * k + 1], rhs=ident[:],
                                      start=True, stop=True)
                            pe.matmul(ps_r[0:1, P:2 * P], lhsT=col[:, 2 * k + 1:2 * k + 2], rhs=ident[:],
                                      start=True, stop=True).then_inc(c_rows, 1)
                            pe.wait_ge(c_carry, k + 1)
                            pe.matmul(ps_c[:, k:k + 1], lhsT=rowb[0:1, 3, :], rhs=ones[0:1, 0:1],
                                      start=True, stop=True).then_inc(c_col, 1)
                        pe.wait_ge(m_ready, 1)
                        for t in range(CT):
                            q, r = divmod(t, 4)
                            if r == 0 and q >= 2:
                                pe.wait_ge(m_used, q - 1)
                            pe.transpose(ps_b[:, q % 2, r * P:(r + 1) * P], sc[:, t * P:(t + 1) * P], ident[:])\
                                .then_inc(m_back, 1)

                    @block.scalar
                    def _(act):
                        to_scan_scalar(act, s, sc)
                        act.wait_ge(m_used, -(-CT // 4))
                        act.activation(att[:].rearrange("p t h -> p (t h)"), att[:].rearrange("p t h -> p (t h)"),
                                       ACT.Exp).then_inc(e_done, 1)

                    @block.vector
                    def _(dve):
                        link = Chain(dve, name + "_step").link
                        r_fw, r_bw = reset[:, 0:SC], reset[:, 1:SC + 1]
                        dve.wait_ge(s["scan_copied"], -(-CT // 4))
                        link(dve.tensor_reduce(col[:, 1:2], r_fw, AX.X, ALU.min))
                        link(dve.tensor_reduce(col[:, 3:4], r_bw, AX.X, ALU.min))
                        for k in range(2):
                            if k == 0:
                                o, r, x = fw[:], r_fw, sc[:]
                                end = fw[:, SC - 1:SC]
                            else:
                                o, r, x = sc[:, ::-1], r_bw[:, ::-1], fw[:, ::-1]
                                end = sc[:, 0:1]
                            link(dve.tensor_tensor_scan(o, r, x, -BIG, ALU.add, ALU.max))
                            link(dve.tensor_copy(col[:, 2 * k:2 * k + 1], end))
                            dve.sem_inc(c_ends, 1)
                            dve.wait_ge(c_rows, k + 1)
                            link(dve.tensor_copy(rowb[0:1, 0, :].rearrange("o (h c) -> o c h", h=8),
                                            ps_r[0:1, 0:P].rearrange("o (c h) -> o c h", h=8)))
                            link(dve.tensor_copy(rowb[0:1, 1, :].rearrange("o (h c) -> o c h", h=8),
                                            ps_r[0:1, P:2 * P].rearrange("o (c h) -> o c h", h=8)))
                            first = CH - 1 if k else 0
                            link(dve.memset(rowb[0:1, 1, :].rearrange("o (h c) -> o h c", h=8)[:, :, first:first + 1], -BIG))
                            rv = (lambda n: rowb[0:1, n, ::-1]) if k else (lambda n: rowb[0:1, n, :])
                            link(dve.tensor_tensor_scan(rv(2), rv(1), rv(0), -BIG, ALU.add, ALU.max))
                            link(dve.memset(rowb[0:1, 3, :], -BIG))
                            src = rowb[0:1, 2, :].rearrange("o (h c) -> o c h", h=8)
                            dst = rowb[0:1, 3, :].rearrange("o (c h) -> o c h", h=8)
                            if k == 0:
                                link(dve.tensor_copy(dst[:, 1:CH, :], src[:, 0:CH - 1, :]))
                                dve.sem_inc(c_carry, 1)
                            else:
                                link(dve.tensor_copy(dst[:, 0:CH - 1, :], src[:, 1:CH, :]))
                                dve.sem_inc(c_carry, 1)
                            dve.wait_ge(c_col, k + 1)
                            link(dve.tensor_copy(col[:, 2 * k:2 * k + 1], ps_c[:, k:k + 1]))
                            link(dve.tensor_tensor_scan(o, r, x, col[:, 2 * k:2 * k + 1], ALU.add, ALU.max))
                        dve.sem_inc(m_ready, 1)
                        for q in range(-(-CT // 4)):
                            n = min(4, CT - 4 * q)
                            dve.wait_ge(m_back, 4 * q + n)
                            av = vb[:, 4 * q * P:(4 * q + n) * P]
                            dve.tensor_tensor(av, av, ps_b[:, q % 2, 0:n * P], ALU.subtract).then_inc(m_used, 1)

        def edge_scores(name, table, wt, node_rows, wn, combine, n_combine):
            with ExitStack() as st:
                gat = SB(st, name + "_gat", [P, 2, G, wt])
                idx = SB(st, name + "_idx", [P, 2, G], I32)
                loc = SB(st, name + "_loc", [P, G])
                hot = SB(st, name + "_hot", [P, G, P])
                hot_t = SB(st, name + "_hot_t", [P, G, P])
                prod = SB(st, name + "_prod", [P, G, P])
                red = SB(st, name + "_red", [P, G, 8])
                tmp = SB(st, name + "_tmp", [P, G, 8])
                ps_t = PS(st, name + "_ps_t", [P, G, P])
                ps_q = PS(st, name + "_ps_q", [P, G, P])
                idx_ready, hot_ready, turned, copied, spread, scored = (
                    sem(name + n) for n in ("_idx_ready", "_hot_ready", "_turned", "_copied", "_spread", "_scored"))
                got = [sem(name + f"_got{h}") for h in range(2)]
                with phase() as block:
                    @block.gpsimd
                    def _(pool):
                        def half(i, h):
                            pool.tensor_copy(idx[:, h, :], src_i[:, bass.ds(i * 2 * G + h * G, G)])\
                                .then_inc(idx_ready, 1)
                            pool.wait_ge(idx_ready, i * 2 + h + 1)
                            pool.nop(nofuse=True)
                            for u in range(G):
                                pool.indirect_dma_start(
                                    out=gat[:, h, u, :], out_offset=None, in_=table,
                                    in_offset=bass.IndirectOffsetOnAxis(ap=idx[:, h, u:u + 1], axis=0))\
                                    .then_inc(got[h], 16)
                        for h in range(2):
                            half(0, h)
                        with pool.Fori(1, STEPS) as i:
                            for h in range(2):
                                pool.wait_ge(scored, i * 2 + h - 1)
                                half(i, h)

                    @block.vector
                    def _(dve):
                        c = Chain(dve, name + "_step")
                        with c.loop(0, STEPS, 2 * (1 + n_combine)) as i:
                            for h in range(2):
                                n = i * 2 + h
                                t0 = i * 2 * G + h * G
                                c.link(move(dve, loc[:], dloc[:, bass.ds(t0, G)]))
                                for u in range(G):
                                    ins = dve.tensor_scalar(hot[:, u, :], iota_f[:], loc[:, u:u + 1], None,
                                                            ALU.is_equal)
                                ins.then_inc(hot_ready, 1)
                                dve.wait_ge(got[h], (i + 1) * (16 * G))
                                dve.wait_ge(spread, n + 1)
                                combine(dve, c.link, t0, gat[:, h, :, :], ps_q, prod, red, tmp)
                                dve.sem_inc(scored, 1)

                    @block.tensor
                    def _(pe):
                        with pe.Fori(0, STEPS) as i:
                            for h in range(2):
                                n = i * 2 + h
                                t0 = i * 2 * G + h * G
                                pe.wait_ge(hot_ready, n + 1)
                                for u in range(G):
                                    ins = pe.transpose(ps_t[:, u, :], hot[:, u, :], ident[:])
                                ins.then_inc(turned, 1)
                                for u in range(G):
                                    k = pe.value_load(blk_i[0:1, bass.ds(t0 + u, 1)], min_val=0, max_val=NB - 1)
                                    if u == 0:
                                        pe.wait_ge(copied, n + 1)
                                    ins = pe.matmul(ps_q[:, u, 0:wn], lhsT=hot_t[:, u, :],
                                                    rhs=node_rows[:, bass.ds(k * wn, wn)], start=True, stop=True)
                                ins.then_inc(spread, 1)

                    @block.scalar
                    def _(act):
                        with act.Fori(0, STEPS) as i:
                            for h in range(2):
                                act.wait_ge(turned, i * 2 + h + 1)
                                act.copy(hot_t[:, 0:G // 2, :], ps_t[:, 0:G // 2, :])
                                act.copy(hot_t[:, G // 2:G, :], ps_t[:, G // 2:G, :]).then_inc(copied, 1)

        def edge_sums(name, table, wt, idx_all, local, blocks, weight, nh, ws, acc, banks, rows=None, n_rows=0, mlp=None):
            with ExitStack() as st:
                gat = SB(st, name + "_gat", [P, 2, G, wt])
                idx = SB(st, name + "_idx", [P, 2, G], I32)
                loc = SB(st, name + "_loc", [P, G])
                wgt = SB(st, name + "_wgt", [P, G, 8])
                hot = SB(st, name + "_hot", [P, G, nh, P])
                made = SB(st, name + "_made", [P, G, ws]) if rows else None
                per = 2 if banks == 2 or mlp else 4
                ps = PS(st, name + "_ps", [P, per * banks, 512])
                idx_ready, hot_ready, rows_ready, summed, added = (
                    sem(name + n) for n in ("_idx_ready", "_hot_ready", "_rows_ready", "_summed", "_added"))
                got = [sem(name + f"_got{h}") for h in range(2)]

                def slot(u):
                    if banks == 1:
                        return ps[:, u % per, 0:ws]
                    return ps[:, (u % per) * 2:(u % per) * 2 + 2, 0:2 * ws]
                m = mlp(st) if mlp else None
                with phase() as block:
                    @block.gpsimd
                    def _(pool):
                        def half(i, h):
                            pool.tensor_copy(idx[:, h, :], idx_all[:, bass.ds(i * 2 * G + h * G, G)])\
                                .then_inc(idx_ready, 1)
                            pool.wait_ge(idx_ready, i * 2 + h + 1)
                            pool.nop(nofuse=True)
                            for u in range(G):
                                pool.indirect_dma_start(
                                    out=gat[:, h, u, :], out_offset=None, in_=table,
                                    in_offset=bass.IndirectOffsetOnAxis(ap=idx[:, h, u:u + 1], axis=0))\
                                    .then_inc(got[h], 16)
                        for h in range(2):
                            half(0, h)
                        with pool.Fori(1, STEPS) as i:
                            for h in range(2):
                                pool.wait_ge(summed, (i * 2 + h - 1) * G)
                                half(i, h)

                    @block.vector
                    def _(dve):
                        c = Chain(dve, name + "_step")
                        c.link(dve.memset(acc[:], 0.0))
                        with c.loop(0, STEPS, 2 * (1 + (weight is not None) + n_rows)) as i:
                            for h in range(2):
                                n = i * 2 + h
                                t0 = i * 2 * G + h * G
                                c.link(move(dve, loc[:], local[:, bass.ds(t0, G)]))
                                if weight is not None:
                                    c.link(move(dve, wgt[:, :, 0:nh], weight[:, bass.ds(t0, G), 0:nh]))
                                for u in range(G):
                                    for k in range(nh):
                                        if weight is None:
                                            ins = dve.tensor_scalar(hot[:, u, k, :], iota_f[:], loc[:, u:u + 1],
                                                                    None, ALU.is_equal)
                                        else:
                                            ins = dve.tensor_scalar(hot[:, u, k, :], iota_f[:], loc[:, u:u + 1],
                                                                    wgt[:, u, k:k + 1], ALU.is_equal, ALU.mult)
                                    ins.then_inc(hot_ready, 1)
                                if rows:
                                    dve.wait_ge(got[h], (i + 1) * (16 * G))
                                    rows(dve, c.link, n, t0, gat[:, h, :, :], made, m)
                                    dve.sem_inc(rows_ready, 1)
                                for u in range(G):
                                    k = dve.value_load(blocks[0:1, bass.ds(t0 + u, 1)], min_val=0, max_val=NB - 1)
                                    dve.wait_ge(summed, t0 + (u + 1))
                                    w = nh * ws
                                    av = acc[:, bass.ds(k * w, w)]
                                    if banks == 2:
                                        av = av.rearrange("p (a b) -> p a b", a=2)
                                    dve.tensor_tensor(av, av, slot(u), ALU.add).then_inc(added, 1)
                                    dve.wait_ge(added, t0 + (u + 1))

                    @block.tensor
                    def _(pe):
                        with pe.Fori(0, STEPS) as i:
                            for h in range(2):
                                n = i * 2 + h
                                t0 = i * 2 * G + h * G
                                if mlp:
                                    m["tensor"](pe, i, h)
                                if rows:
                                    pe.wait_ge(rows_ready, n + 1)
                                else:
                                    pe.wait_ge(got[h], (i + 1) * (16 * G))
                                for u in range(G):
                                    pe.wait_ge(hot_ready, t0 + (u + 1))
                                    if u >= per:
                                        pe.wait_ge(added, t0 + (u + 1 - per))
                                    src = made[:, u, :] if rows else gat[:, h, u, :]
                                    for k in range(nh):
                                        if banks == 1:
                                            o = slot(u)
                                        else:
                                            o = ps[:, (u % 2) * 2 + k // 2, (k % 2) * ws:(k % 2) * ws + ws]
                                        ins = pe.matmul(o, lhsT=hot[:, u, k, :], rhs=src[:, k * ws:(k + 1) * ws],
                                                        start=True, stop=True)
                                    ins.then_inc(summed, 1)

                    if mlp:
                        @block.scalar
                        def _(act):
                            m["scalar"](act)

                        @block.sync
                        def _(sp):
                            m["sync"](sp)

        W5 = NBU * P

        def node_stage(name, fill, kd, tensor, vector, n_vector, scalar, scratch, load=None, store=None,
                       n_scalar=0):
            with ExitStack() as st:
                stage = SB(st, name + "_stage", [P, NBU * kd, P])
                xt = SB(st, name + "_xt", [P, NBU * kd, P])
                nb = -(-NBU * kd // 4)
                ps_x = PS(st, name + "_ps_x", [P, 2, 4, P])
                staged, turned, copied = (sem(name + n) for n in ("_staged", "_turned", "_copied"))
                in_w, outs = sem(name + "_weights"), sem(name + "_stored")
                done_v, taken = sem(name + "_vdone"), sem(name + "_taken")
                s = scratch(st)
                with phase() as block:
                    @block.sync
                    def _(sp):
                        nl = load(sp, s, in_w) if load else 0
                        if store:
                            sp.wait_ge(done_v, 1)
                            ns = store(sp, s, outs)
                            sp.wait_ge(outs, 16 * ns)

                    @block.gpsimd
                    def _(pool):
                        c = Chain(pool, name + "_fill_step")
                        with c.loop(0, NBI, fill[1]) as i:
                            fill[0](pool, c.link, stage, i)
                            pool.sem_inc(staged, 1)
                            pool.wait_ge(turned, (i + 1) * nb)

                    @block.tensor
                    def _(pe):
                        with pe.Fori(0, NBI) as i:
                            pe.wait_ge(staged, i + 1)
                            for q in range(nb):
                                if q >= 2:
                                    pe.wait_ge(copied, i * nb + (q - 1))
                                c = min(4, NBU * kd - 4 * q)
                                for r in range(c):
                                    ins = pe.transpose(ps_x[:, q % 2, r, :], stage[:, 4 * q + r, :], ident[:])
                                ins.then_inc(turned, 1)
                            pe.wait_ge(copied, (i + 1) * nb)
                            tensor(pe, s, i, xt)
                            pe.wait_ge(taken, i + 1)

                    @block.scalar
                    def _(act):
                        steps = Chain(act, name + "_act_step")
                        with steps.loop(0, NBI, n_scalar) as i:
                            for q in range(nb):
                                act.wait_ge(turned, i * nb + (q + 1))
                                c = min(4, NBU * kd - 4 * q)
                                act.copy(xt[:, 4 * q:4 * q + c, :], ps_x[:, q % 2, 0:c, :]).then_inc(copied, 1)
                            scalar(act, steps.link, s, i)

                    @block.vector
                    def _(dve):
                        c = Chain(dve, name + "_step")
                        with c.loop(0, NBI, n_vector) as i:
                            vector(dve, c.link, s, i)
                            dve.sem_inc(taken, 1)
                        dve.sem_inc(done_v, 1)

        def blocks_of(data):
            flat = data[:].rearrange("p b d -> p (b d)") if len(data.shape) == 3 else data[:]

            def fill(pool, link, stage, i):
                link(pool.tensor_copy(stage[:].rearrange("p a d -> p (a d)"), flat[:, bass.ds(i * W5, W5)]))
            return fill, 1

        def nothing(*_):
            pass

        def add_norm(name, update, relu, last=False):
            with ExitStack() as st:
                sq = SB(st, name + "_sq", [P, NB, D])
                mean = SB(st, name + "_mean", [P, NB])
                var = SB(st, name + "_var", [P, NB])
                dev = SB(st, name + "_dev", [P, NB])
                v_ready, r_ready, o_ready, stored = (sem(name + n) for n in ("_var_r", "_dev_r", "_out_r", "_stored"))
                with phase() as block:
                    @block.vector
                    def _(dve):
                        link = Chain(dve, name + "_step").link
                        if relu:
                            link(dve.scalar_tensor_tensor(X[:], update, 0.0, X[:], ALU.max, ALU.add))
                        else:
                            link(dve.tensor_tensor(X[:], X[:], update, ALU.add))
                        link(dve.tensor_reduce(mean[:], X[:], AX.X, ALU.add))
                        link(dve.tensor_scalar(mean[:], mean[:], 1.0 / D, None, ALU.mult))
                        link(dve.tensor_tensor(X[:], X[:], mean[:].unsqueeze(2).to_broadcast([P, NB, D]), ALU.subtract))
                        link(dve.tensor_tensor(sq[:], X[:], X[:], ALU.mult))
                        link(dve.tensor_reduce(var[:], sq[:], AX.X, ALU.add))
                        link(dve.tensor_scalar(var[:], var[:], 1.0 / D, EPS, ALU.mult, ALU.add))
                        dve.sem_inc(v_ready, 1)
                        dve.wait_ge(r_ready, 1)
                        link(dve.reciprocal(dev[:], dev[:]))
                        link(dve.tensor_tensor(X[:], X[:], dev[:].unsqueeze(2).to_broadcast([P, NB, D]), ALU.mult))
                        dve.sem_inc(o_ready, 1)

                    @block.scalar
                    def _(act):
                        act.wait_ge(v_ready, 1)
                        act.activation(dev[:], var[:], ACT.Sqrt).then_inc(r_ready, 1)

                    if last:
                        @block.sync
                        def _(sp):
                            sp.wait_ge(o_ready, 1)
                            full = NB - 1
                            sp.dma_start(out[0:full * P, :].rearrange("(b p) d -> p b d", p=P), X[:, 0:full, :])\
                                .then_inc(stored, 16)
                            sp.dma_start(out[full * P:N_NODES, :], X[0:N_NODES - full * P, full, :])\
                                .then_inc(stored, 16)
                            sp.wait_ge(stored, 32)

        with ExitStack() as st:
            acc = SB(st, "l0_acc", [P, NB * D])

            def scratch(s_):
                return {"w": SB(s_, "l0_w", [P, 3 * D]), "hr": SB(s_, "l0_hr", [P, NB, 3 * D]),
                        "ps": PS(s_, "l0_ps", [P, NBU, 512]), "mm": sem("l0_mm")}

            def load(sp, s, in_w):
                sp.dma_start(s["w"][:].rearrange("p (r o) -> p r o", r=3),
                             a["L0_w"].rearrange("r i o -> i r o")).then_inc(in_w, 16)
                s["in_w"] = in_w
                return 1

            def tensor(pe, s, i, xt):
                pe.wait_ge(s["in_w"], 16)
                for u in range(NBU):
                    pe.matmul(s["ps"][:, u, 0:3 * D], lhsT=xt[:, u, :], rhs=s["w"][:], start=True, stop=True)\
                        .then_inc(s["mm"], 1)

            def vector(dve, link, s, i):
                for u in range(NBU):
                    dve.wait_ge(s["mm"], i * NBU + (u + 1))
                    link(move(dve, s["hr"][:, bass.ds(i * NBU + u, 1), :],
                                         s["ps"][:, u:u + 1, 0:3 * D]))

            def store(sp, s, outs):
                for r in range(3):
                    sp.dma_start(t_hr[r * NP:(r + 1) * NP, :].rearrange("(b p) d -> p b d", p=P),
                                 s["hr"][:, :, r * D:(r + 1) * D]).then_inc(outs, 16)
                return 3
            node_stage("l0n", blocks_of(X), 1, tensor, vector, NBU, nothing, scratch, load, store)
            edge_sums("l0e", t_hr, D, hr_i, dloc, blk_i, ew[:].unsqueeze(2), 1, D, acc, 1)
            add_norm("l0x", acc[:].rearrange("p (b d) -> p b d", b=NB), True)
        with ExitStack() as st:
            q_all = SB(st, "l1_q", [P, NB * D])
            w_all = SB(st, "l1_w", [P, 3 * D])
            b_row = SB(st, "l1_b", [1, 3 * D])
            rel = SB(st, "l1_rel", [P, D])
            with ExitStack() as s2:
                wv = SB(s2, "l1_wv", [P, D])
                bd = SB(s2, "l1_bd", [P, D])
                bv = SB(s2, "l1_bv", [P, 1])
                ps = PS(s2, "l1_ps_w", [P, 512])
                in_w, z_ready, mm = sem("l1_weights"), sem("l1_zeroed"), sem("l1_folded")
                with phase() as block:
                    @block.sync
                    def _(sp):
                        sp.dma_start(w_all[:, 0:D], a["L1_Wk"]).then_inc(in_w, 16)
                        sp.dma_start(w_all[:, D:2 * D], a["L1_Wq"]).then_inc(in_w, 16)
                        sp.dma_start(wv[:], a["L1_Wv"]).then_inc(in_w, 16)
                        sp.dma_start(b_row[:, 0:D], a["L1_bk"].unsqueeze(0)).then_inc(in_w, 16)
                        sp.dma_start(b_row[:, D:2 * D], a["L1_bq"].unsqueeze(0)).then_inc(in_w, 16)
                        sp.dma_start(bv[:], a["L1_bv"].unsqueeze(1)).then_inc(in_w, 16)
                        sp.dma_start(rel[:], a["L1_rel"].unsqueeze(0).to_broadcast([P, D])).then_inc(in_w, 16)
                        sp.wait_ge(z_ready, 1)
                        for h in range(H1):
                            sp.dma_start(bd[h * DK:(h + 1) * DK, h * DK:(h + 1) * DK], a["L1_rel_msg"][h])\
                                .then_inc(in_w, 16)
                        sp.wait_ge(in_w, 16 * (7 + H1))

                    @block.tensor
                    def _(pe):
                        pe.wait_ge(in_w, 16 * (7 + H1))
                        pe.matmul(ps[:, 0:D], lhsT=wv[:], rhs=bd[:], start=True, stop=True)
                        pe.matmul(ps[0:1, D:2 * D], lhsT=bv[:], rhs=bd[:], start=True, stop=True).then_inc(mm, 1)

                    @block.vector
                    def _(dve):
                        link = Chain(dve, "l1_prep_step").link
                        link(dve.memset(bd[:], 0.0))
                        dve.sem_inc(z_ready, 1)
                        dve.wait_ge(mm, 1)
                        link(dve.tensor_copy(w_all[:, 2 * D:3 * D], ps[:, 0:D]))
                        link(dve.tensor_copy(b_row[:, 2 * D:3 * D], ps[0:1, D:2 * D]))

            def scratch(s_):
                return {"k": SB(s_, "l1_k", [P, NB, D + H1]), "v": SB(s_, "l1_v", [P, NB, D]),
                        "t": SB(s_, "l1_t", [P, D]), "r": SB(s_, "l1_r", [P, H1]), "ps": PS(s_, "l1_ps", [P, NBU, 512]), "mm": sem("l1_mm")}

            def tensor(pe, s, i, xt):
                for u in range(NBU):
                    pe.matmul(s["ps"][:, u, 0:3 * D], lhsT=xt[:, u, :], rhs=w_all[:], start=True, stop=False)
                    pe.matmul(s["ps"][:, u, 0:3 * D], lhsT=ones[0:1, :], rhs=b_row[:], start=False, stop=True)\
                        .then_inc(s["mm"], 1)

            def vector(dve, link, s, i):
                for u in range(NBU):
                    dve.wait_ge(s["mm"], i * NBU + (u + 1))
                    b = i * NBU + u
                    kb = s["k"][:, bass.ds(b, 1), 0:D].rearrange("p b d -> p (b d)")
                    link(move(dve, kb, s["ps"][:, u, 0:D]))
                    link(move(dve, q_all[:, bass.ds(b * D, D)], s["ps"][:, u, D:2 * D]))
                    link(move(dve, s["v"][:, bass.ds(b, 1), :].rearrange("p b d -> p (b d)"),
                                         s["ps"][:, u, 2 * D:3 * D]))
                    link(dve.tensor_tensor(s["t"][:], kb, rel[:], ALU.mult))
                    link(dve.tensor_reduce(s["r"][:], s["t"][:].rearrange("p (h d) -> p h d", h=H1), AX.X, ALU.add))
                    link(move(dve, s["k"][:, bass.ds(b, 1), D:D + H1].rearrange("p b h -> p (b h)"), s["r"][:]))

            def store(sp, s, outs):
                sp.dma_start(t_k.rearrange("(b p) d -> p b d", p=P), s["k"][:]).then_inc(outs, 16)
                sp.dma_start(t_v.rearrange("(b p) d -> p b d", p=P), s["v"][:]).then_inc(outs, 16)
                return 2
            node_stage("l1n", blocks_of(X), 1, tensor, vector, 6 * NBU, nothing, scratch, store=store)

            def combine(dve, link, t0, rows, ps_q, prod, red, tmp):
                link(dve.tensor_tensor(prod[:], rows[:, :, 0:D], ps_q[:], ALU.mult))
                link(dve.tensor_reduce(red[:], prod[:].rearrange("p g (h d) -> p g h d", h=H1), AX.X, ALU.add))
                link(dve.tensor_tensor(tmp[:], rows[:, :, D:D + H1],
                                       ew[:, bass.ds(t0, G)].unsqueeze(2).to_broadcast([P, G, H1]), ALU.mult))
                link(dve.tensor_tensor(red[:], red[:], tmp[:], ALU.add))
                link(dve.tensor_scalar(att[:, bass.ds(t0, G), :], red[:], float(DK) ** -0.5, None, ALU.mult))
            edge_scores("l1s", t_k, D + H1, q_all, D, combine, 5)
        segment_exp("l1x")

        with ExitStack() as st:
            acc = SB(st, "l1_acc", [P, NB * (D + H1)])
            upd = SB(st, "l1_upd", [P, NB, D])
            den = SB(st, "l1_den", [P, NB, H1])

            def rows(dve, link, n, t0, got, made, m):
                e = att[:, bass.ds(t0, G), :]
                link(dve.tensor_tensor(made[:, :, 0:D].rearrange("p g (h d) -> p g h d", h=H1),
                                       got.rearrange("p g (h d) -> p g h d", h=H1),
                                       e.unsqueeze(3).to_broadcast([P, G, H1, DK]), ALU.mult))
                link(move(dve, made[:, :, D:D + H1], e))
            edge_sums("l1e", t_v, D, src_i, dloc, blk_i, None, 1, D + H1, acc, 1, rows, 2)
            av = acc[:].rearrange("p (b d) -> p b d", b=NB)
            with phase() as block:
                @block.vector
                def _(dve):
                    link = Chain(dve, "l1_div_step").link
                    link(dve.tensor_scalar(den[:], av[:, :, D:D + H1], 1e-30, None, ALU.max))
                    link(dve.reciprocal(den[:], den[:]))
                    link(dve.tensor_tensor(upd[:].rearrange("p b (h d) -> p b h d", h=H1),
                                           av[:, :, 0:D].rearrange("p b (h d) -> p b h d", h=H1),
                                           den[:].unsqueeze(3).to_broadcast([P, NB, H1, DK]), ALU.mult))
            add_norm("l1x2", upd[:], True)

        def softplus_scalar(act, link, s, n, y):
            act.wait_ge(s["hid"], n + 1)
            link(act.activation(s["y"][:], y, ACT.Identity, bias=s["bias"][:, 0:1]))
            act.sem_inc(s["y_ready"], 1)
            link(act.activation(s["l"][:], s["y"][:], ACT.Abs))
            link(act.activation(s["l"][:], s["l"][:], ACT.Exp, scale=-1.0))
            link(act.activation(s["l"][:], s["l"][:], ACT.Ln, bias=1.0))
            act.sem_inc(s["l_ready"], 1)

        def softplus_vector(dve, link, s, n):
            dve.wait_ge(s["y_ready"], n + 1)
            link(dve.tensor_scalar(s["sp"][:], s["y"][:], 0.0, None, ALU.max))
            dve.wait_ge(s["l_ready"], n + 1)
            link(dve.tensor_tensor(s["sp"][:], s["sp"][:], s["l"][:], ALU.add))
            dve.sem_inc(s["soft"], 1)

        def softplus_scratch(s_, name, width, bias):
            s = {"bias": bias}
            for k in ("y", "l", "sp"):
                s[k] = SB(s_, f"{name}_{k}", [P, width])
            for k in ("hid", "y_ready", "l_ready", "soft"):
                s[k] = sem(f"{name}_{k}")
            return s

        with ExitStack() as st:
            w_in = SB(st, "l2_w_in", [P, D])
            wf1 = SB(st, "l2_wf1", [32, D])
            wf2 = SB(st, "l2_wf2", [P, D])
            wo1 = SB(st, "l2_wo1", [P, D])
            wo2 = SB(st, "l2_wo2", [P, D])
            bf1 = SB(st, "l2_bf1", [P, 1])
            bo1 = SB(st, "l2_bo1", [P, 1])
            rows2 = SB(st, "l2_rows", [1, 2, D])
            nlog2 = SB(st, "l2_nlog2", [P, 1])
            acc = SB(st, "l2_acc", [P, NB * D])
            with ExitStack() as s2:
                ps = PS(s2, "l2_ps_b", [P, 512])
                in_w, set_, mm = sem("l2_weights"), sem("l2_set"), sem("l2_sums")
                with phase() as block:
                    @block.sync
                    def _(sp):
                        for d, k in ((w_in, "W_in"), (wf1, "Wf1"), (wf2, "Wf2"), (wo1, "Wo1"), (wo2, "Wo2")):
                            sp.dma_start(d[:], a["L2_" + k]).then_inc(in_w, 16)
                        sp.dma_start(bf1[:], a["L2_bf1"].unsqueeze(1)).then_inc(in_w, 16)
                        sp.dma_start(bo1[:], a["L2_bo1"].unsqueeze(1)).then_inc(in_w, 16)
                        sp.dma_start(rows2[:, 0, :], a["L2_bf2"].unsqueeze(0)).then_inc(in_w, 16)
                        sp.dma_start(rows2[:, 1, :], a["L2_bo2"].unsqueeze(0)).then_inc(in_w, 16)
                        sp.wait_ge(in_w, 16 * 9)

                    @block.tensor
                    def _(pe):
                        pe.wait_ge(set_, 1)
                        pe.wait_ge(in_w, 16 * 9)
                        pe.matmul(ps[0:1, 0:D], lhsT=nlog2[:], rhs=wf2[:], start=True, stop=True)
                        pe.matmul(ps[0:1, D:2 * D], lhsT=nlog2[:], rhs=wo2[:], start=True, stop=True).then_inc(mm, 1)

                    @block.vector
                    def _(dve):
                        link = Chain(dve, "l2_prep_step").link
                        link(dve.memset(nlog2[:], -LOG2))
                        dve.sem_inc(set_, 1)
                        dve.wait_ge(mm, 1)
                        link(dve.tensor_tensor(rows2[:], rows2[:], ps[0:1, 0:2 * D].rearrange("o (k d) -> o k d", k=2),
                                               ALU.add))

            def scratch(s_):
                return {"h": SB(s_, "l2_h", [P, NB, D]), "ps": PS(s_, "l2_ps", [P, NBU, 512]), "mm": sem("l2_mm")}

            def tensor(pe, s, i, xt):
                for u in range(NBU):
                    pe.matmul(s["ps"][:, u, 0:D], lhsT=xt[:, u, :], rhs=w_in[:], start=True, stop=True)\
                        .then_inc(s["mm"], 1)

            def vector(dve, link, s, i):
                for u in range(NBU):
                    dve.wait_ge(s["mm"], i * NBU + (u + 1))
                    link(move(dve, s["h"][:, bass.ds(i * NBU + u, 1), :], s["ps"][:, u:u + 1, 0:D]))

            def store(sp, s, outs):
                sp.dma_start(t_h.rearrange("(b p) d -> p b d", p=P), s["h"][:]).then_inc(outs, 16)
                return 1
            node_stage("l2n", blocks_of(X), 1, tensor, vector, NBU, nothing, scratch, store=store)

            def filters(s_):
                m = softplus_scratch(s_, "l2f", G * P, bf1)
                m["rec"] = SB(s_, "l2f_rec", [P, 2, G, FR])
                m["ft"] = SB(s_, "l2f_ft", [32, G * P])
                m["ps_f"] = PS(s_, "l2f_ps_f", [32, G, P])
                m["ps_h"] = PS(s_, "l2f_ps_h", [P, G * P])
                m["ps_w"] = PS(s_, "l2f_ps_w", [P, G, P])
                turned, copied, wij = (sem("l2f_" + k) for k in ("turned", "copied", "wij"))
                loaded_f = [sem(f"l2f_loaded{h}") for h in range(2)]
                m["wij"] = wij
                view = rec_s.rearrange("(p t) f -> p (t f)", p=P)

                def sync(sp):
                    def half(i, h):
                        sp.dma_start(m["rec"][:, h, :, :].rearrange("p g f -> p (g f)"),
                                     view[:, bass.ds((i * 2 * G + h * G) * FR, G * FR)]).then_inc(loaded_f[h], 16)
                    for h in range(2):
                        half(0, h)
                    with sp.Fori(1, STEPS) as i:
                        for h in range(2):
                            sp.wait_ge(turned, i * 2 + h - 1)
                            half(i, h)
                    for h in range(2):
                        sp.wait_ge(loaded_f[h], 16 * STEPS)

                def tensor(pe, i, h):
                    n = i * 2 + h
                    pe.wait_ge(loaded_f[h], (i + 1) * 16)
                    for u in range(G):
                        ins = pe.transpose(m["ps_f"][:, u, :], m["rec"][:, h, u, 0:32], ident[:])
                    ins.then_inc(turned, 1)
                    pe.wait_ge(copied, n + 1)
                    for k in range(2):
                        ins = pe.matmul(m["ps_h"][:, k * 512:(k + 1) * 512], lhsT=wf1[:],
                                        rhs=m["ft"][:, k * 512:(k + 1) * 512], start=True, stop=True)
                    ins.then_inc(m["hid"], 1)
                    pe.wait_ge(m["soft"], n + 1)
                    for u in range(G):
                        pe.matmul(m["ps_w"][:, u, :], lhsT=m["sp"][:, u * P:(u + 1) * P], rhs=wf2[:],
                                  start=True, stop=False)
                        ins = pe.matmul(m["ps_w"][:, u, :], lhsT=ones[0:1, :], rhs=rows2[:, 0, :],
                                        start=False, stop=True)
                    ins.then_inc(wij, 1)

                def scalar(act):
                    c = Chain(act, "l2f_act_step")
                    with c.loop(0, STEPS, 8) as i:
                        for h in range(2):
                            n = i * 2 + h
                            act.wait_ge(turned, n + 1)
                            act.copy(m["ft"][:].rearrange("p (g e) -> p g e", g=G), m["ps_f"][:]).then_inc(copied, 1)
                            softplus_scalar(act, c.link, m, n, m["ps_h"][:])
                m.update(sync=sync, tensor=tensor, scalar=scalar)
                return m

            def rows(dve, link, n, t0, got, made, m):
                softplus_vector(dve, link, m, n)
                dve.wait_ge(m["wij"], n + 1)
                link(dve.tensor_tensor(made[:], got, m["ps_w"][:], ALU.mult))
            edge_sums("l2e", t_h, D, dst2_i, rs4[:, :, 2], sblk_i, rs4[:, :, 0:1], 1, D, acc, 1, rows, 3, filters)

            upd = SB(st, "l2_upd", [P, NB, D])

            def scratch(s_):
                s = softplus_scratch(s_, "l2o", W5, bo1)
                s["ps_h"] = PS(s_, "l2o_ps_h", [P, W5])
                s["ps_o"] = PS(s_, "l2o_ps_o", [P, NBU, P])
                s["mm"] = sem("l2o_mm")
                return s

            def tensor(pe, s, i, xt):
                pe.matmul(s["ps_h"][:, 0:512], lhsT=wo1[:], rhs=xt[:].rearrange("p a d -> p (a d)")[:, 0:512],
                          start=True, stop=True)
                pe.matmul(s["ps_h"][:, 512:W5], lhsT=wo1[:], rhs=xt[:].rearrange("p a d -> p (a d)")[:, 512:W5],
                          start=True, stop=True).then_inc(s["hid"], 1)
                pe.wait_ge(s["soft"], i + 1)
                for u in range(NBU):
                    pe.matmul(s["ps_o"][:, u, :], lhsT=s["sp"][:, u * P:(u + 1) * P], rhs=wo2[:],
                              start=True, stop=False)
                    ins = pe.matmul(s["ps_o"][:, u, :], lhsT=ones[0:1, :], rhs=rows2[:, 1, :], start=False, stop=True)
                ins.then_inc(s["mm"], 1)

            def scalar(act, link, s, i):
                softplus_scalar(act, link, s, i, s["ps_h"][:])

            def vector(dve, link, s, i):
                softplus_vector(dve, link, s, i)
                dve.wait_ge(s["mm"], i + 1)
                link(move(dve, upd[:, bass.ds(i * NBU, NBU), :], s["ps_o"][:]))
            node_stage("l2o", blocks_of(acc), 1, tensor, vector, 3, scalar, scratch, n_scalar=4)
            add_norm("l2x", upd[:], False)

        def leaky(dve, link, dst, src, tmp):
            link(dve.tensor_scalar(tmp, src, 0.01, None, ALU.mult))
            link(dve.tensor_tensor(dst, tmp, src, ALU.max))

        def gat_scores(name, heads, table, a_dst, ew_, mw_):
            def combine(dve, link, t0, rows, ps_q, prod, red, tmp):
                link(dve.tensor_tensor(att[:, bass.ds(t0, G), 0:heads], rows[:, :, 0:heads], ps_q[:, :, 0:heads], ALU.add))
            edge_scores(name, table, H3, a_dst, heads, combine, 1)
            with ExitStack() as s2:
                t = SB(s2, name + "_t", [P, T, heads])
                with phase() as block:
                    @block.vector
                    def _(dve):
                        link = Chain(dve, name + "_lin_step").link
                        v = att[:, :, 0:heads]
                        link(dve.tensor_tensor(t[:], v, ew1[:].unsqueeze(2).to_broadcast([P, T, heads]), ALU.mult))
                        link(dve.tensor_tensor(t[:], t[:], ew_.unsqueeze(1).to_broadcast([P, T, heads]), ALU.mult))
                        link(dve.scalar_tensor_tensor(t[:], t[:], 0.01, t[:], ALU.mult, ALU.max))
                        link(dve.memset(att[:], 0.0))
                        link(dve.tensor_tensor(v, t[:], mw_.unsqueeze(1).to_broadcast([P, T, heads]), ALU.mult))
            segment_exp(name + "x")

        with ExitStack() as st:
            acc = SB(st, "l3_acc", [P, NB * H3 * ZW])
            acc4 = acc[:].rearrange("p (b h d) -> p b h d", b=NB, h=H3)
            a_dst = SB(st, "l3_a_dst", [P, NB * H3])
            ao_dst = SB(st, "l3_ao_dst", [P, NB])
            coef = SB(st, "l3_coef", [P, 10])
            with ExitStack() as s2:
                fc = SB(s2, "l3_fc", [P, H3 * D])
                at = SB(s2, "l3_at", [P, 2, H3 * D])
                in_w = sem("l3_weights")
                with phase() as block:
                    @block.sync
                    def _(sp):
                        sp.dma_start(fc[:], a["L3_fc"]).then_inc(in_w, 16)
                        sp.dma_start(at[:].rearrange("p k d -> p (k d)"),
                                     a["L3_at"].unsqueeze(0).to_broadcast([P, 2 * H3 * D])).then_inc(in_w, 16)
                        for k, (n, o) in {"ew": (4, 0), "mw": (4, 4), "oew": (1, 8), "omw": (1, 9)}.items():
                            sp.dma_start(coef[:, o:o + n], a["L3_" + k].unsqueeze(0).to_broadcast([P, n]))\
                                .then_inc(in_w, 16)
                        sp.wait_ge(in_w, 16 * 6)

                    @block.vector
                    def _(dve):
                        link = Chain(dve, "l3_prep_step").link
                        link(dve.memset(acc[:], 1.0))

                def scratch(s_):
                    return {"ps": PS(s_, "l3_ps", [P, NBU, 512]), "mm": sem("l3_mm"),
                            "t": SB(s_, "l3_t", [P, H3, D]), "r": SB(s_, "l3_r", [P, H3]), "as": SB(s_, "l3_as", [P, NB, H3])}

                def tensor(pe, s, i, xt):
                    for u in range(NBU):
                        pe.matmul(s["ps"][:, u, :], lhsT=xt[:, u, :], rhs=fc[:], start=True, stop=True)\
                            .then_inc(s["mm"], 1)

                def vector(dve, link, s, i):
                    for u in range(NBU):
                        b = i * NBU + u
                        dve.wait_ge(s["mm"], i * NBU + (u + 1))
                        z = acc4[:, bass.ds(b, 1), :, 0:D].rearrange("p b h d -> p (b h) d")
                        leaky(dve, link, z, s["ps"][:, u, :].rearrange("p (h d) -> p h d", h=H3), s["t"][:])
                        for k, o in ((0, s["as"][:, bass.ds(b, 1), :].rearrange("p b h -> p (b h)")),
                                     (1, a_dst[:, bass.ds(b * H3, H3)])):
                            link(dve.tensor_tensor(s["t"][:], z, at[:, k, :].rearrange("p (h d) -> p h d", h=H3),
                                                   ALU.mult))
                            link(dve.tensor_reduce(s["r"][:], s["t"][:], AX.X, ALU.add))
                            link(move(dve, o, s["r"][:]))

                def store(sp, s, outs):
                    sp.dma_start(t_z.rearrange("(b p) d -> p b d", p=P),
                                 acc[:].rearrange("p (b d) -> p b d", b=NB)).then_inc(outs, 16)
                    sp.dma_start(t_as.rearrange("(b p) d -> p b d", p=P), s["as"][:]).then_inc(outs, 16)
                    return 2
                node_stage("l3n", blocks_of(X), 1, tensor, vector, 8 * NBU, nothing, scratch, store=store)
            gat_scores("l3s", H3, t_as, a_dst, coef[:, 0:4], coef[:, 4:8])
            edge_sums("l3e", t_z, H3 * ZW, src_i, dloc, blk_i, att, H3, ZW, acc, 2)

            def divide(name, view, heads):
                with ExitStack() as s2:
                    den = SB(s2, name + "_den", [P, NB, heads])
                    with phase() as block:
                        @block.vector
                        def _(dve):
                            link = Chain(dve, name + "_step").link
                            link(dve.tensor_scalar(den[:].unsqueeze(3), view[:, :, :, D:ZW], 1e-30, None, ALU.max))
                            link(dve.reciprocal(den[:], den[:]))
                            for h in range(heads):
                                z = view[:, :, h, 0:D]
                                link(dve.tensor_tensor(z, z, den[:, :, h:h + 1].to_broadcast([P, NB, D]), ALU.mult))
                                link(dve.scalar_tensor_tensor(z, z, 0.01, z, ALU.mult, ALU.max))
            divide("l3d", acc4, H3)

            zo = SB(st, "l3_zo", [P, NB, ZW])
            with ExitStack() as s2:
                ofc = SB(s2, "l3_ofc", [P, H3, D])
                oat = SB(s2, "l3_oat", [P, 2, D])
                aos = SB(s2, "l3_aos", [P, NB, H3])
                in_w = sem("l3_out_weights")
                with phase() as block:
                    @block.sync
                    def _(sp):
                        sp.dma_start(ofc[:], a["L3_ofc"]).then_inc(in_w, 16)
                        sp.dma_start(oat[:].rearrange("p k d -> p (k d)"),
                                     a["L3_oat"].unsqueeze(0).to_broadcast([P, 2 * D])).then_inc(in_w, 16)
                        sp.wait_ge(in_w, 32)

                    @block.vector
                    def _(dve):
                        link = Chain(dve, "l3_oprep_step").link
                        link(dve.memset(zo[:], 1.0))
                        link(dve.memset(aos[:], 0.0))

                def scratch(s_):
                    return {"ps": PS(s_, "l3o_ps", [P, NBU, 512]), "mm": sem("l3o_mm"),
                            "t": SB(s_, "l3o_t", [P, D]), "r": SB(s_, "l3o_r", [P, 1])}

                def fill(pool, link, stage, i):
                    for h in range(H3):
                        link(pool.tensor_copy(stage[:].rearrange("p (b h) d -> p b h d", h=H3)[:, :, h, :],
                                              acc4[:, bass.ds(i * NBU, NBU), h, 0:D]))

                def tensor(pe, s, i, xt):
                    for u in range(NBU):
                        for k in range(H3):
                            ins = pe.matmul(s["ps"][:, u, 0:D], lhsT=xt[:, u * H3 + k, :], rhs=ofc[:, k, :],
                                            start=k == 0, stop=k == H3 - 1)
                        ins.then_inc(s["mm"], 1)

                def vector(dve, link, s, i):
                    for u in range(NBU):
                        b = i * NBU + u
                        dve.wait_ge(s["mm"], i * NBU + (u + 1))
                        z = zo[:, bass.ds(b, 1), 0:D].rearrange("p b d -> p (b d)")
                        leaky(dve, link, z, s["ps"][:, u, 0:D], s["t"][:])
                        for k, o in ((0, aos[:, bass.ds(b, 1), 0:1].rearrange("p b o -> p (b o)")), (1, ao_dst[:, bass.ds(b, 1)])):
                            link(dve.tensor_tensor(s["t"][:], z, oat[:, k, :], ALU.mult))
                            link(dve.tensor_reduce(s["r"][:], s["t"][:], AX.X, ALU.add))
                            link(move(dve, o, s["r"][:]))

                def store(sp, s, outs):
                    sp.dma_start(t_zo.rearrange("(b p) d -> p b d", p=P), zo[:]).then_inc(outs, 16)
                    sp.dma_start(t_ao.rearrange("(b p) d -> p b d", p=P), aos[:]).then_inc(outs, 16)
                    return 2
                node_stage("l3o", (fill, H3), H3, tensor, vector, 8 * NBU, nothing, scratch, store=store)
            gat_scores("l3t", 1, t_ao, ao_dst, coef[:, 8:9], coef[:, 9:10])
            oacc = zo[:].rearrange("p b d -> p (b d)")
            edge_sums("l3f", t_zo, ZW, src_i, dloc, blk_i, att, 1, ZW, oacc, 1)
            divide("l3g", zo[:].unsqueeze(2), 1)

            upd = acc[:, 0:NB * D].rearrange("p (b d) -> p b d", b=NB)
            with ExitStack() as s2:
                wih = SB(s2, "gru_wih", [P, 3 * D])
                whh = SB(s2, "gru_whh", [P, 3 * D])
                gb = SB(s2, "gru_b", [1, 2, 3 * D])
                in_w = sem("gru_in")
                with phase() as block:
                    @block.sync
                    def _(sp):
                        sp.dma_start(wih[:], a["L3_wih"]).then_inc(in_w, 16)
                        sp.dma_start(whh[:], a["L3_whh"]).then_inc(in_w, 16)
                        sp.dma_start(gb[:, 0, :], a["L3_bih"].unsqueeze(0)).then_inc(in_w, 16)
                        sp.dma_start(gb[:, 1, :], a["L3_bhh"].unsqueeze(0)).then_inc(in_w, 16)
                        sp.wait_ge(in_w, 64)

                def scratch(s_):
                    s = {"ps": PS(s_, "gru_ps", [P, NBU, 512]), "rz": SB(s_, "gru_rz", [P, NBU, 2 * D]),
                         "n": SB(s_, "gru_n", [P, NBU, D]), "d": SB(s_, "gru_d", [P, NBU, D])}
                    for k in ("mm", "gates", "pre", "new"):
                        s[k] = sem("gru_" + k)
                    return s

                def fill(pool, link, stage, i):
                    link(pool.tensor_copy(stage[:, 0:NBU, :], zo[:, bass.ds(i * NBU, NBU), 0:D]))
                    link(pool.tensor_copy(stage[:, NBU:2 * NBU, :], X[:, bass.ds(i * NBU, NBU), :]))

                def tensor(pe, s, i, xt):
                    for u in range(NBU):
                        o = s["ps"][:, u, :]
                        pe.matmul(o[:, 0:256], lhsT=xt[:, u, :], rhs=wih[:, 0:256], start=True, stop=False)
                        pe.matmul(o[:, 0:256], lhsT=xt[:, NBU + u, :], rhs=whh[:, 0:256], start=False, stop=False)
                        pe.matmul(o[:, 0:256], lhsT=ones[0:1, :], rhs=gb[:, 0, 0:256], start=False, stop=False)
                        pe.matmul(o[:, 0:256], lhsT=ones[0:1, :], rhs=gb[:, 1, 0:256], start=False, stop=True)
                        for k, (w, x0) in enumerate(((wih, 0), (whh, NBU))):
                            v = o[:, 256 + k * D:256 + (k + 1) * D]
                            pe.matmul(v, lhsT=xt[:, x0 + u, :], rhs=w[:, 256:384], start=True, stop=False)
                            ins = pe.matmul(v, lhsT=ones[0:1, :], rhs=gb[:, k, 256:384], start=False, stop=True)
                    ins.then_inc(s["mm"], 1)

                def scalar(act, link, s, i):
                    act.wait_ge(s["mm"], i + 1)
                    link(act.activation(s["rz"][:], s["ps"][:, :, 0:256], ACT.Sigmoid))
                    act.sem_inc(s["gates"], 1)
                    act.wait_ge(s["pre"], i + 1)
                    link(act.activation(s["n"][:], s["d"][:], ACT.Tanh))
                    act.sem_inc(s["new"], 1)

                def vector(dve, link, s, i):
                    dve.wait_ge(s["gates"], i + 1)
                    link(dve.tensor_tensor(s["d"][:], s["rz"][:, :, 0:D], s["ps"][:, :, 384:512], ALU.mult))
                    link(dve.tensor_tensor(s["d"][:], s["d"][:], s["ps"][:, :, 256:384], ALU.add))
                    dve.sem_inc(s["pre"], 1)
                    dve.wait_ge(s["new"], i + 1)
                    x = X[:, bass.ds(i * NBU, NBU), :]
                    link(dve.tensor_tensor(s["d"][:], x, s["n"][:], ALU.subtract))
                    link(dve.tensor_tensor(s["d"][:], s["d"][:], s["rz"][:, :, D:2 * D], ALU.mult))
                    link(dve.tensor_tensor(s["d"][:], s["d"][:], s["n"][:], ALU.add))
                    link(dve.scalar_tensor_tensor(upd[:, bass.ds(i * NBU, NBU), :], s["d"][:], 0.01, s["d"][:],
                                                  ALU.mult, ALU.max))
                node_stage("gru", (fill, 2), 2, tensor, vector, 6, scalar, scratch, n_scalar=2)
            add_norm("l3y", upd, False, last=True)



def kernel(**inputs):
    import numpy as np
    import concourse.bacc as _bacc
    from concourse import mybir as _mybir
    from concourse.bass_utils import run_bass_kernel_spmd as _run

    i = {k: np.asarray(v) for k, v in inputs.items()}
    pad = TR * P - N_EDGES

    def tiled(v, fill):
        v = np.pad(v, [(0, pad)] + [(0, 0)] * (v.ndim - 1), constant_values=fill)
        return np.ascontiguousarray(np.swapaxes(v.reshape((TR, P) + v.shape[1:]), 0, 1))

    line = np.pad(i["dst"], (0, pad + 1), constant_values=NP)
    arrays = {
        "x": np.pad(i["x"], [(0, NP - N_NODES), (0, 0)]),
        "src": tiled(i["src"], -1), "dst": tiled(i["dst"], -1), "typ": tiled(i["edge_type_3"], 0),
        "w": tiled(i["edge_weight"], 0), "w1": tiled(i["edge_weight1"][:, 0], 0),
        "f": tiled(i["edge_attr3_1x32"][:, 0, :], 0),
        "dst_line": np.ascontiguousarray(np.stack([line[p * TR:(p + 1) * TR + 1] for p in range(P)])),
        "L0_w": i["L0_gnn_weight"],
    }
    for k in ("Wk", "Wq"):
        arrays["L1_" + k] = np.ascontiguousarray(i["L1_gnn_" + k].T)
    for k in ("Wv", "bk", "bq", "bv", "rel_msg"):
        arrays["L1_" + k] = i["L1_gnn_" + k]
    arrays["L1_rel"] = i["L1_gnn_rel_att"].reshape(D)
    for k in ("W_in", "Wf1", "bf1", "Wf2", "bf2", "Wo1", "bo1", "Wo2", "bo2"):
        arrays["L2_" + k] = i["L2_gnn_" + k]
    arrays["L3_fc"] = np.ascontiguousarray(i["L3_gnn_fc_W"].transpose(2, 0, 1).reshape(D, H3 * D))
    arrays["L3_at"] = np.ascontiguousarray(i["L3_gnn_attn_W"].reshape(H3, 2, D).transpose(1, 0, 2).reshape(2 * H3 * D))
    arrays["L3_ew"] = i["L3_gnn_edge_w"].reshape(H3)
    arrays["L3_mw"] = i["L3_gnn_m_w"].reshape(H3)
    arrays["L3_ofc"] = np.ascontiguousarray(i["L3_gnn_out_fc_W"].T.reshape(H3, D, D).transpose(1, 0, 2))
    arrays["L3_oat"] = i["L3_gnn_out_attn_W"].reshape(2 * D)
    arrays["L3_oew"] = i["L3_gnn_out_edge_w"].reshape(1)
    arrays["L3_omw"] = i["L3_gnn_out_m_w"].reshape(1)
    arrays["L3_wih"] = np.ascontiguousarray(i["L3_gnn_gru_Wih"].T)
    arrays["L3_whh"] = np.ascontiguousarray(i["L3_gnn_gru_Whh"].T)
    arrays["L3_bih"] = i["L3_gnn_gru_bih"]
    arrays["L3_bhh"] = i["L3_gnn_gru_bhh"]

    nc = _bacc.Bacc("TRN2", target_bir_lowering=False, num_devices=1)
    aps, feeds = {}, {}
    for k, v in arrays.items():
        feeds["in_" + k] = np.ascontiguousarray(v)
        aps[k] = nc.dram_tensor("in_" + k, v.shape, _mybir.dt.from_np(v.dtype), kind="ExternalInput").ap()
    out = nc.dram_tensor("out_0", (N_NODES, D), _mybir.dt.float32, kind="ExternalOutput").ap()
    gnn_program(nc, aps, out)
    return _run(nc, [feeds], core_ids=[0]).results[0]["out_0"]
```

```python
import concourse.bass as bass
from concourse import mybir
from contextlib import ExitStack, contextmanager

F32 = mybir.dt.float32
BF16 = mybir.dt.bfloat16
I32 = mybir.dt.int32
ALU = mybir.AluOpType
ACT = mybir.ActivationFunctionType
AX = mybir.AxisListType

P = 128
N_NODES, N_EDGES, D = 3125, 50000, 128
NB = -(-N_NODES // P)
NP = NB * P
TR = -(-N_EDGES // P)
LAST = N_EDGES - (TR - 1) * P
T = TR + NB
G = 4
STEPS = T // (4 * G)
H1, DK = 8, 16
H3 = 4
ZW = D + 1
CH = 16
CT = T // CH
SC = CT * P
FR = 36
BIG = 1.0e30
LOG2 = 0.6931471805599453
EPS = 1e-5
NBU, NBI = 5, 5
assert STEPS * 4 * G == T and NBU * NBI == NB and CH * CT == T and NP == NB * P


def gnn_program(nc, a, out):
    top = ExitStack()

    def dram(name, shape):
        return nc.dram_tensor(name, shape, F32, kind="Internal").ap()

    rec_d = dram("rec_d", (P * T, 8))
    rec_s = dram("rec_s", (P * T, FR))
    rec_tmp = dram("rec_tmp", (P * TR, 8))
    t_hr = dram("t_hr", (3 * NP, D))
    t_k = dram("t_k", (NP, D + H1))
    t_v = dram("t_v", (NP, D))
    t_h = dram("t_h", (NP, D))
    t_z = dram("t_z", (NP, H3 * ZW))
    t_as = dram("t_as", (NP, H3))
    t_zo = dram("t_zo", (NP, ZW))
    t_ao = dram("t_ao", (NP, H3))

    with top:
        def SB(stack, name, shape, dt=F32):
            return stack.enter_context(nc.sbuf_tensor(name, shape, dt))

        def PS(stack, name, shape, dt=F32):
            return stack.enter_context(nc.psum_tensor(name, shape, dt))

        phase_sems = []

        def sem(name):
            phase_sems.append(nc.alloc_semaphore(name))
            return phase_sems[-1]

        def end_phase():
            nc.clear_and_free_semaphores(list(phase_sems))
            phase_sems.clear()
            nc.all_engine_barrier()

        @contextmanager
        def phase():
            with nc.Block() as block:
                yield block
            end_phase()

        def move(dve, out_, in_):
            return dve.tensor_scalar(out_, in_, 1.0, None, ALU.mult)

        def split3(dve, link, x, rest, parts):
            link(dve.tensor_copy(parts[0], x))
            link(dve.tensor_tensor(rest, x, parts[0], ALU.subtract))
            link(dve.tensor_copy(parts[1], rest))
            link(dve.tensor_tensor(rest, rest, parts[1], ALU.subtract))
            link(dve.tensor_copy(parts[2], rest))

        class Chain:

            def __init__(self, eng, name):
                self.eng, self.done, self.n, self.base, self.mark = eng, sem(name), 0, 0, 0

            def link(self, ins):
                self.n += 1
                ins.then_inc(self.done, 1)
                self.eng.wait_ge(self.done, self.base + self.n)

            @contextmanager
            def loop(self, lo, hi, per):
                before, self.n = self.n, 0
                with self.eng.Fori(lo, hi) as i:
                    self.base = (i - lo) * per + before
                    yield i
                    assert self.n == per, self.n
                self.base, self.n = 0, before + (hi - lo) * per

        def sb(name, shape, dt=F32):
            return SB(top, name, shape, dt)

        X = sb("X", [P, NB, D])
        iota_f = sb("iota_f", [P, P])
        iota_i = sb("iota_i", [P, P], I32)
        pid_i = sb("pid_i", [P, 1], I32)
        pid = sb("pid", [P, 3])
        ident = sb("ident", [P, P])
        below = sb("below", [P, P])
        above = sb("above", [P, P])
        tri_m1 = sb("tri_m1", [P, P], BF16)
        ones_bf = sb("ones_bf", [P, P], BF16)
        ones = sb("ones", [P, P])
        src_i = sb("src_i", [P, T], I32)
        hr_i = sb("hr_i", [P, T], I32)
        blk_i = sb("blk_i", [P, T], I32)
        dloc = sb("dloc", [P, T])
        ew = sb("ew", [P, T])
        ew1 = sb("ew1", [P, T])
        rs4 = sb("rs4", [P, T, 4])
        dst2_i = sb("dst2_i", [P, T], I32)
        sblk_i = sb("sblk_i", [P, T], I32)
        unsorted_i = sb("unsorted_i", [P, 1], I32)
        reset = sb("reset", [P, SC + 1])
        att = sb("att", [P, T, 8])

        def rank_vector(dve, c, s, key, place, align):
            link = c.link
            link(dve.memset(s["zero"][:], 0.0))
            link(dve.memset(s["base"][:], 0.0))
            link(dve.memset(place[:], 0.0))
            with c.loop(0, NB, 9 if align else 7) as b:
                link(dve.tensor_scalar(s["hit"][:], key[:], 0.0, None, ALU.is_equal))
                dve.sem_inc(s["hit_ready"], 1)
                link(dve.tensor_scalar(key[:], key[:], -1.0, None, ALU.add))
                dve.wait_ge(s["counted"], b + 1)
                link(dve.tensor_tensor_scan(s["run"][:], s["ps_tot"][:, 0:TR], s["zero"][:], s["base"][:, 0:1],
                                       ALU.add, ALU.add))
                link(dve.tensor_tensor(s["spot"][:], s["run"][:], s["ps_pre"][:, 0:TR], ALU.add))
                link(dve.tensor_tensor(s["spot"][:], s["spot"][:], s["hit"][:], ALU.mult))
                link(dve.tensor_tensor(place[:], place[:], s["spot"][:], ALU.add))
                if align:
                    link(dve.tensor_scalar(s["base_i"][:], s["run"][:, TR - 1:TR], float(P - 1), None, ALU.add))
                    link(dve.tensor_scalar(s["base_i"][:], s["base_i"][:], -P, None, ALU.bitwise_and))
                    link(dve.tensor_copy(s["base"][:], s["base_i"][:]))
                else:
                    link(dve.tensor_copy(s["base"][:], s["run"][:, TR - 1:TR]))

        def rank_tensor(pe, s):
            with pe.Fori(0, NB) as b:
                pe.wait_ge(s["hit_ready"], b + 1)
                pe.matmul(s["ps_pre"][:, 0:TR], lhsT=tri_m1[:], rhs=s["hit"][:], start=True, stop=True)
                pe.matmul(s["ps_tot"][:, 0:TR], lhsT=ones_bf[:], rhs=s["hit"][:],
                          start=True, stop=True).then_inc(s["counted"], 1)

        def place_to_row(dve, link, s, place, row, final):
            link(dve.tensor_copy(s["pl_i"][:], place[:]))
            link(dve.tensor_scalar(s["lo_i"][:], s["pl_i"][:], P - 1, None, ALU.bitwise_and))
            link(dve.tensor_scalar(s["pl_i"][:], s["pl_i"][:], 7, None, ALU.arith_shift_right))
            link(dve.tensor_copy(s["run"][:], s["lo_i"][:]))
            link(dve.tensor_copy(s["spot"][:], s["pl_i"][:]))
            if final:
                link(dve.memset(s["zero"][:], 0.0))
                for k in range(1, CH):
                    link(dve.scalar_tensor_tensor(s["zero"][:], s["spot"][:], float(CT * k), s["zero"][:],
                                             ALU.is_ge, ALU.add))
                link(dve.tensor_scalar(s["spot"][:], s["spot"][:], float(CH), None, ALU.mult))
                link(dve.scalar_tensor_tensor(s["spot"][:], s["zero"][:], float(1 - CH * CT), s["spot"][:],
                                         ALU.mult, ALU.add))
            link(dve.scalar_tensor_tensor(s["run"][:], s["run"][:], float(T if final else TR), s["spot"][:],
                                     ALU.mult, ALU.add))
            link(dve.tensor_copy(row[:], s["run"][:]))

        def rank_scratch(st, name):
            s = {"zero": SB(st, name + "_zero", [P, TR]), "base": SB(st, name + "_base", [P, 1]),
                 "base_i": SB(st, name + "_base_i", [P, 1], I32), "hit": SB(st, name + "_hit", [P, TR], BF16),
                 "run": SB(st, name + "_run", [P, TR]), "spot": SB(st, name + "_spot", [P, TR]),
                 "pl_i": SB(st, name + "_pl_i", [P, TR], I32), "lo_i": SB(st, name + "_lo_i", [P, TR], I32),
                 "ps_pre": PS(st, name + "_ps_pre", [P, 512]), "ps_tot": PS(st, name + "_ps_tot", [P, 512]),
                 "hit_ready": sem(name + "_hit_ready"), "counted": sem(name + "_counted")}
            return s

        SG = 13

        def scatter_pool(pool, s, rows, records, table):
            def half(i, h):
                pool.tensor_copy(s["idx"][:, h, :], rows[:, bass.ds(i * 2 * SG + h * SG, SG)])\
                    .then_inc(s["idx_ready"], 1)
                pool.tensor_copy(s["out"][:, h, :, :], records[:, bass.ds(i * 2 * SG + h * SG, SG), :])\
                    .then_inc(s["idx_ready"], 1)
                pool.wait_ge(s["idx_ready"], i * 4 + 2 * h + 2)
                pool.nop(nofuse=True)
                for u in range(SG):
                    pool.indirect_dma_start(
                        out=table, out_offset=bass.IndirectOffsetOnAxis(ap=s["idx"][:, h, u:u + 1], axis=0),
                        in_=s["out"][:, h, u, :],
                        in_offset=None).then_inc(s["written"][h], 16)
            for h in range(2):
                half(0, h)
            with pool.Fori(1, (TR - 1) // (2 * SG)) as i:
                for h in range(2):
                    pool.wait_ge(s["written"][h], i * (16 * SG))
                    half(i, h)
            for h in range(2):
                pool.wait_ge(s["written"][h], (TR - 1) // 2 * 16)
            pool.tensor_copy(s["idx"][:, 0, 0:1], rows[:, TR - 1:TR]).then_inc(s["idx_ready"], 1)
            pool.wait_ge(s["idx_ready"], (TR - 1) // SG * 2 + 1)
            pool.indirect_dma_start(
                out=table, out_offset=bass.IndirectOffsetOnAxis(ap=s["idx"][0:LAST, 0, 0:1], axis=0),
                in_=records[0:LAST, TR - 1, :], in_offset=None).then_inc(s["written"][0], 16)
            pool.wait_ge(s["written"][0], (TR - 1) // 2 * 16 + 16)

        def scatter_scratch(st, name, width):
            return {"out": SB(st, name + "_out", [P, 2, SG, width]), "idx": SB(st, name + "_idx", [P, 2, SG], I32), "idx_ready": sem(name + "_idx_ready"),
                    "written": [sem(name + f"_written{h}") for h in range(2)]}
        assert (TR - 1) % (2 * SG) == 0

        with ExitStack() as st:
            recs = SB(st, "recs", [P, TR, FR])
            recd = SB(st, "recd", [P, TR, 8])
            key_s = SB(st, "key_s", [P, TR])
            place_s = SB(st, "place_s", [P, TR])
            row_s = SB(st, "row_s", [P, TR], I32)
            key_d = SB(st, "key_d", [P, TR])
            place_d = SB(st, "place_d", [P, TR])
            row_d = SB(st, "row_d", [P, TR], I32)
            c_ready = sem("consts_ready")
            loaded = sem("edges_loaded")
            filled = sem("tables_filled")
            fill_ready = sem("fill_ready")
            with ExitStack() as s2:
                e_src = SB(s2, "e_src", [P, TR], I32)
                e_dst = SB(s2, "e_dst", [P, TR], I32)
                e_typ = SB(s2, "e_typ", [P, TR], I32)
                e_tmp = SB(s2, "e_tmp", [P, TR], I32)
                e_tf = SB(s2, "e_tf", [P, TR])
                e_w = SB(s2, "e_w", [P, 2, TR])
                d_line = SB(s2, "d_line", [P, TR + 1], I32)
                d_viol = SB(s2, "d_viol", [P, TR])
                viol = SB(s2, "viol", [P, 1])
                fill_d = SB(s2, "fill_d", [P, 8])
                fill_s = SB(s2, "fill_s", [P, FR])
                fill_dt = SB(s2, "fill_dt", [P, T, 8])
                fill_st = SB(s2, "fill_st", [P, T // STEPS, FR])
                ps_v = PS(s2, "ps_v", [P, 512])
                viol_ready = sem("viol_ready")
                viol_sum = sem("viol_sum")
                with phase() as block:
                    @block.sync
                    def _(sp):
                        sp.dma_start(e_src[:], a["src"]).then_inc(loaded, 16)
                        sp.dma_start(e_dst[:], a["dst"]).then_inc(loaded, 16)
                        sp.dma_start(e_typ[:], a["typ"]).then_inc(loaded, 16)
                        sp.dma_start(e_w[:, 0, :], a["w"]).then_inc(loaded, 16)
                        sp.dma_start(e_w[:, 1, :], a["w1"]).then_inc(loaded, 16)
                        sp.dma_start(d_line[:], a["dst_line"]).then_inc(loaded, 16)
                        sp.dma_start(X[:], a["x"].rearrange("(b p) d -> p b d", p=P)).then_inc(loaded, 16)
                        sp.dma_start(recs[:, :, 0:32], a["f"]).then_inc(loaded, 16)
                        sp.wait_ge(fill_ready, 1)
                        sp.dma_start(rec_d.rearrange("(p t) f -> p (t f)", p=P),
                                     fill_dt[:].rearrange("p t f -> p (t f)")).then_inc(filled, 16)
                        for c in range(STEPS):
                            sp.dma_start(rec_s.rearrange("(p c t) f -> p c (t f)", p=P, c=STEPS)[:, c, :],
                                         fill_st[:].rearrange("p t f -> p (t f)")).then_inc(filled, 16)
                        sp.dma_start(rec_tmp.rearrange("(p t) f -> p (t f)", p=P),
                                     fill_dt[:, 0:TR, :].rearrange("p t f -> p (t f)")).then_inc(filled, 16)
                        sp.wait_ge(filled, 16 * (STEPS + 2))
                        sp.wait_ge(loaded, 16 * 8)

                    @block.gpsimd
                    def _(pool):
                        pool.iota(iota_i[:], pattern=[[1, P]], base=0, channel_multiplier=0).then_inc(c_ready, 1)
                        pool.iota(pid_i[:], pattern=[[0, 1]], base=0, channel_multiplier=1).then_inc(c_ready, 1)

                    @block.tensor
                    def _(pe):
                        pe.wait_ge(viol_ready, 1)
                        pe.matmul(ps_v[:, 0:1], lhsT=ones[:], rhs=viol[:], start=True, stop=True)\
                            .then_inc(viol_sum, 1)

                    @block.vector
                    def _(dve):
                        link = Chain(dve, "setup_step").link
                        link(dve.memset(fill_d[:], 0.0))
                        link(dve.memset(fill_d[:, 1:2], -1.0))
                        link(dve.memset(fill_d[:, 5:6], -1.0))
                        link(dve.memset(fill_s[:], 0.0))
                        link(dve.memset(fill_s[:, 34:35], -1.0))
                        link(dve.tensor_copy(fill_dt[:], fill_d[:].unsqueeze(1).to_broadcast([P, T, 8])))
                        link(dve.tensor_copy(fill_st[:], fill_s[:].unsqueeze(1).to_broadcast([P, T // STEPS, FR])))
                        dve.sem_inc(fill_ready, 1)
                        dve.wait_ge(c_ready, 2)
                        link(dve.tensor_copy(iota_f[:], iota_i[:]))
                        link(dve.tensor_copy(pid[:, 0:1], pid_i[:]))
                        link(dve.tensor_scalar(pid[:, 1:2], pid[:, 0:1], 8.0, None, ALU.add))
                        link(dve.tensor_scalar(pid[:, 2:3], pid[:, 0:1], -8.0, None, ALU.add))
                        link(dve.tensor_scalar(ident[:], iota_f[:], pid[:, 0:1], None, ALU.is_equal))
                        link(dve.tensor_scalar(below[:], iota_f[:], pid[:, 1:2], None, ALU.is_equal))
                        link(dve.tensor_scalar(above[:], iota_f[:], pid[:, 2:3], None, ALU.is_equal))
                        link(dve.tensor_scalar(tri_m1[:], iota_f[:], pid[:, 0:1], -1.0, ALU.is_le, ALU.mult))
                        link(dve.memset(ones_bf[:], 1.0))
                        link(dve.memset(ones[:], 1.0))
                        dve.wait_ge(loaded, 16 * 8)
                        link(dve.tensor_tensor(d_viol[:], d_line[:, 1:TR + 1], d_line[:, 0:TR], ALU.is_lt))
                        link(dve.tensor_reduce(viol[:], d_viol[:], AX.X, ALU.add))
                        dve.sem_inc(viol_ready, 1)
                        link(dve.tensor_copy(recs[:, :, 32], e_w[:, 1, :]))
                        link(dve.tensor_copy(recs[:, :, 33], e_dst[:]))
                        link(dve.tensor_scalar(e_tmp[:], e_src[:], P - 1, None, ALU.bitwise_and))
                        link(dve.tensor_copy(recs[:, :, 34], e_tmp[:]))
                        link(dve.tensor_scalar(e_tmp[:], e_src[:], 7, None, ALU.arith_shift_right))
                        link(dve.tensor_copy(recs[:, :, 35], e_tmp[:]))
                        link(dve.tensor_copy(key_s[:], e_tmp[:]))
                        link(dve.memset(recd[:], 0.0))
                        link(dve.tensor_copy(recd[:, :, 0], e_src[:]))
                        link(dve.tensor_copy(recd[:, :, 1], e_dst[:]))
                        link(dve.tensor_copy(e_tf[:], e_typ[:]))
                        link(dve.scalar_tensor_tensor(recd[:, :, 2], e_tf[:], float(NP), recd[:, :, 0],
                                                 ALU.mult, ALU.add))
                        link(dve.tensor_copy(recd[:, :, 3], e_w[:, 0, :]))
                        link(dve.tensor_copy(recd[:, :, 4], e_w[:, 1, :]))
                        link(dve.tensor_scalar(e_tmp[:], e_dst[:], P - 1, None, ALU.bitwise_and))
                        link(dve.tensor_copy(recd[:, :, 5], e_tmp[:]))
                        link(dve.tensor_scalar(e_tmp[:], e_dst[:], 7, None, ALU.arith_shift_right))
                        link(dve.tensor_copy(recd[:, :, 6], e_tmp[:]))
                        dve.wait_ge(viol_sum, 1)
                        link(dve.tensor_copy(unsorted_i[:], ps_v[:, 0:1]))

            def bucket_key(dve, link, key, digit, t):
                link(dve.tensor_scalar(t[:], recd[:, :, 1], 0.0, None, ALU.is_ge))
                link(dve.scalar_tensor_tensor(key[:], digit, 1.0, t[:], ALU.add, ALU.mult))
                link(dve.tensor_scalar(key[:], key[:], -1.0, None, ALU.add))

            with ExitStack() as s2:
                rt = [rank_scratch(s2, "rank_t0")]
                sct = [scatter_scratch(s2, "scat_t0", 8)]
                rt.append(dict(rt[0], hit_ready=sem("rank_t1_hit_ready"), counted=sem("rank_t1_counted")))
                sct.append(dict(sct[0], idx_ready=sem("scat_t1_idx_ready"),
                                written=[sem(f"scat_t1_written{h}") for h in range(2)]))
                placed, passed, reloaded = sem("pass_placed"), sem("pass_scattered"), sem("pass_reloaded")

                def out_of_order(eng):
                    return eng.If(eng.value_load(unsorted_i[0:1, 0:1], min_val=0, max_val=P * (TR + 1)))

                with phase() as block:
                    @block.vector
                    def _(dve):
                        c = Chain(dve, "pass_step")
                        with out_of_order(dve):
                            for k in range(2):
                                r = rt[k]
                                if k:
                                    dve.wait_ge(reloaded, 16 * k)
                                c.link(dve.tensor_copy(r["lo_i"][:], recd[:, :, 5]))
                                if k == 0:
                                    c.link(dve.tensor_scalar(r["lo_i"][:], r["lo_i"][:], 15, None, ALU.bitwise_and))
                                else:
                                    c.link(dve.tensor_scalar(r["lo_i"][:], r["lo_i"][:], 4, None,
                                                             ALU.arith_shift_right))
                                c.link(dve.tensor_copy(r["spot"][:], r["lo_i"][:]))
                                bucket_key(dve, c.link, key_d, r["spot"][:], r["run"])
                                rank_vector(dve, c, r, key_d, place_d, False)
                                place_to_row(dve, c.link, r, place_d, row_d, False)
                                dve.sem_inc(placed, 1)

                    @block.tensor
                    def _(pe):
                        with out_of_order(pe):
                            for k in range(2):
                                rank_tensor(pe, rt[k])

                    @block.gpsimd
                    def _(pool):
                        with out_of_order(pool):
                            for k in range(2):
                                pool.wait_ge(placed, k + 1)
                                scatter_pool(pool, sct[k], row_d, recd, rec_tmp)
                                pool.sem_inc(passed, 1)

                    @block.sync
                    def _(sp):
                        with out_of_order(sp):
                            for k in range(2):
                                sp.wait_ge(passed, k + 1)
                                sp.dma_start(recd[:].rearrange("p t f -> p (t f)"),
                                             rec_tmp.rearrange("(p t) f -> p (t f)", p=P)).then_inc(reloaded, 16)
                                sp.wait_ge(reloaded, 16 * (k + 1))

            with ExitStack() as s2:
                rs = rank_scratch(s2, "rank_s")
                with phase() as block:
                    @block.vector
                    def _(dve):
                        c = Chain(dve, "rank_s_step")
                        rank_vector(dve, c, rs, key_s, place_s, True)
                        place_to_row(dve, c.link, rs, place_s, row_s, True)

                    @block.tensor
                    def _(pe):
                        rank_tensor(pe, rs)

            with ExitStack() as s2:
                ss = scatter_scratch(s2, "scat_s", FR)
                rd = rank_scratch(s2, "rank_d")
                with phase() as block:
                    @block.gpsimd
                    def _(pool):
                        scatter_pool(pool, ss, row_s, recs, rec_s)

                    @block.vector
                    def _(dve):
                        c = Chain(dve, "rank_d_step")
                        link = c.link
                        bucket_key(dve, link, key_d, recd[:, :, 6], rd["run"])
                        rank_vector(dve, c, rd, key_d, place_d, True)
                        place_to_row(dve, c.link, rd, place_d, row_d, True)

                    @block.tensor
                    def _(pe):
                        rank_tensor(pe, rd)

            with ExitStack() as s2:
                sd = scatter_scratch(s2, "scat_d", 8)
                with phase() as block:
                    @block.gpsimd
                    def _(pool):
                        scatter_pool(pool, sd, row_d, recd, rec_d)

                    @block.tensor
                    def _(pe):
                        pe.nop()

        def to_scan_tensor(pe, s, data):
            v = data[:].rearrange("p (a c) h -> p a (c h)", c=CH)
            for t in range(CT):
                q, r = divmod(t, 4)
                if r == 0 and q >= 2:
                    pe.wait_ge(s["scan_copied"], q - 1)
                pe.transpose(s["ps_scan"][:, q % 2, r * P:(r + 1) * P], v[:, t, :], ident[:])\
                    .then_inc(s["scan_turned"], 1)

        def to_scan_scalar(act, s, dest):
            for q in range(-(-CT // 4)):
                n = min(4, CT - 4 * q)
                act.wait_ge(s["scan_turned"], 4 * q + n)
                act.copy(dest[:, q * 4 * P:q * 4 * P + n * P], s["ps_scan"][:, q % 2, 0:n * P])\
                    .then_inc(s["scan_copied"], 1)

        with ExitStack() as st:
            rec2 = SB(st, "rec2", [P, T, 8])
            dst8 = SB(st, "dst8", [P, T, 8])
            dscan = SB(st, "dscan", [P, SC + 1])
            s = {"ps_scan": PS(st, "r_ps_scan", [P, 2, 512]), "scan_copied": sem("r_copied"),
                 "scan_turned": sem("r_turned")}
            ps_n = PS(st, "r_ps_n", [P, 512])
            r_loaded = sem("r_loaded")
            r_dst8 = sem("r_dst8")
            r_col = sem("r_col")
            r_shift = sem("r_shift")
            with phase() as block:
                @block.sync
                def _(sp):
                    sp.dma_start(rec2[:].rearrange("p t f -> p (t f)"),
                                 rec_d.rearrange("(p t) f -> p (t f)", p=P)).then_inc(r_loaded, 16)
                    sp.dma_start(rs4[:], rec_s.rearrange("(p t) f -> p t f", p=P)[:, :, 32:36]).then_inc(r_loaded, 16)
                    sp.wait_ge(r_loaded, 32)

                @block.tensor
                def _(pe):
                    pe.wait_ge(r_dst8, 1)
                    to_scan_tensor(pe, s, dst8)
                    pe.wait_ge(s["scan_copied"], -(-CT // 4))
                    pe.matmul(ps_n[:, 0:1], lhsT=below[:], rhs=dscan[:, SC:SC + 1], start=True, stop=True)\
                        .then_inc(r_shift, 1)
                    pe.wait_ge(r_col, 1)
                    pe.matmul(ps_n[:, 1:2], lhsT=above[:], rhs=reset[:, 0:1], start=True, stop=True)\
                        .then_inc(r_shift, 1)

                @block.scalar
                def _(act):
                    to_scan_scalar(act, s, dscan[:, 1:SC + 1])

                @block.vector
                def _(dve):
                    link = Chain(dve, "reload_step").link
                    dve.wait_ge(r_loaded, 32)
                    link(dve.tensor_copy(dst8[:], rec2[:, :, 1:2].to_broadcast([P, T, 8])))
                    dve.sem_inc(r_dst8, 1)
                    link(dve.tensor_copy(src_i[:], rec2[:, :, 0]))
                    link(dve.tensor_copy(hr_i[:], rec2[:, :, 2]))
                    link(dve.tensor_copy(ew[:], rec2[:, :, 3]))
                    link(dve.tensor_copy(ew1[:], rec2[:, :, 4]))
                    link(dve.tensor_copy(dloc[:], rec2[:, :, 5]))
                    link(dve.tensor_copy(blk_i[:], rec2[:, :, 6]))
                    link(dve.tensor_copy(dst2_i[:], rs4[:, :, 1]))
                    link(dve.tensor_copy(sblk_i[:], rs4[:, :, 3]))
                    dve.wait_ge(r_shift, 1)
                    link(dve.tensor_copy(dscan[:, 0:1], ps_n[:, 0:1]))
                    link(dve.tensor_tensor(reset[:, 0:SC], dscan[:, 1:SC + 1], dscan[:, 0:SC], ALU.not_equal))
                    link(dve.tensor_scalar(reset[:, 0:SC], reset[:, 0:SC], -BIG, None, ALU.mult))
                    dve.sem_inc(r_col, 1)
                    dve.wait_ge(r_shift, 2)
                    link(dve.tensor_copy(reset[:, SC:SC + 1], ps_n[:, 1:2]))

        def segment_exp(name):
            with ExitStack() as st:
                sc = SB(st, name + "_sc", [P, SC])
                fw = SB(st, name + "_fw", [P, SC])
                col = SB(st, name + "_col", [P, 4])
                rowb = SB(st, name + "_row", [1, 4, P])
                s = {"ps_scan": PS(st, name + "_ps_scan", [P, 2, 512]), "scan_copied": sem(name + "_copied"),
                     "scan_turned": sem(name + "_turned")}
                ps_b = PS(st, name + "_ps_b", [P, 2, 512])
                ps_r = PS(st, name + "_ps_r", [P, 512])
                ps_c = PS(st, name + "_ps_c", [P, 512])
                c_ends, c_rows, c_carry, c_col = (sem(name + n) for n in ("_ends", "_rows", "_carry", "_col"))
                m_ready, m_back, m_used = (sem(name + n) for n in ("_max", "_back", "_used"))
                e_done = sem(name + "_exp")
                vb = att[:].rearrange("p (a c) h -> p (a c h)", c=CH)
                with phase() as block:
                    @block.tensor
                    def _(pe):
                        to_scan_tensor(pe, s, att)
                        for k in range(2):
                            pe.wait_ge(c_ends, k + 1)
                            pe.matmul(ps_r[0:1, 0:P], lhsT=col[:, 2 * k:2 * k + 1], rhs=ident[:],
                                      start=True, stop=True)
                            pe.matmul(ps_r[0:1, P:2 * P], lhsT=col[:, 2 * k + 1:2 * k + 2], rhs=ident[:],
                                      start=True, stop=True).then_inc(c_rows, 1)
                            pe.wait_ge(c_carry, k + 1)
                            pe.matmul(ps_c[:, k:k + 1], lhsT=rowb[0:1, 3, :], rhs=ones[0:1, 0:1],
                                      start=True, stop=True).then_inc(c_col, 1)
                        pe.wait_ge(m_ready, 1)
                        for t in range(CT):
                            q, r = divmod(t, 4)
                            if r == 0 and q >= 2:
                                pe.wait_ge(m_used, q - 1)
                            pe.transpose(ps_b[:, q % 2, r * P:(r + 1) * P], sc[:, t * P:(t + 1) * P], ident[:])\
                                .then_inc(m_back, 1)

                    @block.scalar
                    def _(act):
                        to_scan_scalar(act, s, sc)
                        act.wait_ge(m_used, -(-CT // 4))
                        act.activation(att[:].rearrange("p t h -> p (t h)"), att[:].rearrange("p t h -> p (t h)"),
                                       ACT.Exp).then_inc(e_done, 1)

                    @block.vector
                    def _(dve):
                        link = Chain(dve, name + "_step").link
                        r_fw, r_bw = reset[:, 0:SC], reset[:, 1:SC + 1]
                        dve.wait_ge(s["scan_copied"], -(-CT // 4))
                        link(dve.tensor_reduce(col[:, 1:2], r_fw, AX.X, ALU.min))
                        link(dve.tensor_reduce(col[:, 3:4], r_bw, AX.X, ALU.min))
                        for k in range(2):
                            if k == 0:
                                o, r, x = fw[:], r_fw, sc[:]
                                end = fw[:, SC - 1:SC]
                            else:
                                o, r, x = sc[:, ::-1], r_bw[:, ::-1], fw[:, ::-1]
                                end = sc[:, 0:1]
                            link(dve.tensor_tensor_scan(o, r, x, -BIG, ALU.add, ALU.max))
                            link(dve.tensor_copy(col[:, 2 * k:2 * k + 1], end))
                            dve.sem_inc(c_ends, 1)
                            dve.wait_ge(c_rows, k + 1)
                            link(dve.tensor_copy(rowb[0:1, 0, :].rearrange("o (h c) -> o c h", h=8),
                                            ps_r[0:1, 0:P].rearrange("o (c h) -> o c h", h=8)))
                            link(dve.tensor_copy(rowb[0:1, 1, :].rearrange("o (h c) -> o c h", h=8),
                                            ps_r[0:1, P:2 * P].rearrange("o (c h) -> o c h", h=8)))
                            first = CH - 1 if k else 0
                            link(dve.memset(rowb[0:1, 1, :].rearrange("o (h c) -> o h c", h=8)[:, :, first:first + 1], -BIG))
                            rv = (lambda n: rowb[0:1, n, ::-1]) if k else (lambda n: rowb[0:1, n, :])
                            link(dve.tensor_tensor_scan(rv(2), rv(1), rv(0), -BIG, ALU.add, ALU.max))
                            link(dve.memset(rowb[0:1, 3, :], -BIG))
                            src = rowb[0:1, 2, :].rearrange("o (h c) -> o c h", h=8)
                            dst = rowb[0:1, 3, :].rearrange("o (c h) -> o c h", h=8)
                            if k == 0:
                                link(dve.tensor_copy(dst[:, 1:CH, :], src[:, 0:CH - 1, :]))
                                dve.sem_inc(c_carry, 1)
                            else:
                                link(dve.tensor_copy(dst[:, 0:CH - 1, :], src[:, 1:CH, :]))
                                dve.sem_inc(c_carry, 1)
                            dve.wait_ge(c_col, k + 1)
                            link(dve.tensor_copy(col[:, 2 * k:2 * k + 1], ps_c[:, k:k + 1]))
                            link(dve.tensor_tensor_scan(o, r, x, col[:, 2 * k:2 * k + 1], ALU.add, ALU.max))
                        dve.sem_inc(m_ready, 1)
                        for q in range(-(-CT // 4)):
                            n = min(4, CT - 4 * q)
                            dve.wait_ge(m_back, 4 * q + n)
                            av = vb[:, 4 * q * P:(4 * q + n) * P]
                            dve.tensor_tensor(av, av, ps_b[:, q % 2, 0:n * P], ALU.subtract).then_inc(m_used, 1)

        def rolled(eng, body, chain=None):
            body(0)
            if chain is None:
                with eng.Fori(1, STEPS - 1) as i:
                    body(i)
            else:
                with chain.loop(1, STEPS - 1, chain.n - chain.mark) as i:
                    body(i)
            body(STEPS - 1)

        def wait(eng, s, value):
            if not (isinstance(value, int) and value <= 0):
                eng.wait_ge(s, value)

        def exists(i, q):
            return q < 4 or not (isinstance(i, int) and i == STEPS - 1)

        def block_numbers(eng, engine_type, blocks, t):
            return nc.values_load_multi_w_load_instructions(
                blocks[0:1, bass.ds(t, G)], engines=(engine_type,), min_val=0, max_val=NB - 1)[1]

        def gather_ring(pool, table, idx_all, idx, gat, idx_ready, got, used, used_per_quarter):
            def indices(i, q):
                if q < 4:
                    wait(pool, got[q], i * (16 * G))
                else:
                    pool.wait_ge(got[q - 4], (i + 1) * (16 * G))
                pool.nop(nofuse=True)
                pool.tensor_copy(idx[:, q % 4, :], idx_all[:, bass.ds(i * 16 + q * G, G)]).then_inc(idx_ready, 1)

            def body(i):
                for q in range(4):
                    if exists(i, q + 1):
                        indices(i, q + 1)
                    wait(pool, used, (i * 4 + (q - 3)) * used_per_quarter)
                    pool.wait_ge(idx_ready, i * 4 + (q + 1))
                    pool.nop(nofuse=True)
                    for u in range(G):
                        pool.indirect_dma_start(
                            out=gat[:, q, u, :], out_offset=None, in_=table,
                            in_offset=bass.IndirectOffsetOnAxis(ap=idx[:, q, u:u + 1], axis=0))\
                            .then_inc(got[q], 16)
            indices(0, 0)
            rolled(pool, body)

        def edge_scores(name, table, wt, node_rows, wn, combine):
            with ExitStack() as st:
                gat = SB(st, name + "_gat", [P, 4, G, wt])
                idx = SB(st, name + "_idx", [P, 4, G], I32)
                loc = SB(st, name + "_loc", [P, 2, G])
                hot = SB(st, name + "_hot", [P, 2, G, P])
                hot_t = SB(st, name + "_hot_t", [P, 2, G, P])
                prod = SB(st, name + "_prod", [P, G, P])
                red = SB(st, name + "_red", [P, G, 8])
                tmp = SB(st, name + "_tmp", [P, G, 8])
                ps_t = PS(st, name + "_ps_t", [P, 2, G, P])
                ps_q = PS(st, name + "_ps_q", [P, 2, G, P])
                idx_ready, hot_ready, turned, copied, spread, scored = (
                    sem(name + n) for n in ("_idx_ready", "_hot_ready", "_turned", "_copied", "_spread", "_scored"))
                got = [sem(name + f"_got{q}") for q in range(4)]
                with phase() as block:
                    @block.gpsimd
                    def _(pool):
                        gather_ring(pool, table, src_i, idx, gat, idx_ready, got, scored, 1)

                    @block.vector
                    def _(dve):
                        c = Chain(dve, name + "_step")

                        def one_hots(i, q):
                            wait(dve, turned, i * 4 + (q - 1))
                            c.link(move(dve, loc[:, q % 2, :], dloc[:, bass.ds(i * 16 + q * G, G)]))
                            for u in range(G):
                                ins = dve.tensor_scalar(hot[:, q % 2, u, :], iota_f[:], loc[:, q % 2, u:u + 1], None,
                                                        ALU.is_equal)
                            ins.then_inc(hot_ready, 1)

                        def body(i):
                            for q in range(4):
                                if exists(i, q + 2):
                                    one_hots(i, q + 2)
                                dve.wait_ge(got[q], (i + 1) * (16 * G))
                                dve.wait_ge(spread, i * 4 + (q + 1))
                                combine(dve, c.link, i * 16 + q * G, gat[:, q, :, :], ps_q[:, q % 2, :, :],
                                        prod, red, tmp)
                                dve.sem_inc(scored, 1)
                        one_hots(0, 0)
                        one_hots(0, 1)
                        c.mark = c.n
                        rolled(dve, body, c)

                    @block.tensor
                    def _(pe):
                        def turn(i, q):
                            pe.wait_ge(hot_ready, i * 4 + (q + 1))
                            wait(pe, copied, i * 4 + (q - 1))
                            for u in range(G):
                                ins = pe.transpose(ps_t[:, q % 2, u, :], hot[:, q % 2, u, :], ident[:])
                            ins.then_inc(turned, 1)

                        def spread_rows(i, q):
                            ks = block_numbers(pe, mybir.EngineType.PE, blk_i, i * 16 + q * G)
                            pe.wait_ge(copied, i * 4 + (q + 1))
                            wait(pe, scored, i * 4 + (q - 1))
                            for u in range(G):
                                ins = pe.matmul(ps_q[:, q % 2, u, 0:wn], lhsT=hot_t[:, q % 2, u, :],
                                                rhs=node_rows[:, bass.ds(ks[u] * wn, wn)],
                                                start=True, stop=True)
                            ins.then_inc(spread, 1)

                        def body(i):
                            for q in range(4):
                                if exists(i, q + 1):
                                    spread_rows(i, q + 1)
                                if exists(i, q + 2):
                                    turn(i, q + 2)
                        turn(0, 0)
                        turn(0, 1)
                        spread_rows(0, 0)
                        rolled(pe, body)

                    @block.scalar
                    def _(act):
                        def body(i):
                            for q in range(4):
                                act.wait_ge(turned, i * 4 + (q + 1))
                                wait(act, spread, i * 4 + (q - 1))
                                act.copy(hot_t[:, q % 2, :, :], ps_t[:, q % 2, :, :]).then_inc(copied, 1)
                        rolled(act, body)

        def edge_sums(name, table, wt, idx_all, local, blocks, weight, nh, ws, acc, banks, rows=None, mlp=None):
            with ExitStack() as st:
                gat = SB(st, name + "_gat", [P, 4, G, wt])
                idx = SB(st, name + "_idx", [P, 4, G], I32)
                loc = SB(st, name + "_loc", [P, 2, G])
                wgt = SB(st, name + "_wgt", [P, 2, G, 8])
                hot = SB(st, name + "_hot", [P, 2, G, nh, P])
                made = SB(st, name + "_made", [P, 2, G, ws]) if rows else None
                helped = nh > 1
                plain = SB(st, name + "_plain", [P, 2, G, P]) if helped else None
                wgt_a = SB(st, name + "_wgt_a", [P, 2, G, 8]) if helped else None
                plain_ready, weighed, fetched = (sem(name + n) for n in ("_plain_ready", "_weighed", "_fetched"))
                shared = G * ws * banks <= 512
                per = 2 if shared else 8 // banks
                ps = PS(st, name + "_ps", [P, per * banks, 512])
                idx_ready, hot_ready, rows_ready, summed, added = (
                    sem(name + n) for n in ("_idx_ready", "_hot_ready", "_rows_ready", "_summed", "_added"))
                got = [sem(name + f"_got{q}") for q in range(4)]

                def slot(q, u):
                    if shared:
                        return ps[:, q % 2, u * ws:(u + 1) * ws]
                    if banks == 1:
                        return ps[:, (q % 2) * G + u, 0:ws]
                    return ps[:, 2 * u:2 * u + 2, 0:2 * ws]
                m = mlp(st) if mlp else None
                with phase() as block:
                    @block.gpsimd
                    def _(pool):
                        gather_ring(pool, table, idx_all, idx, gat, idx_ready, got, summed, G)

                    @block.vector
                    def _(dve):
                        c = Chain(dve, name + "_step")
                        c.link(dve.memset(acc[:], 0.0))

                        def targets(i, q):
                            t0 = i * 16 + q * G
                            wait(dve, hot_ready, (i * 4 + (q - 1)) * G)
                            ins = move(dve, loc[:, q % 2, :], local[:, bass.ds(t0, G)])
                            if weight is not None:
                                ins = move(dve, wgt[:, q % 2, :, 0:nh], weight[:, bass.ds(t0, G), 0:nh])
                            c.link(ins)

                        def one_hot(i, q, u):
                            b, at_ = q % 2, loc[:, q % 2, u:u + 1]
                            if helped:
                                dve.tensor_scalar(plain[:, b, u, :], iota_f[:], at_, None, ALU.is_equal)\
                                    .then_inc(plain_ready, 1)
                            if weight is None:
                                ins = dve.tensor_scalar(hot[:, b, u, 0, :], iota_f[:], at_, None, ALU.is_equal)
                            else:
                                ins = dve.tensor_scalar(hot[:, b, u, 0, :], iota_f[:], at_,
                                                        wgt[:, b, u, 0:1], ALU.is_equal, ALU.mult)
                            ins.then_inc(hot_ready, 1)

                        def tiles(i, q, add, make):
                            t0 = i * 16 + q * G
                            if add:
                                ks = block_numbers(dve, mybir.EngineType.DVE, blocks, t0)
                            if make:
                                targets(i, q + 2)
                            for u in range(G):
                                if add:
                                    dve.wait_ge(summed, t0 + (G if shared else u + 1))
                                    w = nh * ws
                                    av = acc[:, bass.ds(ks[u] * w, w)]
                                    if banks == 2:
                                        av = av.rearrange("p (a b) -> p a b", a=2)
                                    dve.tensor_tensor(av, av, slot(q % 4, u), ALU.add).then_inc(added, 1)
                                if make:
                                    if helped and add:
                                        dve.wait_ge(weighed, t0 + (u + 1))
                                    one_hot(i, q + 2, u)
                                if add:
                                    dve.wait_ge(added, t0 + (u + 1))

                        def body(i):
                            first = isinstance(i, int) and i == 0
                            for q in range(4):
                                if mlp and exists(i, q + 1):
                                    softplus_vector(dve, c.link, m, i * 4 + (q + 1), (q + 1) % 2)
                                if rows:
                                    dve.wait_ge(got[q], (i + 1) * (16 * G))
                                    rows(dve, c.link, i * 4 + q, q % 2, i * 16 + q * G, gat[:, q, :, :],
                                         made[:, q % 2, :, :], m)
                                    dve.sem_inc(rows_ready, 1)
                                tiles(i, q - 1, q or not first, exists(i, q + 1))
                        if mlp:
                            softplus_vector(dve, c.link, m, 0, 0)
                        tiles(0, -2, False, True)
                        c.mark = c.n
                        rolled(dve, body, c)
                        tiles(STEPS - 1, 3, True, False)

                    @block.tensor
                    def _(pe):
                        def body(i):
                            for q in range(4):
                                if mlp and exists(i, q + 3):
                                    m["turn"](pe, i, q + 3)
                                if mlp and exists(i, q + 2):
                                    m["front"](pe, i, q + 2)
                                if mlp and exists(i, q + 1):
                                    m["back"](pe, i, q + 1)
                                if rows:
                                    pe.wait_ge(rows_ready, i * 4 + (q + 1))
                                else:
                                    pe.wait_ge(got[q], (i + 1) * (16 * G))
                                t0 = i * 16 + q * G
                                for u in range(G):
                                    pe.wait_ge(hot_ready, t0 + (u + 1))
                                    if helped:
                                        pe.wait_ge(weighed, t0 + (u + 1))
                                    wait(pe, added, t0 + (-G if shared else u + 1 - per))
                                    src = made[:, q % 2, u, :] if rows else gat[:, q, u, :]
                                    for k in range(nh):
                                        if banks == 1:
                                            o = slot(q, u)
                                        else:
                                            o = ps[:, u * 2 + k // 2, (k % 2) * ws:(k % 2) * ws + ws]
                                        ins = pe.matmul(o, lhsT=hot[:, q % 2, u, k, :],
                                                        rhs=src[:, k * ws:(k + 1) * ws], start=True, stop=True)
                                    ins.then_inc(summed, 1)
                        if mlp:
                            for q in range(3):
                                m["turn"](pe, 0, q)
                                if q < 2:
                                    m["front"](pe, 0, q)
                            m["back"](pe, 0, 0)
                        rolled(pe, body)

                    if helped:
                        @block.scalar
                        def _(act):
                            def body(i):
                                for q in range(4):
                                    t0 = i * 16 + q * G
                                    wait(act, weighed, t0 - G)
                                    act.copy(wgt_a[:, q % 2, :, 0:nh], weight[:, bass.ds(t0, G), 0:nh])\
                                        .then_inc(fetched, 1)
                                    act.wait_ge(fetched, i * 4 + (q + 1))
                                    for u in range(G):
                                        act.wait_ge(plain_ready, t0 + (u + 1))
                                        wait(act, summed, t0 + (u + 1 - 2 * G))
                                        for k in range(1, nh):
                                            ins = act.activation(hot[:, q % 2, u, k, :], plain[:, q % 2, u, :],
                                                                 ACT.Copy, scale=wgt_a[:, q % 2, u, k:k + 1])
                                        ins.then_inc(weighed, 1)
                            rolled(act, body)

                    if mlp:
                        @block.scalar
                        def _(act):
                            m["scalar"](act)

                        @block.sync
                        def _(sp):
                            m["sync"](sp)

        W5 = NBU * P

        def node_stage(name, fill, kd, tensor, vector, n_vector, scalar, scratch, load=None, store=None,
                       n_scalar=0):
            with ExitStack() as st:
                stage = SB(st, name + "_stage", [P, NBU * kd, P])
                xt = SB(st, name + "_xt", [P, NBU * kd, P])
                nb = -(-NBU * kd // 4)
                ps_x = PS(st, name + "_ps_x", [P, 2, 4, P])
                staged, turned, copied = (sem(name + n) for n in ("_staged", "_turned", "_copied"))
                in_w, outs = sem(name + "_weights"), sem(name + "_stored")
                done_v, taken = sem(name + "_vdone"), sem(name + "_taken")
                s = scratch(st)
                with phase() as block:
                    @block.sync
                    def _(sp):
                        nl = load(sp, s, in_w) if load else 0
                        if store:
                            sp.wait_ge(done_v, 1)
                            ns = store(sp, s, outs)
                            sp.wait_ge(outs, 16 * ns)

                    @block.gpsimd
                    def _(pool):
                        c = Chain(pool, name + "_fill_step")
                        with c.loop(0, NBI, fill[1]) as i:
                            fill[0](pool, c.link, stage, i)
                            pool.sem_inc(staged, 1)
                            pool.wait_ge(turned, (i + 1) * nb)

                    @block.tensor
                    def _(pe):
                        with pe.Fori(0, NBI) as i:
                            pe.wait_ge(staged, i + 1)
                            for q in range(nb):
                                if q >= 2:
                                    pe.wait_ge(copied, i * nb + (q - 1))
                                c = min(4, NBU * kd - 4 * q)
                                for r in range(c):
                                    ins = pe.transpose(ps_x[:, q % 2, r, :], stage[:, 4 * q + r, :], ident[:])
                                ins.then_inc(turned, 1)
                            pe.wait_ge(copied, (i + 1) * nb)
                            tensor(pe, s, i, xt)
                            pe.wait_ge(taken, i + 1)

                    @block.scalar
                    def _(act):
                        steps = Chain(act, name + "_act_step")
                        with steps.loop(0, NBI, n_scalar) as i:
                            for q in range(nb):
                                act.wait_ge(turned, i * nb + (q + 1))
                                c = min(4, NBU * kd - 4 * q)
                                act.copy(xt[:, 4 * q:4 * q + c, :], ps_x[:, q % 2, 0:c, :]).then_inc(copied, 1)
                            scalar(act, steps.link, s, i)

                    @block.vector
                    def _(dve):
                        c = Chain(dve, name + "_step")
                        with c.loop(0, NBI, n_vector) as i:
                            vector(dve, c.link, s, i)
                            dve.sem_inc(taken, 1)
                        dve.sem_inc(done_v, 1)

        def blocks_of(data):
            flat = data[:].rearrange("p b d -> p (b d)") if len(data.shape) == 3 else data[:]

            def fill(pool, link, stage, i):
                link(pool.tensor_copy(stage[:].rearrange("p a d -> p (a d)"), flat[:, bass.ds(i * W5, W5)]))
            return fill, 1

        def nothing(*_):
            pass

        def add_norm(name, update, relu, last=False):
            with ExitStack() as st:
                sq = SB(st, name + "_sq", [P, NB, D])
                mean = SB(st, name + "_mean", [P, NB])
                var = SB(st, name + "_var", [P, NB])
                dev = SB(st, name + "_dev", [P, NB])
                v_ready, r_ready, o_ready, stored = (sem(name + n) for n in ("_var_r", "_dev_r", "_out_r", "_stored"))
                with phase() as block:
                    @block.vector
                    def _(dve):
                        link = Chain(dve, name + "_step").link
                        if relu:
                            link(dve.scalar_tensor_tensor(X[:], update, 0.0, X[:], ALU.max, ALU.add))
                        else:
                            link(dve.tensor_tensor(X[:], X[:], update, ALU.add))
                        link(dve.tensor_reduce(mean[:], X[:], AX.X, ALU.add))
                        link(dve.tensor_scalar(mean[:], mean[:], 1.0 / D, None, ALU.mult))
                        link(dve.tensor_tensor(X[:], X[:], mean[:].unsqueeze(2).to_broadcast([P, NB, D]), ALU.subtract))
                        link(dve.tensor_tensor(sq[:], X[:], X[:], ALU.mult))
                        link(dve.tensor_reduce(var[:], sq[:], AX.X, ALU.add))
                        link(dve.tensor_scalar(var[:], var[:], 1.0 / D, EPS, ALU.mult, ALU.add))
                        dve.sem_inc(v_ready, 1)
                        dve.wait_ge(r_ready, 1)
                        link(dve.reciprocal(dev[:], dev[:]))
                        link(dve.tensor_tensor(X[:], X[:], dev[:].unsqueeze(2).to_broadcast([P, NB, D]), ALU.mult))
                        dve.sem_inc(o_ready, 1)

                    @block.scalar
                    def _(act):
                        act.wait_ge(v_ready, 1)
                        act.activation(dev[:], var[:], ACT.Sqrt).then_inc(r_ready, 1)

                    if last:
                        @block.sync
                        def _(sp):
                            sp.wait_ge(o_ready, 1)
                            full = NB - 1
                            sp.dma_start(out[0:full * P, :].rearrange("(b p) d -> p b d", p=P), X[:, 0:full, :])\
                                .then_inc(stored, 16)
                            sp.dma_start(out[full * P:N_NODES, :], X[0:N_NODES - full * P, full, :])\
                                .then_inc(stored, 16)
                            sp.wait_ge(stored, 32)

        with ExitStack() as st:
            acc = SB(st, "l0_acc", [P, NB * D])

            def scratch(s_):
                return {"w": SB(s_, "l0_w", [P, 3 * D]), "hr": SB(s_, "l0_hr", [P, NB, 3 * D]),
                        "ps": PS(s_, "l0_ps", [P, NBU, 512]), "mm": sem("l0_mm")}

            def load(sp, s, in_w):
                sp.dma_start(s["w"][:].rearrange("p (r o) -> p r o", r=3),
                             a["L0_w"].rearrange("r i o -> i r o")).then_inc(in_w, 16)
                s["in_w"] = in_w
                return 1

            def tensor(pe, s, i, xt):
                pe.wait_ge(s["in_w"], 16)
                for u in range(NBU):
                    pe.matmul(s["ps"][:, u, 0:3 * D], lhsT=xt[:, u, :], rhs=s["w"][:], start=True, stop=True)\
                        .then_inc(s["mm"], 1)

            def vector(dve, link, s, i):
                for u in range(NBU):
                    dve.wait_ge(s["mm"], i * NBU + (u + 1))
                    link(move(dve, s["hr"][:, bass.ds(i * NBU + u, 1), :],
                                         s["ps"][:, u:u + 1, 0:3 * D]))

            def store(sp, s, outs):
                for r in range(3):
                    sp.dma_start(t_hr[r * NP:(r + 1) * NP, :].rearrange("(b p) d -> p b d", p=P),
                                 s["hr"][:, :, r * D:(r + 1) * D]).then_inc(outs, 16)
                return 3
            node_stage("l0n", blocks_of(X), 1, tensor, vector, NBU, nothing, scratch, load, store)
            edge_sums("l0e", t_hr, D, hr_i, dloc, blk_i, ew[:].unsqueeze(2), 1, D, acc, 1)
            add_norm("l0x", acc[:].rearrange("p (b d) -> p b d", b=NB), True)
        with ExitStack() as st:
            q_all = SB(st, "l1_q", [P, NB * D])
            w_all = SB(st, "l1_w", [P, 3 * D])
            b_row = SB(st, "l1_b", [1, 3 * D])
            rel = SB(st, "l1_rel", [P, D])
            with ExitStack() as s2:
                wv = SB(s2, "l1_wv", [P, D])
                bd = SB(s2, "l1_bd", [P, D])
                bv = SB(s2, "l1_bv", [P, 1])
                ps = PS(s2, "l1_ps_w", [P, 512])
                in_w, z_ready, mm = sem("l1_weights"), sem("l1_zeroed"), sem("l1_folded")
                with phase() as block:
                    @block.sync
                    def _(sp):
                        sp.dma_start(w_all[:, 0:D], a["L1_Wk"]).then_inc(in_w, 16)
                        sp.dma_start(w_all[:, D:2 * D], a["L1_Wq"]).then_inc(in_w, 16)
                        sp.dma_start(wv[:], a["L1_Wv"]).then_inc(in_w, 16)
                        sp.dma_start(b_row[:, 0:D], a["L1_bk"].unsqueeze(0)).then_inc(in_w, 16)
                        sp.dma_start(b_row[:, D:2 * D], a["L1_bq"].unsqueeze(0)).then_inc(in_w, 16)
                        sp.dma_start(bv[:], a["L1_bv"].unsqueeze(1)).then_inc(in_w, 16)
                        sp.dma_start(rel[:], a["L1_rel"].unsqueeze(0).to_broadcast([P, D])).then_inc(in_w, 16)
                        sp.wait_ge(z_ready, 1)
                        for h in range(H1):
                            sp.dma_start(bd[h * DK:(h + 1) * DK, h * DK:(h + 1) * DK], a["L1_rel_msg"][h])\
                                .then_inc(in_w, 16)
                        sp.wait_ge(in_w, 16 * (7 + H1))

                    @block.tensor
                    def _(pe):
                        pe.wait_ge(in_w, 16 * (7 + H1))
                        pe.matmul(ps[:, 0:D], lhsT=wv[:], rhs=bd[:], start=True, stop=True)
                        pe.matmul(ps[0:1, D:2 * D], lhsT=bv[:], rhs=bd[:], start=True, stop=True).then_inc(mm, 1)

                    @block.vector
                    def _(dve):
                        link = Chain(dve, "l1_prep_step").link
                        link(dve.memset(bd[:], 0.0))
                        dve.sem_inc(z_ready, 1)
                        dve.wait_ge(mm, 1)
                        link(dve.tensor_copy(w_all[:, 2 * D:3 * D], ps[:, 0:D]))
                        link(dve.tensor_copy(b_row[:, 2 * D:3 * D], ps[0:1, D:2 * D]))

            def scratch(s_):
                return {"k": SB(s_, "l1_k", [P, NB, D + H1]), "v": SB(s_, "l1_v", [P, NB, D]),
                        "t": SB(s_, "l1_t", [P, D]), "r": SB(s_, "l1_r", [P, H1]), "ps": PS(s_, "l1_ps", [P, NBU, 512]), "mm": sem("l1_mm")}

            def tensor(pe, s, i, xt):
                for u in range(NBU):
                    pe.matmul(s["ps"][:, u, 0:3 * D], lhsT=xt[:, u, :], rhs=w_all[:], start=True, stop=False)
                    pe.matmul(s["ps"][:, u, 0:3 * D], lhsT=ones[0:1, :], rhs=b_row[:], start=False, stop=True)\
                        .then_inc(s["mm"], 1)

            def vector(dve, link, s, i):
                for u in range(NBU):
                    dve.wait_ge(s["mm"], i * NBU + (u + 1))
                    b = i * NBU + u
                    kb = s["k"][:, bass.ds(b, 1), 0:D].rearrange("p b d -> p (b d)")
                    link(move(dve, kb, s["ps"][:, u, 0:D]))
                    link(move(dve, q_all[:, bass.ds(b * D, D)], s["ps"][:, u, D:2 * D]))
                    link(move(dve, s["v"][:, bass.ds(b, 1), :].rearrange("p b d -> p (b d)"),
                                         s["ps"][:, u, 2 * D:3 * D]))
                    link(dve.tensor_tensor(s["t"][:], kb, rel[:], ALU.mult))
                    link(dve.tensor_reduce(s["r"][:], s["t"][:].rearrange("p (h d) -> p h d", h=H1), AX.X, ALU.add))
                    link(move(dve, s["k"][:, bass.ds(b, 1), D:D + H1].rearrange("p b h -> p (b h)"), s["r"][:]))

            def store(sp, s, outs):
                sp.dma_start(t_k.rearrange("(b p) d -> p b d", p=P), s["k"][:]).then_inc(outs, 16)
                sp.dma_start(t_v.rearrange("(b p) d -> p b d", p=P), s["v"][:]).then_inc(outs, 16)
                return 2
            node_stage("l1n", blocks_of(X), 1, tensor, vector, 6 * NBU, nothing, scratch, store=store)

            def combine(dve, link, t0, rows, ps_q, prod, red, tmp):
                link(dve.tensor_tensor(prod[:], rows[:, :, 0:D], ps_q, ALU.mult))
                link(dve.tensor_reduce(red[:], prod[:].rearrange("p g (h d) -> p g h d", h=H1), AX.X, ALU.add))
                link(dve.tensor_tensor(tmp[:], rows[:, :, D:D + H1],
                                       ew[:, bass.ds(t0, G)].unsqueeze(2).to_broadcast([P, G, H1]), ALU.mult))
                link(dve.tensor_tensor(red[:], red[:], tmp[:], ALU.add))
                link(dve.tensor_scalar(att[:, bass.ds(t0, G), :], red[:], float(DK) ** -0.5, None, ALU.mult))
            edge_scores("l1s", t_k, D + H1, q_all, D, combine)
        segment_exp("l1x")

        with ExitStack() as st:
            acc = SB(st, "l1_acc", [P, NB * (D + H1)])
            upd = SB(st, "l1_upd", [P, NB, D])
            den = SB(st, "l1_den", [P, NB, H1])

            def rows(dve, link, n, b, t0, got, made, m):
                e = att[:, bass.ds(t0, G), :]
                link(dve.tensor_tensor(made[:, :, 0:D].rearrange("p g (h d) -> p g h d", h=H1),
                                       got.rearrange("p g (h d) -> p g h d", h=H1),
                                       e.unsqueeze(3).to_broadcast([P, G, H1, DK]), ALU.mult))
                link(move(dve, made[:, :, D:D + H1], e))
            edge_sums("l1e", t_v, D, src_i, dloc, blk_i, None, 1, D + H1, acc, 1, rows)
            av = acc[:].rearrange("p (b d) -> p b d", b=NB)
            with phase() as block:
                @block.vector
                def _(dve):
                    link = Chain(dve, "l1_div_step").link
                    link(dve.tensor_scalar(den[:], av[:, :, D:D + H1], 1e-30, None, ALU.max))
                    link(dve.reciprocal(den[:], den[:]))
                    link(dve.tensor_tensor(upd[:].rearrange("p b (h d) -> p b h d", h=H1),
                                           av[:, :, 0:D].rearrange("p b (h d) -> p b h d", h=H1),
                                           den[:].unsqueeze(3).to_broadcast([P, NB, H1, DK]), ALU.mult))
            add_norm("l1x2", upd[:], True)

        def softplus_scalar(act, link, s, n, b, y):
            act.wait_ge(s["hid"], n + 1)
            wait(act, s["soft"], n + (1 - s["bufs"]))
            link(act.activation(s["y"][:, b, :], y, ACT.Identity, bias=s["bias"][:, 0:1]))
            act.sem_inc(s["y_ready"], 1)
            link(act.activation(s["l"][:, b, :], s["y"][:, b, :], ACT.Abs))
            link(act.activation(s["l"][:, b, :], s["l"][:, b, :], ACT.Exp, scale=-1.0))
            link(act.activation(s["l"][:, b, :], s["l"][:, b, :], ACT.Ln, bias=1.0))
            act.sem_inc(s["l_ready"], 1)

        def softplus_vector(dve, link, s, n, b):
            dve.wait_ge(s["y_ready"], n + 1)
            wait(dve, s["sp_used"], n + (1 - s["bufs"]))
            link(dve.tensor_scalar(s["sp"][:, b, :], s["y"][:, b, :], 0.0, None, ALU.max))
            dve.wait_ge(s["l_ready"], n + 1)
            link(dve.tensor_tensor(s["sp"][:, b, :], s["sp"][:, b, :], s["l"][:, b, :], ALU.add))
            dve.sem_inc(s["soft"], 1)

        def softplus_scratch(s_, name, width, bias, bufs):
            s = {"bias": bias, "bufs": bufs}
            for k in ("y", "l", "sp"):
                s[k] = SB(s_, f"{name}_{k}", [P, bufs, width])
            for k in ("hid", "y_ready", "l_ready", "soft", "sp_used"):
                s[k] = sem(f"{name}_{k}")
            return s

        with ExitStack() as st:
            w_in = SB(st, "l2_w_in", [P, D])
            wf1 = SB(st, "l2_wf1", [32, D])
            wf2 = SB(st, "l2_wf2", [P, D])
            wo1 = SB(st, "l2_wo1", [P, D])
            wo2 = SB(st, "l2_wo2", [P, D])
            bf1 = SB(st, "l2_bf1", [P, 1])
            bo1 = SB(st, "l2_bo1", [P, 1])
            rows2 = SB(st, "l2_rows", [1, 2, D])
            nlog2 = SB(st, "l2_nlog2", [P, 1])
            bias3 = SB(st, "l2_bias3", [3, 2, D], BF16)
            parts = SB(st, "l2_parts", [1, 3, 2, D], BF16)
            part_f = SB(st, "l2_part_f", [1, 2, D])
            acc = SB(st, "l2_acc", [P, NB * D])
            with ExitStack() as s2:
                ps = PS(s2, "l2_ps_b", [P, 512])
                in_w, set_, mm, split = (sem("l2_" + k) for k in ("weights", "set", "sums", "split"))
                with phase() as block:
                    @block.sync
                    def _(sp):
                        for d, k in ((w_in, "W_in"), (wf1, "Wf1"), (wf2, "Wf2"), (wo1, "Wo1"), (wo2, "Wo2")):
                            sp.dma_start(d[:], a["L2_" + k]).then_inc(in_w, 16)
                        sp.dma_start(bf1[:], a["L2_bf1"].unsqueeze(1)).then_inc(in_w, 16)
                        sp.dma_start(bo1[:], a["L2_bo1"].unsqueeze(1)).then_inc(in_w, 16)
                        sp.dma_start(rows2[:, 0, :], a["L2_bf2"].unsqueeze(0)).then_inc(in_w, 16)
                        sp.dma_start(rows2[:, 1, :], a["L2_bo2"].unsqueeze(0)).then_inc(in_w, 16)
                        sp.wait_ge(in_w, 16 * 9)
                        sp.wait_ge(split, 1)
                        for k in range(3):
                            sp.dma_start(bias3[k:k + 1, :, :], parts[:, k, :, :]).then_inc(in_w, 16)
                        sp.wait_ge(in_w, 16 * 12)

                    @block.tensor
                    def _(pe):
                        pe.wait_ge(set_, 1)
                        pe.wait_ge(in_w, 16 * 9)
                        pe.matmul(ps[0:1, 0:D], lhsT=nlog2[:], rhs=wf2[:], start=True, stop=True)
                        pe.matmul(ps[0:1, D:2 * D], lhsT=nlog2[:], rhs=wo2[:], start=True, stop=True).then_inc(mm, 1)

                    @block.vector
                    def _(dve):
                        link = Chain(dve, "l2_prep_step").link
                        link(dve.memset(nlog2[:], -LOG2))
                        dve.sem_inc(set_, 1)
                        dve.wait_ge(mm, 1)
                        link(dve.tensor_tensor(rows2[:], rows2[:], ps[0:1, 0:2 * D].rearrange("o (k d) -> o k d", k=2),
                                               ALU.add))
                        split3(dve, link, rows2[:], part_f[:], [parts[:, k, :, :] for k in range(3)])
                        dve.sem_inc(split, 1)

            def scratch(s_):
                return {"h": SB(s_, "l2_h", [P, NB, D]), "ps": PS(s_, "l2_ps", [P, NBU, 512]), "mm": sem("l2_mm")}

            def tensor(pe, s, i, xt):
                for u in range(NBU):
                    pe.matmul(s["ps"][:, u, 0:D], lhsT=xt[:, u, :], rhs=w_in[:], start=True, stop=True)\
                        .then_inc(s["mm"], 1)

            def vector(dve, link, s, i):
                for u in range(NBU):
                    dve.wait_ge(s["mm"], i * NBU + (u + 1))
                    link(move(dve, s["h"][:, bass.ds(i * NBU + u, 1), :], s["ps"][:, u:u + 1, 0:D]))

            def store(sp, s, outs):
                sp.dma_start(t_h.rearrange("(b p) d -> p b d", p=P), s["h"][:]).then_inc(outs, 16)
                return 1
            node_stage("l2n", blocks_of(X), 1, tensor, vector, NBU, nothing, scratch, store=store)

            def filters(s_):
                m = softplus_scratch(s_, "l2f", G * P, bf1, 2)
                rec = SB(s_, "l2f_rec", [P, 4, G, FR])
                ft = SB(s_, "l2f_ft", [32, 2, G * P])
                ps_f = PS(s_, "l2f_ps_f", [32, 2, G * P])
                ps_h = PS(s_, "l2f_ps_h", [P, 2, G * P])
                ps_w = PS(s_, "l2f_ps_w", [P, 2, G, P])
                turned, copied, w_used = (sem("l2f_" + k) for k in ("turned", "copied", "w_used"))
                loaded_f = [sem(f"l2f_loaded{q}") for q in range(4)]
                view = rec_s.rearrange("(p t) f -> p (t f)", p=P)

                def sync(sp):
                    def body(i):
                        for q in range(4):
                            wait(sp, turned, i * 4 + (q - 3))
                            sp.dma_start(rec[:, q, :, :].rearrange("p g f -> p (g f)"),
                                         view[:, bass.ds((i * 16 + q * G) * FR, G * FR)]).then_inc(loaded_f[q], 16)
                    rolled(sp, body)
                    for q in range(4):
                        sp.wait_ge(loaded_f[q], 16 * STEPS)

                def turn(pe, i, q):
                    n, r, b = i * 4 + q, q % 4, q % 2
                    pe.wait_ge(loaded_f[r], (i + (q // 4 + 1)) * 16)
                    wait(pe, copied, n - 1)
                    for u in range(G):
                        ins = pe.transpose(ps_f[:, b, u * P:(u + 1) * P], rec[:, r, u, 0:32], ident[:])
                    ins.then_inc(turned, 1)

                def front(pe, i, q):
                    n, b = i * 4 + q, q % 2
                    pe.wait_ge(copied, n + 1)
                    wait(pe, m["y_ready"], n - 1)
                    pe.matmul(ps_h[:, b, :], lhsT=wf1[:], rhs=ft[:, b, :], start=True, stop=True)\
                        .then_inc(m["hid"], 1)

                def back(pe, i, q):
                    n, b = i * 4 + q, q % 2
                    pe.wait_ge(m["soft"], n + 1)
                    wait(pe, w_used, n - 1)
                    for u in range(G):
                        pe.matmul(ps_w[:, b, u, :], lhsT=ones_bf[0:3, :], rhs=bias3[:, 0, :],
                                  start=True, stop=False)
                        ins = pe.matmul(ps_w[:, b, u, :], lhsT=m["sp"][:, b, u * P:(u + 1) * P], rhs=wf2[:],
                                        start=False, stop=True)
                    ins.then_inc(m["sp_used"], 1)

                def scalar(act):
                    c = Chain(act, "l2f_act_step")

                    def features(i, q):
                        act.wait_ge(turned, i * 4 + (q + 1))
                        wait(act, m["hid"], i * 4 + (q - 1))
                        act.copy(ft[:, q % 2, :], ps_f[:, q % 2, :]).then_inc(copied, 1)

                    def body(i):
                        for q in range(4):
                            if exists(i, q + 3):
                                features(i, q + 3)
                            if exists(i, q + 2):
                                softplus_scalar(act, c.link, m, i * 4 + (q + 2), q % 2, ps_h[:, q % 2, :])
                    for q in range(3):
                        features(0, q)
                        if q < 2:
                            softplus_scalar(act, c.link, m, q, q, ps_h[:, q, :])
                    c.mark = c.n
                    rolled(act, body, c)
                m.update(sync=sync, turn=turn, front=front, back=back, scalar=scalar, ps_w=ps_w, w_used=w_used)
                return m

            def rows(dve, link, n, b, t0, got, made, m):
                dve.wait_ge(m["sp_used"], n + 1)
                link(dve.tensor_tensor(made, got, m["ps_w"][:, b, :, :], ALU.mult))
                dve.sem_inc(m["w_used"], 1)
            edge_sums("l2e", t_h, D, dst2_i, rs4[:, :, 2], sblk_i, rs4[:, :, 0:1], 1, D, acc, 1, rows, filters)

            upd = SB(st, "l2_upd", [P, NB, D])

            def scratch(s_):
                s = softplus_scratch(s_, "l2o", W5, bo1, 1)
                s["ps_h"] = PS(s_, "l2o_ps_h", [P, 2, 512])
                s["ps_o"] = PS(s_, "l2o_ps_o", [P, NBU, P])
                return s

            def tensor(pe, s, i, xt):
                pe.matmul(s["ps_h"][:, 0, 0:512], lhsT=wo1[:], rhs=xt[:].rearrange("p a d -> p (a d)")[:, 0:512],
                          start=True, stop=True)
                pe.matmul(s["ps_h"][:, 1, 0:W5 - 512], lhsT=wo1[:], rhs=xt[:].rearrange("p a d -> p (a d)")[:, 512:W5],
                          start=True, stop=True).then_inc(s["hid"], 1)
                pe.wait_ge(s["soft"], i + 1)
                for u in range(NBU):
                    pe.matmul(s["ps_o"][:, u, :], lhsT=s["sp"][:, 0, u * P:(u + 1) * P], rhs=wo2[:],
                              start=True, stop=False)
                    ins = pe.matmul(s["ps_o"][:, u, :], lhsT=ones[0:1, :], rhs=rows2[:, 1, :], start=False, stop=True)
                ins.then_inc(s["sp_used"], 1)

            def scalar(act, link, s, i):
                softplus_scalar(act, link, s, i, 0, s["ps_h"][:].rearrange("p a d -> p (a d)")[:, 0:W5])

            def vector(dve, link, s, i):
                softplus_vector(dve, link, s, i, 0)
                dve.wait_ge(s["sp_used"], i + 1)
                link(move(dve, upd[:, bass.ds(i * NBU, NBU), :], s["ps_o"][:]))
            node_stage("l2o", blocks_of(acc), 1, tensor, vector, 3, scalar, scratch, n_scalar=4)
            add_norm("l2x", upd[:], False)

        def leaky(dve, link, dst, src, tmp):
            link(dve.tensor_scalar(tmp, src, 0.01, None, ALU.mult))
            link(dve.tensor_tensor(dst, tmp, src, ALU.max))

        def gat_scores(name, heads, table, a_dst, ew_, mw_):
            def combine(dve, link, t0, rows, ps_q, prod, red, tmp):
                link(dve.tensor_tensor(att[:, bass.ds(t0, G), 0:heads], rows[:, :, 0:heads], ps_q[:, :, 0:heads], ALU.add))
            edge_scores(name, table, H3, a_dst, heads, combine)
            with ExitStack() as s2:
                t = SB(s2, name + "_t", [P, T, heads])
                with phase() as block:
                    @block.vector
                    def _(dve):
                        link = Chain(dve, name + "_lin_step").link
                        v = att[:, :, 0:heads]
                        link(dve.tensor_tensor(t[:], v, ew1[:].unsqueeze(2).to_broadcast([P, T, heads]), ALU.mult))
                        link(dve.tensor_tensor(t[:], t[:], ew_.unsqueeze(1).to_broadcast([P, T, heads]), ALU.mult))
                        link(dve.scalar_tensor_tensor(t[:], t[:], 0.01, t[:], ALU.mult, ALU.max))
                        link(dve.memset(att[:], 0.0))
                        link(dve.tensor_tensor(v, t[:], mw_.unsqueeze(1).to_broadcast([P, T, heads]), ALU.mult))
            segment_exp(name + "x")

        with ExitStack() as st:
            acc = SB(st, "l3_acc", [P, NB * H3 * ZW])
            acc4 = acc[:].rearrange("p (b h d) -> p b h d", b=NB, h=H3)
            a_dst = SB(st, "l3_a_dst", [P, NB * H3])
            ao_dst = SB(st, "l3_ao_dst", [P, NB])
            coef = SB(st, "l3_coef", [P, 10])
            with ExitStack() as s2:
                fc = SB(s2, "l3_fc", [P, H3 * D])
                at = SB(s2, "l3_at", [P, 2, H3 * D])
                in_w = sem("l3_weights")
                with phase() as block:
                    @block.sync
                    def _(sp):
                        sp.dma_start(fc[:], a["L3_fc"]).then_inc(in_w, 16)
                        sp.dma_start(at[:].rearrange("p k d -> p (k d)"),
                                     a["L3_at"].unsqueeze(0).to_broadcast([P, 2 * H3 * D])).then_inc(in_w, 16)
                        for k, (n, o) in {"ew": (4, 0), "mw": (4, 4), "oew": (1, 8), "omw": (1, 9)}.items():
                            sp.dma_start(coef[:, o:o + n], a["L3_" + k].unsqueeze(0).to_broadcast([P, n]))\
                                .then_inc(in_w, 16)
                        sp.wait_ge(in_w, 16 * 6)

                    @block.vector
                    def _(dve):
                        link = Chain(dve, "l3_prep_step").link
                        link(dve.memset(acc[:], 1.0))

                def scratch(s_):
                    return {"ps": PS(s_, "l3_ps", [P, NBU, 512]), "mm": sem("l3_mm"),
                            "t": SB(s_, "l3_t", [P, H3, D]), "r": SB(s_, "l3_r", [P, H3]), "as": SB(s_, "l3_as", [P, NB, H3])}

                def tensor(pe, s, i, xt):
                    for u in range(NBU):
                        pe.matmul(s["ps"][:, u, :], lhsT=xt[:, u, :], rhs=fc[:], start=True, stop=True)\
                            .then_inc(s["mm"], 1)

                def vector(dve, link, s, i):
                    for u in range(NBU):
                        b = i * NBU + u
                        dve.wait_ge(s["mm"], i * NBU + (u + 1))
                        z = acc4[:, bass.ds(b, 1), :, 0:D].rearrange("p b h d -> p (b h) d")
                        leaky(dve, link, z, s["ps"][:, u, :].rearrange("p (h d) -> p h d", h=H3), s["t"][:])
                        for k, o in ((0, s["as"][:, bass.ds(b, 1), :].rearrange("p b h -> p (b h)")),
                                     (1, a_dst[:, bass.ds(b * H3, H3)])):
                            link(dve.tensor_tensor(s["t"][:], z, at[:, k, :].rearrange("p (h d) -> p h d", h=H3),
                                                   ALU.mult))
                            link(dve.tensor_reduce(s["r"][:], s["t"][:], AX.X, ALU.add))
                            link(move(dve, o, s["r"][:]))

                def store(sp, s, outs):
                    sp.dma_start(t_z.rearrange("(b p) d -> p b d", p=P),
                                 acc[:].rearrange("p (b d) -> p b d", b=NB)).then_inc(outs, 16)
                    sp.dma_start(t_as.rearrange("(b p) d -> p b d", p=P), s["as"][:]).then_inc(outs, 16)
                    return 2
                node_stage("l3n", blocks_of(X), 1, tensor, vector, 8 * NBU, nothing, scratch, store=store)
            gat_scores("l3s", H3, t_as, a_dst, coef[:, 0:4], coef[:, 4:8])
            edge_sums("l3e", t_z, H3 * ZW, src_i, dloc, blk_i, att, H3, ZW, acc, 2)

            def divide(name, view, heads):
                with ExitStack() as s2:
                    den = SB(s2, name + "_den", [P, NB, heads])
                    with phase() as block:
                        @block.vector
                        def _(dve):
                            link = Chain(dve, name + "_step").link
                            link(dve.tensor_scalar(den[:].unsqueeze(3), view[:, :, :, D:ZW], 1e-30, None, ALU.max))
                            link(dve.reciprocal(den[:], den[:]))
                            for h in range(heads):
                                z = view[:, :, h, 0:D]
                                link(dve.tensor_tensor(z, z, den[:, :, h:h + 1].to_broadcast([P, NB, D]), ALU.mult))
                                link(dve.scalar_tensor_tensor(z, z, 0.01, z, ALU.mult, ALU.max))
            divide("l3d", acc4, H3)

            zo = SB(st, "l3_zo", [P, NB, ZW])
            with ExitStack() as s2:
                ofc = SB(s2, "l3_ofc", [P, H3, D])
                oat = SB(s2, "l3_oat", [P, 2, D])
                aos = SB(s2, "l3_aos", [P, NB, H3])
                in_w = sem("l3_out_weights")
                with phase() as block:
                    @block.sync
                    def _(sp):
                        sp.dma_start(ofc[:], a["L3_ofc"]).then_inc(in_w, 16)
                        sp.dma_start(oat[:].rearrange("p k d -> p (k d)"),
                                     a["L3_oat"].unsqueeze(0).to_broadcast([P, 2 * D])).then_inc(in_w, 16)
                        sp.wait_ge(in_w, 32)

                    @block.vector
                    def _(dve):
                        link = Chain(dve, "l3_oprep_step").link
                        link(dve.memset(zo[:], 1.0))
                        link(dve.memset(aos[:], 0.0))

                def scratch(s_):
                    return {"ps": PS(s_, "l3o_ps", [P, NBU, 512]), "mm": sem("l3o_mm"),
                            "t": SB(s_, "l3o_t", [P, D]), "r": SB(s_, "l3o_r", [P, 1])}

                def fill(pool, link, stage, i):
                    for h in range(H3):
                        link(pool.tensor_copy(stage[:].rearrange("p (b h) d -> p b h d", h=H3)[:, :, h, :],
                                              acc4[:, bass.ds(i * NBU, NBU), h, 0:D]))

                def tensor(pe, s, i, xt):
                    for u in range(NBU):
                        for k in range(H3):
                            ins = pe.matmul(s["ps"][:, u, 0:D], lhsT=xt[:, u * H3 + k, :], rhs=ofc[:, k, :],
                                            start=k == 0, stop=k == H3 - 1)
                        ins.then_inc(s["mm"], 1)

                def vector(dve, link, s, i):
                    for u in range(NBU):
                        b = i * NBU + u
                        dve.wait_ge(s["mm"], i * NBU + (u + 1))
                        z = zo[:, bass.ds(b, 1), 0:D].rearrange("p b d -> p (b d)")
                        leaky(dve, link, z, s["ps"][:, u, 0:D], s["t"][:])
                        for k, o in ((0, aos[:, bass.ds(b, 1), 0:1].rearrange("p b o -> p (b o)")), (1, ao_dst[:, bass.ds(b, 1)])):
                            link(dve.tensor_tensor(s["t"][:], z, oat[:, k, :], ALU.mult))
                            link(dve.tensor_reduce(s["r"][:], s["t"][:], AX.X, ALU.add))
                            link(move(dve, o, s["r"][:]))

                def store(sp, s, outs):
                    sp.dma_start(t_zo.rearrange("(b p) d -> p b d", p=P), zo[:]).then_inc(outs, 16)
                    sp.dma_start(t_ao.rearrange("(b p) d -> p b d", p=P), aos[:]).then_inc(outs, 16)
                    return 2
                node_stage("l3o", (fill, H3), H3, tensor, vector, 8 * NBU, nothing, scratch, store=store)
            gat_scores("l3t", 1, t_ao, ao_dst, coef[:, 8:9], coef[:, 9:10])
            oacc = zo[:].rearrange("p b d -> p (b d)")
            edge_sums("l3f", t_zo, ZW, src_i, dloc, blk_i, att, 1, ZW, oacc, 1)
            divide("l3g", zo[:].unsqueeze(2), 1)

            upd = acc[:, 0:NB * D].rearrange("p (b d) -> p b d", b=NB)
            with ExitStack() as s2:
                wih = SB(s2, "gru_wih", [P, 3 * D])
                whh = SB(s2, "gru_whh", [P, 3 * D])
                gb = SB(s2, "gru_b", [1, 2, 3 * D])
                in_w = sem("gru_in")
                with phase() as block:
                    @block.sync
                    def _(sp):
                        sp.dma_start(wih[:], a["L3_wih"]).then_inc(in_w, 16)
                        sp.dma_start(whh[:], a["L3_whh"]).then_inc(in_w, 16)
                        sp.dma_start(gb[:, 0, :], a["L3_bih"].unsqueeze(0)).then_inc(in_w, 16)
                        sp.dma_start(gb[:, 1, :], a["L3_bhh"].unsqueeze(0)).then_inc(in_w, 16)
                        sp.wait_ge(in_w, 64)

                def scratch(s_):
                    s = {"ps": PS(s_, "gru_ps", [P, NBU, 512]), "rz": SB(s_, "gru_rz", [P, NBU, 2 * D]),
                         "n": SB(s_, "gru_n", [P, NBU, D]), "d": SB(s_, "gru_d", [P, NBU, D])}
                    for k in ("mm", "gates", "pre", "new"):
                        s[k] = sem("gru_" + k)
                    return s

                def fill(pool, link, stage, i):
                    link(pool.tensor_copy(stage[:, 0:NBU, :], zo[:, bass.ds(i * NBU, NBU), 0:D]))
                    link(pool.tensor_copy(stage[:, NBU:2 * NBU, :], X[:, bass.ds(i * NBU, NBU), :]))

                def tensor(pe, s, i, xt):
                    for u in range(NBU):
                        o = s["ps"][:, u, :]
                        pe.matmul(o[:, 0:256], lhsT=xt[:, u, :], rhs=wih[:, 0:256], start=True, stop=False)
                        pe.matmul(o[:, 0:256], lhsT=xt[:, NBU + u, :], rhs=whh[:, 0:256], start=False, stop=False)
                        pe.matmul(o[:, 0:256], lhsT=ones[0:1, :], rhs=gb[:, 0, 0:256], start=False, stop=False)
                        pe.matmul(o[:, 0:256], lhsT=ones[0:1, :], rhs=gb[:, 1, 0:256], start=False, stop=True)
                        for k, (w, x0) in enumerate(((wih, 0), (whh, NBU))):
                            v = o[:, 256 + k * D:256 + (k + 1) * D]
                            pe.matmul(v, lhsT=xt[:, x0 + u, :], rhs=w[:, 256:384], start=True, stop=False)
                            ins = pe.matmul(v, lhsT=ones[0:1, :], rhs=gb[:, k, 256:384], start=False, stop=True)
                    ins.then_inc(s["mm"], 1)

                def scalar(act, link, s, i):
                    act.wait_ge(s["mm"], i + 1)
                    link(act.activation(s["rz"][:], s["ps"][:, :, 0:256], ACT.Sigmoid))
                    act.sem_inc(s["gates"], 1)
                    act.wait_ge(s["pre"], i + 1)
                    link(act.activation(s["n"][:], s["d"][:], ACT.Tanh))
                    act.sem_inc(s["new"], 1)

                def vector(dve, link, s, i):
                    dve.wait_ge(s["gates"], i + 1)
                    link(dve.tensor_tensor(s["d"][:], s["rz"][:, :, 0:D], s["ps"][:, :, 384:512], ALU.mult))
                    link(dve.tensor_tensor(s["d"][:], s["d"][:], s["ps"][:, :, 256:384], ALU.add))
                    dve.sem_inc(s["pre"], 1)
                    dve.wait_ge(s["new"], i + 1)
                    x = X[:, bass.ds(i * NBU, NBU), :]
                    link(dve.tensor_tensor(s["d"][:], x, s["n"][:], ALU.subtract))
                    link(dve.tensor_tensor(s["d"][:], s["d"][:], s["rz"][:, :, D:2 * D], ALU.mult))
                    link(dve.tensor_tensor(s["d"][:], s["d"][:], s["n"][:], ALU.add))
                    link(dve.scalar_tensor_tensor(upd[:, bass.ds(i * NBU, NBU), :], s["d"][:], 0.01, s["d"][:],
                                                  ALU.mult, ALU.max))
                node_stage("gru", (fill, 2), 2, tensor, vector, 6, scalar, scratch, n_scalar=2)
            add_norm("l3y", upd, False, last=True)



def kernel(**inputs):
    import numpy as np
    import concourse.bacc as _bacc
    from concourse import mybir as _mybir
    from concourse.bass_utils import run_bass_kernel_spmd as _run

    i = {k: np.asarray(v) for k, v in inputs.items()}
    pad = TR * P - N_EDGES

    def tiled(v, fill):
        v = np.pad(v, [(0, pad)] + [(0, 0)] * (v.ndim - 1), constant_values=fill)
        return np.ascontiguousarray(np.swapaxes(v.reshape((TR, P) + v.shape[1:]), 0, 1))

    line = np.pad(i["dst"], (0, pad + 1), constant_values=NP)
    arrays = {
        "x": np.pad(i["x"], [(0, NP - N_NODES), (0, 0)]),
        "src": tiled(i["src"], -1), "dst": tiled(i["dst"], -1), "typ": tiled(i["edge_type_3"], 0),
        "w": tiled(i["edge_weight"], 0), "w1": tiled(i["edge_weight1"][:, 0], 0),
        "f": tiled(i["edge_attr3_1x32"][:, 0, :], 0),
        "dst_line": np.ascontiguousarray(np.stack([line[p * TR:(p + 1) * TR + 1] for p in range(P)])),
        "L0_w": i["L0_gnn_weight"],
    }
    for k in ("Wk", "Wq"):
        arrays["L1_" + k] = np.ascontiguousarray(i["L1_gnn_" + k].T)
    for k in ("Wv", "bk", "bq", "bv", "rel_msg"):
        arrays["L1_" + k] = i["L1_gnn_" + k]
    arrays["L1_rel"] = i["L1_gnn_rel_att"].reshape(D)
    for k in ("W_in", "Wf1", "bf1", "Wf2", "bf2", "Wo1", "bo1", "Wo2", "bo2"):
        arrays["L2_" + k] = i["L2_gnn_" + k]
    arrays["L3_fc"] = np.ascontiguousarray(i["L3_gnn_fc_W"].transpose(2, 0, 1).reshape(D, H3 * D))
    arrays["L3_at"] = np.ascontiguousarray(i["L3_gnn_attn_W"].reshape(H3, 2, D).transpose(1, 0, 2).reshape(2 * H3 * D))
    arrays["L3_ew"] = i["L3_gnn_edge_w"].reshape(H3)
    arrays["L3_mw"] = i["L3_gnn_m_w"].reshape(H3)
    arrays["L3_ofc"] = np.ascontiguousarray(i["L3_gnn_out_fc_W"].T.reshape(H3, D, D).transpose(1, 0, 2))
    arrays["L3_oat"] = i["L3_gnn_out_attn_W"].reshape(2 * D)
    arrays["L3_oew"] = i["L3_gnn_out_edge_w"].reshape(1)
    arrays["L3_omw"] = i["L3_gnn_out_m_w"].reshape(1)
    arrays["L3_wih"] = np.ascontiguousarray(i["L3_gnn_gru_Wih"].T)
    arrays["L3_whh"] = np.ascontiguousarray(i["L3_gnn_gru_Whh"].T)
    arrays["L3_bih"] = i["L3_gnn_gru_bih"]
    arrays["L3_bhh"] = i["L3_gnn_gru_bhh"]

    nc = _bacc.Bacc("TRN2", target_bir_lowering=False, num_devices=1)
    aps, feeds = {}, {}
    for k, v in arrays.items():
        feeds["in_" + k] = np.ascontiguousarray(v)
        aps[k] = nc.dram_tensor("in_" + k, v.shape, _mybir.dt.from_np(v.dtype), kind="ExternalInput").ap()
    out = nc.dram_tensor("out_0", (N_NODES, D), _mybir.dt.float32, kind="ExternalOutput").ap()
    gnn_program(nc, aps, out)
    return _run(nc, [feeds], core_ids=[0]).results[0]["out_0"]
```

```python
import concourse.bass as bass
from concourse import mybir
from contextlib import ExitStack, contextmanager

F32 = mybir.dt.float32
BF16 = mybir.dt.bfloat16
I32 = mybir.dt.int32
ALU = mybir.AluOpType
ACT = mybir.ActivationFunctionType
AX = mybir.AxisListType

P = 128
N_NODES, N_EDGES, D = 3125, 50000, 128
NB = -(-N_NODES // P)
NP = NB * P
TR = -(-N_EDGES // P)
LAST = N_EDGES - (TR - 1) * P
T = TR + NB
G = 4
STEPS = T // (4 * G)
H1, DK = 8, 16
H3 = 4
ZW = D + 1
CH = 16
CT = T // CH
SC = CT * P
FR = 36
BIG = 1.0e30
LOG2 = 0.6931471805599453
EPS = 1e-5
NBU, NBI = 5, 5
assert STEPS * 4 * G == T and NBU * NBI == NB and CH * CT == T and NP == NB * P


def gnn_program(nc, a, out):
    top = ExitStack()

    def dram(name, shape):
        return nc.dram_tensor(name, shape, F32, kind="Internal").ap()

    rec_lin = dram("rec_lin", (TR * P + P, 8))
    rec_s = dram("rec_s", (P * T, FR))
    rec_tmp = dram("rec_tmp", (P * TR, 8))
    t_hr = dram("t_hr", (3 * NP, D))
    t_k = dram("t_k", (NP, D + H1))
    t_v = dram("t_v", (NP, D))
    t_h = dram("t_h", (NP, D))
    t_z = dram("t_z", (NP, H3 * ZW))
    t_as = dram("t_as", (NP, H3))
    t_zo = dram("t_zo", (NP, ZW))
    t_ao = dram("t_ao", (NP, H3))

    with top:
        def SB(stack, name, shape, dt=F32):
            return stack.enter_context(nc.sbuf_tensor(name, shape, dt))

        def PS(stack, name, shape, dt=F32):
            return stack.enter_context(nc.psum_tensor(name, shape, dt))

        phase_sems = []

        def sem(name):
            phase_sems.append(nc.alloc_semaphore(name))
            return phase_sems[-1]

        def end_phase():
            nc.clear_and_free_semaphores(list(phase_sems))
            phase_sems.clear()
            nc.all_engine_barrier()

        @contextmanager
        def phase():
            with nc.Block() as block:
                yield block
            end_phase()

        def move(dve, out_, in_):
            return dve.tensor_scalar(out_, in_, 1.0, None, ALU.mult)

        def split3(dve, link, x, rest, parts):
            link(dve.tensor_copy(parts[0], x))
            link(dve.tensor_tensor(rest, x, parts[0], ALU.subtract))
            link(dve.tensor_copy(parts[1], rest))
            link(dve.tensor_tensor(rest, rest, parts[1], ALU.subtract))
            link(dve.tensor_copy(parts[2], rest))

        class Chain:

            def __init__(self, eng, name):
                self.eng, self.done, self.n, self.base, self.mark = eng, sem(name), 0, 0, 0

            def start(self, ins):
                self.n += 1
                ins.then_inc(self.done, 1)

            def finish(self):
                self.eng.wait_ge(self.done, self.base + self.n)

            def link(self, ins):
                self.start(ins)
                self.finish()

            @contextmanager
            def loop(self, lo, hi, per):
                before, self.n = self.n, 0
                with self.eng.Fori(lo, hi) as i:
                    self.base = (i - lo) * per + before
                    yield i
                    assert self.n == per, self.n
                self.base, self.n = 0, before + (hi - lo) * per

        def sb(name, shape, dt=F32):
            return SB(top, name, shape, dt)

        X = sb("X", [P, NB, D])
        iota_f = sb("iota_f", [P, P])
        iota_i = sb("iota_i", [P, P], I32)
        pid_i = sb("pid_i", [P, 1], I32)
        pid = sb("pid", [P, 3])
        ident = sb("ident", [P, P])
        below = sb("below", [P, P])
        above = sb("above", [P, P])
        tri_m1 = sb("tri_m1", [P, P], BF16)
        ones_bf = sb("ones_bf", [P, P], BF16)
        ones = sb("ones", [P, P])
        ident_bf = sb("ident_bf", [P, P], BF16)
        src_i = sb("src_i", [P, T], I32)
        hr_i = sb("hr_i", [P, T], I32)
        blk_i = sb("blk_i", [P, T], I32)
        dloc = sb("dloc", [P, T])
        ew = sb("ew", [P, T])
        ew1 = sb("ew1", [P, T])
        rs4 = sb("rs4", [P, T, 4])
        dst2_i = sb("dst2_i", [P, T], I32)
        sblk_i = sb("sblk_i", [P, T], I32)
        unsorted_i = sb("unsorted_i", [P, 1], I32)
        reset = sb("reset", [P, SC + 1])
        att = sb("att", [P, T, 8])

        def rank_vector(dve, c, s, key, place, align):
            link = c.link
            link(dve.memset(s["zero"][:], 0.0))
            link(dve.memset(s["base"][:], 0.0))
            link(dve.memset(place[:], 0.0))

            def bucket(b):
                link(dve.tensor_scalar(s["hit"][:], key[:], iota_f[:, bass.ds(b, 1)], None, ALU.is_equal))
                dve.sem_inc(s["hit_ready"], 1)
            bucket(0)
            with c.loop(0, NB, 8 if align else 6) as b:
                dve.wait_ge(s["counted"], b + 1)
                link(dve.tensor_tensor_scan(s["run"][:], s["ps_tot"][:, 0:TR], s["zero"][:], s["base"][:, 0:1],
                                       ALU.add, ALU.add))
                link(dve.tensor_tensor(s["spot"][:], s["run"][:], s["ps_pre"][:, 0:TR], ALU.add))
                link(dve.tensor_tensor(s["spot"][:], s["spot"][:], s["hit"][:], ALU.mult))
                bucket(b + 1)
                link(dve.tensor_tensor(place[:], place[:], s["spot"][:], ALU.add))
                if align:
                    link(dve.tensor_scalar(s["base_i"][:], s["run"][:, TR - 1:TR], float(P - 1), None, ALU.add))
                    link(dve.tensor_scalar(s["base_i"][:], s["base_i"][:], -P, None, ALU.bitwise_and))
                    link(dve.tensor_copy(s["base"][:], s["base_i"][:]))
                else:
                    link(dve.tensor_copy(s["base"][:], s["run"][:, TR - 1:TR]))

        def rank_tensor(pe, s):
            with pe.Fori(0, NB) as b:
                pe.wait_ge(s["hit_ready"], b + 1)
                pe.matmul(s["ps_pre"][:, 0:TR], lhsT=tri_m1[:], rhs=s["hit"][:], start=True, stop=True)
                pe.matmul(s["ps_tot"][:, 0:TR], lhsT=ones_bf[:], rhs=s["hit"][:],
                          start=True, stop=True).then_inc(s["counted"], 1)

        def place_to_row(dve, link, s, place, row, final):
            link(dve.tensor_copy(s["pl_i"][:], place[:]))
            link(dve.tensor_scalar(s["lo_i"][:], s["pl_i"][:], P - 1, None, ALU.bitwise_and))
            link(dve.tensor_scalar(s["pl_i"][:], s["pl_i"][:], 7, None, ALU.arith_shift_right))
            link(dve.tensor_copy(s["run"][:], s["lo_i"][:]))
            link(dve.tensor_copy(s["spot"][:], s["pl_i"][:]))
            if final:
                link(dve.memset(s["zero"][:], 0.0))
                for k in range(1, CH):
                    link(dve.scalar_tensor_tensor(s["zero"][:], s["spot"][:], float(CT * k), s["zero"][:],
                                             ALU.is_ge, ALU.add))
                link(dve.tensor_scalar(s["spot"][:], s["spot"][:], float(CH), None, ALU.mult))
                link(dve.scalar_tensor_tensor(s["spot"][:], s["zero"][:], float(1 - CH * CT), s["spot"][:],
                                         ALU.mult, ALU.add))
            link(dve.scalar_tensor_tensor(s["run"][:], s["run"][:], float(T if final else TR), s["spot"][:],
                                     ALU.mult, ALU.add))
            link(dve.tensor_copy(row[:], s["run"][:]))

        def rank_scratch(st, name):
            s = {"zero": SB(st, name + "_zero", [P, TR]), "base": SB(st, name + "_base", [P, 1]),
                 "base_i": SB(st, name + "_base_i", [P, 1], I32), "hit": SB(st, name + "_hit", [P, TR], BF16),
                 "run": SB(st, name + "_run", [P, TR]), "spot": SB(st, name + "_spot", [P, TR]),
                 "pl_i": SB(st, name + "_pl_i", [P, TR], I32), "lo_i": SB(st, name + "_lo_i", [P, TR], I32),
                 "ps_pre": PS(st, name + "_ps_pre", [P, 512]), "ps_tot": PS(st, name + "_ps_tot", [P, 512]),
                 "hit_ready": sem(name + "_hit_ready"), "counted": sem(name + "_counted")}
            return s

        SG = 13

        def scatter_pool(pool, s, rows, records, table):
            def half(i, h):
                pool.tensor_copy(s["idx"][:, h, :], rows[:, bass.ds(i * 2 * SG + h * SG, SG)])\
                    .then_inc(s["idx_ready"], 1)
                pool.tensor_copy(s["out"][:, h, :, :], records[:, bass.ds(i * 2 * SG + h * SG, SG), :])\
                    .then_inc(s["idx_ready"], 1)
                pool.wait_ge(s["idx_ready"], i * 4 + 2 * h + 2)
                pool.nop(nofuse=True)
                for u in range(SG):
                    pool.indirect_dma_start(
                        out=table, out_offset=bass.IndirectOffsetOnAxis(ap=s["idx"][:, h, u:u + 1], axis=0),
                        in_=s["out"][:, h, u, :],
                        in_offset=None).then_inc(s["written"][h], 16)
            for h in range(2):
                half(0, h)
            with pool.Fori(1, (TR - 1) // (2 * SG)) as i:
                for h in range(2):
                    pool.wait_ge(s["written"][h], i * (16 * SG))
                    half(i, h)
            for h in range(2):
                pool.wait_ge(s["written"][h], (TR - 1) // 2 * 16)
            pool.tensor_copy(s["idx"][:, 0, 0:1], rows[:, TR - 1:TR]).then_inc(s["idx_ready"], 1)
            pool.wait_ge(s["idx_ready"], (TR - 1) // SG * 2 + 1)
            pool.indirect_dma_start(
                out=table, out_offset=bass.IndirectOffsetOnAxis(ap=s["idx"][0:LAST, 0, 0:1], axis=0),
                in_=records[0:LAST, TR - 1, :], in_offset=None).then_inc(s["written"][0], 16)
            pool.wait_ge(s["written"][0], (TR - 1) // 2 * 16 + 16)

        def scatter_scratch(st, name, width):
            return {"out": SB(st, name + "_out", [P, 2, SG, width]), "idx": SB(st, name + "_idx", [P, 2, SG], I32),
                    "idx_ready": sem(name + "_idx_ready"),
                    "written": [sem(name + f"_written{h}") for h in range(2)]}
        assert (TR - 1) % (2 * SG) == 0

        with ExitStack() as st:
            recs = SB(st, "recs", [P, TR, FR])
            recd = SB(st, "recd", [P, TR, 8])
            key_s = SB(st, "key_s", [P, TR])
            place_s = SB(st, "place_s", [P, TR])
            row_s = SB(st, "row_s", [P, TR], I32)
            key_d = SB(st, "key_d", [P, TR])
            place_d = SB(st, "place_d", [P, TR])
            row_d = SB(st, "row_d", [P, TR], I32)
            fill_st = SB(st, "fill_st", [P, T // STEPS, FR])
            c_ready = sem("consts_ready")
            loaded = sem("edges_loaded")
            filled = sem("tables_filled")
            fill_ready = sem("fill_ready")
            tau = SB(st, "tau", [P, T])
            with ExitStack() as s2:
                e_src = SB(s2, "e_src", [P, TR], I32)
                e_dst = SB(s2, "e_dst", [P, TR], I32)
                e_typ = SB(s2, "e_typ", [P, TR], I32)
                e_tmp = SB(s2, "e_tmp", [P, TR], I32)
                e_tf = SB(s2, "e_tf", [P, TR])
                e_w = SB(s2, "e_w", [P, 2, TR])
                d_line = SB(s2, "d_line", [P, TR + 1], I32)
                d_viol = SB(s2, "d_viol", [P, TR])
                viol = SB(s2, "viol", [P, 1])
                fill_d = SB(s2, "fill_d", [P, 8])
                fill_s = SB(s2, "fill_s", [P, FR])
                fill_dt = SB(s2, "fill_dt", [P, TR, 8])
                tau_i = SB(s2, "tau_i", [P, T], I32)
                ps_v = PS(s2, "ps_v", [P, 512])
                viol_ready = sem("viol_ready")
                viol_sum = sem("viol_sum")
                with phase() as block:
                    @block.sync
                    def _(sp):
                        sp.dma_start(e_src[:], a["src"]).then_inc(loaded, 16)
                        sp.dma_start(e_dst[:], a["dst"]).then_inc(loaded, 16)
                        sp.dma_start(e_typ[:], a["typ"]).then_inc(loaded, 16)
                        sp.dma_start(e_w[:, 0, :], a["w"]).then_inc(loaded, 16)
                        sp.dma_start(e_w[:, 1, :], a["w1"]).then_inc(loaded, 16)
                        sp.dma_start(d_line[:], a["dst_line"]).then_inc(loaded, 16)
                        sp.dma_start(X[:], a["x"].rearrange("(b p) d -> p b d", p=P)).then_inc(loaded, 16)
                        sp.wait_ge(fill_ready, 1)
                        sp.dma_start(rec_lin[TR * P:TR * P + P, :], fill_d[:]).then_inc(filled, 16)
                        sp.dma_start(rec_tmp.rearrange("(p t) f -> p (t f)", p=P),
                                     fill_dt[:].rearrange("p t f -> p (t f)")).then_inc(filled, 16)
                        sp.wait_ge(filled, 16 * 2)
                        sp.wait_ge(loaded, 16 * 7)

                    @block.gpsimd
                    def _(pool):
                        pool.iota(iota_i[:], pattern=[[1, P]], base=0, channel_multiplier=0).then_inc(c_ready, 1)
                        pool.iota(pid_i[:], pattern=[[0, 1]], base=0, channel_multiplier=1).then_inc(c_ready, 1)
                        pool.iota(tau_i[:], pattern=[[1, CT], [CT, CH]], base=0, channel_multiplier=0)\
                            .then_inc(c_ready, 1)

                    @block.tensor
                    def _(pe):
                        pe.wait_ge(viol_ready, 1)
                        pe.matmul(ps_v[:, 0:1], lhsT=ones[:], rhs=viol[:], start=True, stop=True)\
                            .then_inc(viol_sum, 1)

                    @block.vector
                    def _(dve):
                        link = Chain(dve, "setup_step").link
                        link(dve.memset(fill_d[:], 0.0))
                        link(dve.memset(fill_d[:, 1:2], -1.0))
                        link(dve.memset(fill_d[:, 5:7], -1.0))
                        link(dve.memset(fill_s[:], 0.0))
                        link(dve.memset(fill_s[:, 34:35], -1.0))
                        link(dve.tensor_copy(fill_dt[:], fill_d[:].unsqueeze(1).to_broadcast([P, TR, 8])))
                        link(dve.tensor_copy(fill_st[:], fill_s[:].unsqueeze(1).to_broadcast([P, T // STEPS, FR])))
                        dve.sem_inc(fill_ready, 1)
                        dve.wait_ge(c_ready, 3)
                        link(dve.tensor_copy(tau[:], tau_i[:]))
                        link(dve.tensor_copy(iota_f[:], iota_i[:]))
                        link(dve.tensor_copy(pid[:, 0:1], pid_i[:]))
                        link(dve.tensor_scalar(pid[:, 1:2], pid[:, 0:1], 8.0, None, ALU.add))
                        link(dve.tensor_scalar(pid[:, 2:3], pid[:, 0:1], -8.0, None, ALU.add))
                        link(dve.tensor_scalar(ident[:], iota_f[:], pid[:, 0:1], None, ALU.is_equal))
                        link(dve.tensor_scalar(below[:], iota_f[:], pid[:, 1:2], None, ALU.is_equal))
                        link(dve.tensor_scalar(above[:], iota_f[:], pid[:, 2:3], None, ALU.is_equal))
                        link(dve.tensor_scalar(tri_m1[:], iota_f[:], pid[:, 0:1], -1.0, ALU.is_le, ALU.mult))
                        link(dve.memset(ones_bf[:], 1.0))
                        link(dve.tensor_copy(ident_bf[:], ident[:]))
                        link(dve.memset(ones[:], 1.0))
                        dve.wait_ge(loaded, 16 * 7)
                        link(dve.tensor_tensor(d_viol[:], d_line[:, 1:TR + 1], d_line[:, 0:TR], ALU.is_lt))
                        link(dve.tensor_reduce(viol[:], d_viol[:], AX.X, ALU.add))
                        dve.sem_inc(viol_ready, 1)
                        link(dve.tensor_copy(recs[:, :, 32], e_w[:, 1, :]))
                        link(dve.tensor_copy(recs[:, :, 33], e_dst[:]))
                        link(dve.tensor_scalar(e_tmp[:], e_src[:], P - 1, None, ALU.bitwise_and))
                        link(dve.tensor_copy(recs[:, :, 34], e_tmp[:]))
                        link(dve.tensor_scalar(e_tmp[:], e_src[:], 7, None, ALU.arith_shift_right))
                        link(dve.tensor_copy(recs[:, :, 35], e_tmp[:]))
                        link(dve.tensor_copy(key_s[:], e_tmp[:]))
                        link(dve.memset(recd[:], 0.0))
                        link(dve.tensor_copy(recd[:, :, 0], e_src[:]))
                        link(dve.tensor_copy(recd[:, :, 1], e_dst[:]))
                        link(dve.tensor_copy(e_tf[:], e_typ[:]))
                        link(dve.scalar_tensor_tensor(recd[:, :, 2], e_tf[:], float(NP), recd[:, :, 0],
                                                 ALU.mult, ALU.add))
                        link(dve.tensor_copy(recd[:, :, 3], e_w[:, 0, :]))
                        link(dve.tensor_copy(recd[:, :, 4], e_w[:, 1, :]))
                        link(dve.tensor_scalar(e_tmp[:], e_dst[:], P - 1, None, ALU.bitwise_and))
                        link(dve.tensor_copy(recd[:, :, 5], e_tmp[:]))
                        link(dve.tensor_scalar(e_tmp[:], e_dst[:], 7, None, ALU.arith_shift_right))
                        link(dve.tensor_copy(recd[:, :, 6], e_tmp[:]))
                        dve.wait_ge(viol_sum, 1)
                        link(dve.tensor_copy(unsorted_i[:], ps_v[:, 0:1]))

            def bucket_key(dve, link, key, digit, t):
                link(dve.tensor_scalar(t[:], recd[:, :, 1], 0.0, None, ALU.is_ge))
                link(dve.scalar_tensor_tensor(key[:], digit, 1.0, t[:], ALU.add, ALU.mult))
                link(dve.tensor_scalar(key[:], key[:], -1.0, None, ALU.add))

            with ExitStack() as s2:
                rt = [rank_scratch(s2, "rank_t0")]
                sct = [scatter_scratch(s2, "scat_t0", 8)]
                for k in (1, 2):
                    rt.append(dict(rt[0], hit_ready=sem(f"rank_t{k}_hit_ready"), counted=sem(f"rank_t{k}_counted")))
                    sct.append(dict(sct[0], idx_ready=sem(f"scat_t{k}_idx_ready"),
                                    written=[sem(f"scat_t{k}_written{h}") for h in range(2)]))
                placed, passed, reloaded = sem("pass_placed"), sem("pass_scattered"), sem("pass_reloaded")

                def out_of_order(eng):
                    return eng.If(eng.value_load(unsorted_i[0:1, 0:1], min_val=0, max_val=P * (TR + 1)))

                with phase() as block:
                    @block.vector
                    def _(dve):
                        c = Chain(dve, "pass_step")
                        with out_of_order(dve):
                            for k in range(3):
                                r = rt[k]
                                if k:
                                    dve.wait_ge(reloaded, 16 * k)
                                c.link(dve.tensor_copy(r["lo_i"][:], recd[:, :, 6 if k == 2 else 5]))
                                if k == 0:
                                    c.link(dve.tensor_scalar(r["lo_i"][:], r["lo_i"][:], 15, None, ALU.bitwise_and))
                                elif k == 1:
                                    c.link(dve.tensor_scalar(r["lo_i"][:], r["lo_i"][:], 4, None,
                                                             ALU.arith_shift_right))
                                c.link(dve.tensor_copy(r["spot"][:], r["lo_i"][:]))
                                bucket_key(dve, c.link, key_d, r["spot"][:], r["run"])
                                rank_vector(dve, c, r, key_d, place_d, False)
                                place_to_row(dve, c.link, r, place_d, row_d, False)
                                dve.sem_inc(placed, 1)

                    @block.tensor
                    def _(pe):
                        with out_of_order(pe):
                            for k in range(3):
                                rank_tensor(pe, rt[k])

                    @block.gpsimd
                    def _(pool):
                        with out_of_order(pool):
                            for k in range(3):
                                pool.wait_ge(placed, k + 1)
                                scatter_pool(pool, sct[k], row_d, recd, rec_tmp)
                                pool.sem_inc(passed, 1)

                    @block.sync
                    def _(sp):
                        with out_of_order(sp):
                            for k in range(3):
                                sp.wait_ge(passed, k + 1)
                                sp.dma_start(recd[:].rearrange("p t f -> p (t f)"),
                                             rec_tmp.rearrange("(p t) f -> p (t f)", p=P)).then_inc(reloaded, 16)
                                sp.wait_ge(reloaded, 16 * (k + 1))

            with ExitStack() as s2:
                rs = rank_scratch(s2, "rank_s")
                f_loaded, s_filled = sem("features_loaded"), sem("source_table_filled")
                with phase() as block:
                    @block.sync
                    def _(sp):
                        sp.dma_start(recs[:, :, 0:32], a["f"]).then_inc(f_loaded, 16)
                        for c in range(STEPS):
                            sp.dma_start(rec_s.rearrange("(p c t) f -> p c (t f)", p=P, c=STEPS)[:, c, :],
                                         fill_st[:].rearrange("p t f -> p (t f)")).then_inc(s_filled, 16)
                        sp.wait_ge(f_loaded, 16)
                        sp.wait_ge(s_filled, 16 * STEPS)

                    @block.vector
                    def _(dve):
                        c = Chain(dve, "rank_s_step")
                        rank_vector(dve, c, rs, key_s, place_s, True)
                        place_to_row(dve, c.link, rs, place_s, row_s, True)

                    @block.tensor
                    def _(pe):
                        rank_tensor(pe, rs)

            with ExitStack() as s2:
                ss = scatter_scratch(s2, "scat_s", FR)
                at_least = SB(s2, "at_least", [P, T // 4, NB])
                part = SB(s2, "part", [P, NB])
                from_ = SB(s2, "from", [P, NB + 1])
                tiles_b = SB(s2, "tiles_b", [P, NB])
                tiles_i = SB(s2, "tiles_i", [P, NB], I32)
                ends_b = SB(s2, "ends_b", [P, NB])
                pad_b = SB(s2, "pad_b", [P, NB + 1])
                zero_b = SB(s2, "zero_b", [P, NB])
                pads = SB(s2, "pads", [P, T])
                blk_f = SB(s2, "blk_f", [P, T])
                first_i = SB(s2, "first_i", [P, T], I32)
                ps_n = PS(s2, "lay_ps", [P, 512])
                stored, counted, totals, planned = (sem("lay_" + k) for k in ("stored", "counted", "totals", "planned"))
                with phase() as block:
                    @block.gpsimd
                    def _(pool):
                        scatter_pool(pool, ss, row_s, recs, rec_s)

                    @block.tensor
                    def _(pe):
                        pe.wait_ge(counted, 1)
                        pe.matmul(ps_n[:, 0:NB], lhsT=ones[:], rhs=part[:], start=True, stop=True).then_inc(totals, 1)

                    @block.vector
                    def _(dve):
                        link = Chain(dve, "lay_step").link
                        for k in range(NBU):
                            hit = at_least[:].rearrange("p t b -> p (t b)")[:, 0:NBU * TR].rearrange("p (b t) -> p b t", b=NBU)
                            link(dve.tensor_tensor(hit, recd[:, :, 6].unsqueeze(1).to_broadcast([P, NBU, TR]),
                                                   iota_f[:, k * NBU:(k + 1) * NBU].unsqueeze(2)
                                                   .to_broadcast([P, NBU, TR]), ALU.is_ge))
                            link(dve.tensor_reduce(part[:, k * NBU:(k + 1) * NBU], hit, AX.X, ALU.add))
                        dve.sem_inc(counted, 1)
                        link(dve.memset(from_[:], 0.0))
                        link(dve.memset(pad_b[:], 0.0))
                        link(dve.memset(zero_b[:], 0.0))
                        dve.wait_ge(totals, 1)
                        link(dve.tensor_copy(from_[:, 0:NB], ps_n[:, 0:NB]))
                        link(dve.tensor_tensor(tiles_b[:], from_[:, 0:NB], from_[:, 1:NB + 1], ALU.subtract))
                        link(dve.tensor_scalar(tiles_i[:], tiles_b[:], float(P - 1), None, ALU.add))
                        link(dve.tensor_scalar(tiles_i[:], tiles_i[:], 7, None, ALU.arith_shift_right))
                        link(dve.tensor_copy(tiles_b[:], tiles_i[:]))
                        link(dve.tensor_tensor_scan(ends_b[:], tiles_b[:], zero_b[:], 0.0, ALU.add, ALU.add))
                        link(dve.tensor_tensor(tiles_b[:], ends_b[:], tiles_b[:], ALU.subtract))
                        link(dve.scalar_tensor_tensor(pad_b[:, 1:NB + 1], tiles_b[:], float(P), from_[:, 0:NB],
                                                      ALU.mult, ALU.add))
                        link(dve.tensor_scalar(pad_b[:, 1:NB + 1], pad_b[:, 1:NB + 1], from_[:, 0:1], None,
                                               ALU.subtract))
                        link(dve.tensor_tensor(ends_b[:], pad_b[:, 1:NB + 1], pad_b[:, 0:NB], ALU.subtract))
                        for k in range(4):
                            c = slice(k * (T // 4), (k + 1) * (T // 4))
                            link(dve.tensor_tensor(at_least[:], tau[:, c].unsqueeze(2).to_broadcast([P, T // 4, NB]),
                                                   tiles_b[:].unsqueeze(1).to_broadcast([P, T // 4, NB]), ALU.is_ge))
                            link(dve.tensor_reduce(blk_f[:, c], at_least[:], AX.X, ALU.add))
                            link(dve.tensor_tensor(at_least[:], at_least[:],
                                                   ends_b[:].unsqueeze(1).to_broadcast([P, T // 4, NB]), ALU.mult))
                            link(dve.tensor_reduce(pads[:, c], at_least[:], AX.X, ALU.add))
                        link(dve.tensor_scalar(blk_i[:], blk_f[:], -1.0, None, ALU.add))
                        link(dve.scalar_tensor_tensor(pads[:], tau[:], float(P), pads[:], ALU.mult, ALU.subtract))
                        link(dve.tensor_scalar(first_i[:], pads[:], float(TR * P), None, ALU.min))
                        dve.sem_inc(planned, 1)

                    def fetch_tiles(eng, engine_type, fetched, half):
                        eng.wait_ge(stored, 16)
                        eng.wait_ge(planned, 1)
                        with eng.Fori(0, CT) as i:
                            j = i * CH + half * 8
                            first = nc.values_load_multi_w_load_instructions(
                                first_i[0:1, bass.ds(j, 8)], engines=(engine_type,), min_val=0, max_val=TR * P)[1]
                            for k in range(8):
                                eng.dma_start(att[:, bass.ds(j + k, 1), :].rearrange("p t f -> p (t f)"),
                                              rec_lin[bass.ds(first[k], P), :]).then_inc(fetched, 16)
                        eng.wait_ge(fetched, 16 * 8 * CT)

                    fetched = [sem(f"tiles_fetched{h}") for h in range(2)]

                    @block.sync
                    def _(sp):
                        sp.dma_start(rec_lin[0:TR * P, :].rearrange("(t p) f -> p t f", p=P), recd[:])\
                            .then_inc(stored, 16)
                        fetch_tiles(sp, mybir.EngineType.SP, fetched[0], 0)

                    @block.scalar
                    def _(act):
                        fetch_tiles(act, mybir.EngineType.Activation, fetched[1], 1)

        def to_scan_tensor(pe, s, data):
            v = data[:].rearrange("p (a c) h -> p a (c h)", c=CH)
            for t in range(CT):
                q, r = divmod(t, 4)
                if r == 0 and q >= 2:
                    pe.wait_ge(s["scan_copied"], q - 1)
                pe.transpose(s["ps_scan"][:, q % 2, r * P:(r + 1) * P], v[:, t, :], ident[:])\
                    .then_inc(s["scan_turned"], 1)

        def to_scan_scalar(act, s, dest):
            for q in range(-(-CT // 4)):
                n = min(4, CT - 4 * q)
                act.wait_ge(s["scan_turned"], 4 * q + n)
                act.copy(dest[:, q * 4 * P:q * 4 * P + n * P], s["ps_scan"][:, q % 2, 0:n * P])\
                    .then_inc(s["scan_copied"], 1)

        with ExitStack() as st:
            rec2 = att
            own = SB(st, "own", [P, T])
            dst8 = SB(st, "dst8", [P, T, 8])
            dscan = SB(st, "dscan", [P, SC + 1])
            s = {"ps_scan": PS(st, "r_ps_scan", [P, 2, 512]), "scan_copied": sem("r_copied"),
                 "scan_turned": sem("r_turned")}
            ps_n = PS(st, "r_ps_n", [P, 512])
            r_loaded = sem("r_loaded")
            r_dst8 = sem("r_dst8")
            r_col = sem("r_col")
            r_shift = sem("r_shift")
            with phase() as block:
                @block.sync
                def _(sp):
                    sp.dma_start(rs4[:], rec_s.rearrange("(p t) f -> p t f", p=P)[:, :, 32:36]).then_inc(r_loaded, 16)
                    sp.wait_ge(r_loaded, 16)

                @block.tensor
                def _(pe):
                    pe.wait_ge(r_dst8, 1)
                    to_scan_tensor(pe, s, dst8)
                    pe.wait_ge(s["scan_copied"], -(-CT // 4))
                    pe.matmul(ps_n[:, 0:1], lhsT=below[:], rhs=dscan[:, SC:SC + 1], start=True, stop=True)\
                        .then_inc(r_shift, 1)
                    pe.wait_ge(r_col, 1)
                    pe.matmul(ps_n[:, 1:2], lhsT=above[:], rhs=reset[:, 0:1], start=True, stop=True)\
                        .then_inc(r_shift, 1)

                @block.scalar
                def _(act):
                    to_scan_scalar(act, s, dscan[:, 1:SC + 1])

                @block.vector
                def _(dve):
                    link = Chain(dve, "reload_step").link
                    link(dve.tensor_copy(own[:], blk_i[:]))
                    link(dve.tensor_tensor(own[:], own[:], rec2[:, :, 6], ALU.is_equal))
                    for k in (1, 5):
                        link(dve.scalar_tensor_tensor(rec2[:, :, k], rec2[:, :, k], 1.0, own[:], ALU.add, ALU.mult))
                        link(dve.tensor_scalar(rec2[:, :, k], rec2[:, :, k], -1.0, None, ALU.add))
                    for k in (0, 2):
                        link(dve.tensor_tensor(rec2[:, :, k], rec2[:, :, k], own[:], ALU.mult))
                    link(dve.tensor_copy(dst8[:], rec2[:, :, 1:2].to_broadcast([P, T, 8])))
                    dve.sem_inc(r_dst8, 1)
                    link(dve.tensor_copy(src_i[:], rec2[:, :, 0]))
                    link(dve.tensor_copy(hr_i[:], rec2[:, :, 2]))
                    link(dve.tensor_copy(ew[:], rec2[:, :, 3]))
                    link(dve.tensor_copy(ew1[:], rec2[:, :, 4]))
                    link(dve.tensor_copy(dloc[:], rec2[:, :, 5]))
                    dve.wait_ge(r_loaded, 16)
                    link(dve.tensor_copy(dst2_i[:], rs4[:, :, 1]))
                    link(dve.tensor_copy(sblk_i[:], rs4[:, :, 3]))
                    dve.wait_ge(r_shift, 1)
                    link(dve.tensor_copy(dscan[:, 0:1], ps_n[:, 0:1]))
                    link(dve.tensor_tensor(reset[:, 0:SC], dscan[:, 1:SC + 1], dscan[:, 0:SC], ALU.not_equal))
                    link(dve.tensor_scalar(reset[:, 0:SC], reset[:, 0:SC], -BIG, None, ALU.mult))
                    dve.sem_inc(r_col, 1)
                    dve.wait_ge(r_shift, 2)
                    link(dve.tensor_copy(reset[:, SC:SC + 1], ps_n[:, 1:2]))

        def segment_exp(name):
            with ExitStack() as st:
                sc = SB(st, name + "_sc", [P, SC])
                fw = SB(st, name + "_fw", [P, SC])
                col = SB(st, name + "_col", [P, 4])
                rowb = SB(st, name + "_row", [1, 4, P])
                s = {"ps_scan": PS(st, name + "_ps_scan", [P, 2, 512]), "scan_copied": sem(name + "_copied"),
                     "scan_turned": sem(name + "_turned")}
                ps_b = PS(st, name + "_ps_b", [P, 2, 512])
                ps_r = PS(st, name + "_ps_r", [P, 512])
                ps_c = PS(st, name + "_ps_c", [P, 512])
                c_ends, c_rows, c_carry, c_col = (sem(name + n) for n in ("_ends", "_rows", "_carry", "_col"))
                m_ready, m_back, m_used = (sem(name + n) for n in ("_max", "_back", "_used"))
                e_done = sem(name + "_exp")
                vb = att[:].rearrange("p (a c) h -> p (a c h)", c=CH)
                with phase() as block:
                    @block.tensor
                    def _(pe):
                        to_scan_tensor(pe, s, att)
                        for k in range(2):
                            pe.wait_ge(c_ends, k + 1)
                            pe.matmul(ps_r[0:1, 0:P], lhsT=col[:, 2 * k:2 * k + 1], rhs=ident[:],
                                      start=True, stop=True)
                            pe.matmul(ps_r[0:1, P:2 * P], lhsT=col[:, 2 * k + 1:2 * k + 2], rhs=ident[:],
                                      start=True, stop=True).then_inc(c_rows, 1)
                            pe.wait_ge(c_carry, k + 1)
                            pe.matmul(ps_c[:, k:k + 1], lhsT=rowb[0:1, 3, :], rhs=ones[0:1, 0:1],
                                      start=True, stop=True).then_inc(c_col, 1)
                        pe.wait_ge(m_ready, 1)
                        for t in range(CT):
                            q, r = divmod(t, 4)
                            if r == 0 and q >= 2:
                                pe.wait_ge(m_used, q - 1)
                            pe.transpose(ps_b[:, q % 2, r * P:(r + 1) * P], sc[:, t * P:(t + 1) * P], ident[:])\
                                .then_inc(m_back, 1)

                    @block.scalar
                    def _(act):
                        to_scan_scalar(act, s, sc)
                        act.wait_ge(m_used, -(-CT // 4))
                        act.activation(att[:].rearrange("p t h -> p (t h)"), att[:].rearrange("p t h -> p (t h)"),
                                       ACT.Exp).then_inc(e_done, 1)

                    @block.vector
                    def _(dve):
                        link = Chain(dve, name + "_step").link
                        r_fw, r_bw = reset[:, 0:SC], reset[:, 1:SC + 1]
                        dve.wait_ge(s["scan_copied"], -(-CT // 4))
                        link(dve.tensor_reduce(col[:, 1:2], r_fw, AX.X, ALU.min))
                        link(dve.tensor_reduce(col[:, 3:4], r_bw, AX.X, ALU.min))
                        for k in range(2):
                            if k == 0:
                                o, r, x = fw[:], r_fw, sc[:]
                                end = fw[:, SC - 1:SC]
                            else:
                                o, r, x = sc[:, ::-1], r_bw[:, ::-1], fw[:, ::-1]
                                end = sc[:, 0:1]
                            link(dve.tensor_tensor_scan(o, r, x, -BIG, ALU.add, ALU.max))
                            link(dve.tensor_copy(col[:, 2 * k:2 * k + 1], end))
                            dve.sem_inc(c_ends, 1)
                            dve.wait_ge(c_rows, k + 1)
                            link(dve.tensor_copy(rowb[0:1, 0, :].rearrange("o (h c) -> o c h", h=8),
                                            ps_r[0:1, 0:P].rearrange("o (c h) -> o c h", h=8)))
                            link(dve.tensor_copy(rowb[0:1, 1, :].rearrange("o (h c) -> o c h", h=8),
                                            ps_r[0:1, P:2 * P].rearrange("o (c h) -> o c h", h=8)))
                            first = CH - 1 if k else 0
                            link(dve.memset(rowb[0:1, 1, :].rearrange("o (h c) -> o h c", h=8)[:, :, first:first + 1], -BIG))
                            rv = (lambda n: rowb[0:1, n, ::-1]) if k else (lambda n: rowb[0:1, n, :])
                            link(dve.tensor_tensor_scan(rv(2), rv(1), rv(0), -BIG, ALU.add, ALU.max))
                            link(dve.memset(rowb[0:1, 3, :], -BIG))
                            src = rowb[0:1, 2, :].rearrange("o (h c) -> o c h", h=8)
                            dst = rowb[0:1, 3, :].rearrange("o (c h) -> o c h", h=8)
                            if k == 0:
                                link(dve.tensor_copy(dst[:, 1:CH, :], src[:, 0:CH - 1, :]))
                                dve.sem_inc(c_carry, 1)
                            else:
                                link(dve.tensor_copy(dst[:, 0:CH - 1, :], src[:, 1:CH, :]))
                                dve.sem_inc(c_carry, 1)
                            dve.wait_ge(c_col, k + 1)
                            link(dve.tensor_copy(col[:, 2 * k:2 * k + 1], ps_c[:, k:k + 1]))
                            link(dve.tensor_tensor_scan(o, r, x, col[:, 2 * k:2 * k + 1], ALU.add, ALU.max))
                        dve.sem_inc(m_ready, 1)
                        for q in range(-(-CT // 4)):
                            n = min(4, CT - 4 * q)
                            dve.wait_ge(m_back, 4 * q + n)
                            av = vb[:, 4 * q * P:(4 * q + n) * P]
                            dve.tensor_tensor(av, av, ps_b[:, q % 2, 0:n * P], ALU.subtract).then_inc(m_used, 1)

        def rolled(eng, body, chain=None):
            body(0)
            if chain is None:
                with eng.Fori(1, STEPS - 1) as i:
                    body(i)
            else:
                with chain.loop(1, STEPS - 1, chain.n - chain.mark) as i:
                    body(i)
            body(STEPS - 1)

        def wait(eng, s, value):
            if not (isinstance(value, int) and value <= 0):
                eng.wait_ge(s, value)

        def exists(i, q):
            return q < 4 or not (isinstance(i, int) and i == STEPS - 1)

        def block_numbers(eng, engine_type, blocks, t):
            return nc.values_load_multi_w_load_instructions(
                blocks[0:1, bass.ds(t, G)], engines=(engine_type,), min_val=0, max_val=NB - 1)[1]

        def gather_ring(pool, table, idx_all, idx, gat, idx_ready, got, used, used_per_quarter):
            def indices(i, q):
                if q < 4:
                    wait(pool, got[q], i * (16 * G))
                else:
                    pool.wait_ge(got[q - 4], (i + 1) * (16 * G))
                pool.nop(nofuse=True)
                pool.tensor_copy(idx[:, q % 4, :], idx_all[:, bass.ds(i * 16 + q * G, G)]).then_inc(idx_ready, 1)

            def body(i):
                for q in range(4):
                    if exists(i, q + 1):
                        indices(i, q + 1)
                    wait(pool, used, (i * 4 + (q - 3)) * used_per_quarter)
                    pool.wait_ge(idx_ready, i * 4 + (q + 1))
                    pool.nop(nofuse=True)
                    for u in range(G):
                        pool.indirect_dma_start(
                            out=gat[:, q, u, :], out_offset=None, in_=table,
                            in_offset=bass.IndirectOffsetOnAxis(ap=idx[:, q, u:u + 1], axis=0))\
                            .then_inc(got[q], 16)
            indices(0, 0)
            rolled(pool, body)

        def edge_scores(name, table, wt, node_rows, wn, combine):
            with ExitStack() as st:
                gat = SB(st, name + "_gat", [P, 4, G, wt])
                idx = SB(st, name + "_idx", [P, 4, G], I32)
                loc = SB(st, name + "_loc", [P, 2, G])
                hot = SB(st, name + "_hot", [P, 2, G, P])
                hot_t = SB(st, name + "_hot_t", [P, 2, G, P])
                prod = SB(st, name + "_prod", [P, G, P])
                red = SB(st, name + "_red", [P, G, 8])
                tmp = SB(st, name + "_tmp", [P, G, 8])
                ps_t = PS(st, name + "_ps_t", [P, 2, G, P])
                ps_q = PS(st, name + "_ps_q", [P, 2, G, P])
                idx_ready, hot_ready, turned, copied, spread, scored = (
                    sem(name + n) for n in ("_idx_ready", "_hot_ready", "_turned", "_copied", "_spread", "_scored"))
                got = [sem(name + f"_got{q}") for q in range(4)]
                with phase() as block:
                    @block.gpsimd
                    def _(pool):
                        gather_ring(pool, table, src_i, idx, gat, idx_ready, got, scored, 1)

                    @block.vector
                    def _(dve):
                        c = Chain(dve, name + "_step")

                        def one_hots(i, q):
                            wait(dve, turned, i * 4 + (q - 1))
                            c.link(move(dve, loc[:, q % 2, :], dloc[:, bass.ds(i * 16 + q * G, G)]))
                            for u in range(G):
                                ins = dve.tensor_scalar(hot[:, q % 2, u, :], iota_f[:], loc[:, q % 2, u:u + 1], None,
                                                        ALU.is_equal)
                            ins.then_inc(hot_ready, 1)

                        def body(i):
                            for q in range(4):
                                if exists(i, q + 2):
                                    one_hots(i, q + 2)
                                dve.wait_ge(got[q], (i + 1) * (16 * G))
                                dve.wait_ge(spread, i * 4 + (q + 1))
                                combine(dve, c.link, i * 16 + q * G, gat[:, q, :, :], ps_q[:, q % 2, :, :],
                                        prod, red, tmp)
                                dve.sem_inc(scored, 1)
                        one_hots(0, 0)
                        one_hots(0, 1)
                        c.mark = c.n
                        rolled(dve, body, c)

                    @block.tensor
                    def _(pe):
                        def turn(i, q):
                            pe.wait_ge(hot_ready, i * 4 + (q + 1))
                            wait(pe, copied, i * 4 + (q - 1))
                            for u in range(G):
                                ins = pe.transpose(ps_t[:, q % 2, u, :], hot[:, q % 2, u, :], ident[:])
                            ins.then_inc(turned, 1)

                        def spread_rows(i, q):
                            ks = block_numbers(pe, mybir.EngineType.PE, blk_i, i * 16 + q * G)
                            pe.wait_ge(copied, i * 4 + (q + 1))
                            wait(pe, scored, i * 4 + (q - 1))
                            for u in range(G):
                                ins = pe.matmul(ps_q[:, q % 2, u, 0:wn], lhsT=hot_t[:, q % 2, u, :],
                                                rhs=node_rows[:, bass.ds(ks[u] * wn, wn)],
                                                start=True, stop=True)
                            ins.then_inc(spread, 1)

                        def body(i):
                            for q in range(4):
                                if exists(i, q + 1):
                                    spread_rows(i, q + 1)
                                if exists(i, q + 2):
                                    turn(i, q + 2)
                        turn(0, 0)
                        turn(0, 1)
                        spread_rows(0, 0)
                        rolled(pe, body)

                    @block.scalar
                    def _(act):
                        def body(i):
                            for q in range(4):
                                act.wait_ge(turned, i * 4 + (q + 1))
                                wait(act, spread, i * 4 + (q - 1))
                                act.copy(hot_t[:, q % 2, :, :], ps_t[:, q % 2, :, :]).then_inc(copied, 1)
                        rolled(act, body)

        def near_scores(name, table, by_src, src_local, src_block, by_dst, heads):
            w = heads * NB
            with ExitStack() as st:
                hot = SB(st, name + "_hot", [P, 2, 2, G, P], BF16)
                hot_t = SB(st, name + "_hot_t", [P, 2, 2, G, P], BF16)
                src3 = SB(st, name + "_src3", [P, 3, NB, heads], BF16)
                dst3 = SB(st, name + "_dst3", [P, 3, w], BF16)
                rest = SB(st, name + "_rest", [P, NB, heads])
                own = SB(st, name + "_own", [P, G, NB])
                sel = SB(st, name + "_sel", [P, G, NB, heads])
                gat = SB(st, name + "_gat", [P, 2, G, H3])
                idx = SB(st, name + "_idx", [P, 2, G], I32)
                red = SB(st, name + "_red", [P, G, heads])
                ps_t = PS(st, name + "_ps_t", [P, 2, 2, G, P], BF16)
                ps_v = PS(st, name + "_ps_v", [P, 2, 512])
                hot_ready, turned, copied, spread, scored = (
                    sem(name + n) for n in ("_hot_ready", "_turned", "_copied", "_spread", "_scored"))
                split = sem(name + "_split")
                idx_ready, got = sem(name + "_idx_ready"), [sem(name + f"_got{k}") for k in range(2)]

                def gathered(q):
                    return q % 2 == 0

                def values(b):
                    v = ps_v[:, b, 0:G * (w + heads)].rearrange("p (g v) -> p g v", g=G)
                    return v[:, :, 0:w], v[:, :, w:w + heads]
                with phase() as block:
                    @block.gpsimd
                    def _(pool):
                        def indices(i, k):
                            wait(pool, got[k % 2], (i + k // 2) * (16 * G))
                            pool.nop(nofuse=True)
                            pool.tensor_copy(idx[:, k % 2, :], src_i[:, bass.ds(i * 16 + 2 * k * G, G)])\
                                .then_inc(idx_ready, 1)

                        def body(i):
                            for k in range(2):
                                if exists(i, 2 * k + 2):
                                    indices(i, k + 1)
                                wait(pool, scored, i * 4 + (2 * k - 3))
                                pool.wait_ge(idx_ready, i * 2 + (k + 1))
                                pool.nop(nofuse=True)
                                for u in range(G):
                                    pool.indirect_dma_start(
                                        out=gat[:, k, u, :], out_offset=None, in_=table,
                                        in_offset=bass.IndirectOffsetOnAxis(ap=idx[:, k, u:u + 1], axis=0))\
                                        .then_inc(got[k], 16)
                        indices(0, 0)
                        rolled(pool, body)

                    @block.vector
                    def _(dve):
                        c = Chain(dve, name + "_step")

                        def is_it(out_, nodes, width, t0):
                            return dve.tensor_tensor(out_, iota_f[:, 0:width].unsqueeze(1).to_broadcast([P, G, width]),
                                                     nodes[:, bass.ds(t0, G)].unsqueeze(2).to_broadcast([P, G, width]),
                                                     ALU.is_equal)

                        def one_hots(i, q):
                            wait(dve, turned, i * 4 + (q - 1))
                            ins = is_it(hot[:, q % 2, 0, :, :], dloc, P, i * 16 + q * G)
                            if not gathered(q):
                                ins = is_it(hot[:, q % 2, 1, :, :], src_local, P, i * 16 + q * G)
                            ins.then_inc(hot_ready, 1)

                        def body(i):
                            for q in range(4):
                                if exists(i, q + 2):
                                    one_hots(i, q + 2)
                                vs, vd = values(q % 2)
                                if gathered(q):
                                    dve.wait_ge(got[q // 2], (i + 1) * (16 * G))
                                    dve.wait_ge(spread, i * 4 + (q + 1))
                                    at_source = gat[:, q // 2, :, 0:heads]
                                else:
                                    c.link(is_it(own[:], src_block, NB, i * 16 + q * G))
                                    dve.wait_ge(spread, i * 4 + (q + 1))
                                    wait(dve, scored, i * 4 + q)
                                    c.link(dve.tensor_tensor(
                                        sel[:], vs.rearrange("p g (b h) -> p g b h", h=heads),
                                        own[:].unsqueeze(3).to_broadcast([P, G, NB, heads]), ALU.mult))
                                    c.link(dve.tensor_reduce(red[:], sel[:].rearrange("p g b h -> p g h b"),
                                                             AX.X, ALU.add))
                                    at_source = red[:]
                                dve.tensor_tensor(att[:, bass.ds(i * 16 + q * G, G), 0:heads], at_source, vd, ALU.add)\
                                    .then_inc(scored, 1)
                        split3(dve, c.link, by_src[:, :, 0:heads], rest[:], [src3[:, k, :, :] for k in range(3)])
                        split3(dve, c.link, by_dst[:], rest[:].rearrange("p b h -> p (b h)"),
                               [dst3[:, k, :] for k in range(3)])
                        dve.sem_inc(split, 1)
                        one_hots(0, 0)
                        one_hots(0, 1)
                        c.mark = c.n
                        rolled(dve, body, c)

                    @block.tensor
                    def _(pe):
                        pe.wait_ge(split, 1)

                        def turn(i, q):
                            pe.wait_ge(hot_ready, i * 4 + (q + 1))
                            wait(pe, copied, i * 4 + (q - 1))
                            for k in range(1 if gathered(q) else 2):
                                for u in range(G):
                                    ins = pe.transpose(ps_t[:, q % 2, k, u, :], hot[:, q % 2, k, u, :], ident_bf[:])
                            ins.then_inc(turned, 1)

                        def look_up(i, q):
                            ks = block_numbers(pe, mybir.EngineType.PE, blk_i, i * 16 + q * G)
                            pe.wait_ge(copied, i * 4 + (q + 1))
                            wait(pe, scored, i * 4 + (q - 1))
                            vs, vd = values(q % 2)
                            for u in range(G):
                                for k in range(3):
                                    ins = pe.matmul(vd[:, u, :], lhsT=hot_t[:, q % 2, 0, u, :],
                                                    rhs=dst3[:, k, bass.ds(ks[u] * heads, heads)],
                                                    start=k == 0, stop=k == 2)
                                for k in range(0 if gathered(q) else 3):
                                    ins = pe.matmul(vs[:, u, :], lhsT=hot_t[:, q % 2, 1, u, :],
                                                    rhs=src3[:, k, :, :].rearrange("p b h -> p (b h)"),
                                                    start=k == 0, stop=k == 2)
                            ins.then_inc(spread, 1)

                        def body(i):
                            for q in range(4):
                                if exists(i, q + 2):
                                    turn(i, q + 2)
                                if exists(i, q + 1):
                                    look_up(i, q + 1)
                        turn(0, 0)
                        turn(0, 1)
                        look_up(0, 0)
                        rolled(pe, body)

                    @block.scalar
                    def _(act):
                        def body(i):
                            for q in range(4):
                                act.wait_ge(turned, i * 4 + (q + 1))
                                wait(act, spread, i * 4 + (q - 1))
                                n = 1 if gathered(q) else 2
                                act.copy(hot_t[:, q % 2, 0:n, :, :], ps_t[:, q % 2, 0:n, :, :]).then_inc(copied, 1)
                        rolled(act, body)

        def edge_sums(name, table, wt, idx_all, local, blocks, weight, nh, ws, acc, banks, rows=None, mlp=None):
            with ExitStack() as st:
                gat = SB(st, name + "_gat", [P, 4, G, wt])
                idx = SB(st, name + "_idx", [P, 4, G], I32)
                loc = SB(st, name + "_loc", [P, 2, G])
                wgt = SB(st, name + "_wgt", [P, 2, G, 8])
                hot = SB(st, name + "_hot", [P, 2, G, nh, P])
                made = SB(st, name + "_made", [P, 2, G, ws]) if rows else None
                helped = nh > 1
                plain = SB(st, name + "_plain", [P, 2, G, P]) if helped else None
                wgt_a = SB(st, name + "_wgt_a", [P, 2, G, 8]) if helped else None
                weighed, fetched = (sem(name + n) for n in ("_weighed", "_fetched"))
                shared = G * ws * banks <= 512
                per = 2 if shared else 8 // banks
                ps = PS(st, name + "_ps", [P, per * banks, 512])
                idx_ready, hot_ready, rows_ready, summed, added = (
                    sem(name + n) for n in ("_idx_ready", "_hot_ready", "_rows_ready", "_summed", "_added"))
                got = [sem(name + f"_got{q}") for q in range(4)]

                def slot(q, u):
                    if shared:
                        return ps[:, q % 2, u * ws:(u + 1) * ws]
                    if banks == 1:
                        return ps[:, (q % 2) * G + u, 0:ws]
                    return ps[:, 2 * u:2 * u + 2, 0:2 * ws]
                m = mlp(st, rows_ready) if mlp else None
                with phase() as block:
                    @block.gpsimd
                    def _(pool):
                        gather_ring(pool, table, idx_all, idx, gat, idx_ready, got, summed, G)

                    @block.vector
                    def _(dve):
                        c = Chain(dve, name + "_step")
                        c.link(dve.memset(acc[:], 0.0))

                        def targets(i, q):
                            t0 = i * 16 + q * G
                            wait(dve, hot_ready, (i * 4 + (q - 1)) * G)
                            ins = move(dve, loc[:, q % 2, :], local[:, bass.ds(t0, G)])
                            if weight is not None:
                                ins = move(dve, wgt[:, q % 2, :, 0:nh], weight[:, bass.ds(t0, G), 0:nh])
                            c.start(ins)

                        def one_hot(i, q, u):
                            b, at_ = q % 2, loc[:, q % 2, u:u + 1]
                            if weight is None:
                                dve.tensor_scalar(hot[:, b, u, 0, :], iota_f[:], at_, None, ALU.is_equal)\
                                    .then_inc(hot_ready, 1)
                            else:
                                dve.tensor_scalar(hot[:, b, u, 0, :], iota_f[:], at_, wgt[:, b, u, 0:1],
                                                  ALU.is_equal, ALU.mult).then_inc(hot_ready, 1)

                        def tiles(i, q, add, make):
                            t0 = i * 16 + q * G

                            def make_hot(u):
                                if add:
                                    dve.wait_ge(summed, t0 + (u + 1))
                                one_hot(i, q + 2, u)

                            ahead = 0 if rows else 2
                            if make and helped:
                                if add:
                                    dve.wait_ge(weighed, t0 + G)
                                dve.tensor_tensor(
                                    plain[:, q % 2, :, :], iota_f[:].unsqueeze(1).to_broadcast([P, G, P]),
                                    local[:, bass.ds(t0 + 2 * G, G)].unsqueeze(2).to_broadcast([P, G, P]),
                                    ALU.is_equal).then_inc(hot_ready, 1)
                            elif make:
                                targets(i, q + 2)
                                if not rows:
                                    c.finish()
                                for u in range(ahead):
                                    make_hot(u)
                            if add:
                                ks = block_numbers(dve, mybir.EngineType.DVE, blocks, t0)
                            if make and rows:
                                c.finish()
                            if make and mlp:
                                softplus_sum(dve, m, i * 4 + (q + 2), q % 2)
                            for u in range(G):
                                if add:
                                    dve.wait_ge(summed, t0 + (G if shared else u + 1))
                                    w = nh * ws
                                    av = acc[:, bass.ds(ks[u] * w, w)]
                                    if banks == 2:
                                        av = av.rearrange("p (a b) -> p a b", a=2)
                                    dve.tensor_tensor(av, av, slot(q % 4, u), ALU.add).then_inc(added, 1)
                                if make and not helped and u + ahead < G:
                                    make_hot(u + ahead)
                                if add:
                                    dve.wait_ge(added, t0 + (u + 1))

                        def body(i):
                            first = isinstance(i, int) and i == 0
                            for q in range(4):
                                if mlp and exists(i, q + 1):
                                    softplus_ramp(dve, m, i * 4 + (q + 1), (q + 1) % 2, m["ps_h"][:, (q + 1) % 2, :])
                                if rows:
                                    dve.wait_ge(got[q], (i + 1) * (16 * G))
                                    rows(dve, i * 4 + q, q % 2, i * 16 + q * G, gat[:, q, :, :],
                                         made[:, q % 2, :, :], m).then_inc(rows_ready, 1)
                                tiles(i, q - 1, q or not first, exists(i, q + 1))
                        if mlp:
                            softplus_ramp(dve, m, 0, 0, m["ps_h"][:, 0, :])
                        tiles(0, -2, False, True)
                        c.mark = c.n
                        rolled(dve, body, c)
                        tiles(STEPS - 1, 3, True, False)

                    @block.tensor
                    def _(pe):
                        def body(i):
                            for q in range(4):
                                if mlp and exists(i, q + 3):
                                    m["turn"](pe, i, q + 3)
                                if mlp and exists(i, q + 2):
                                    m["front"](pe, i, q + 2)
                                if mlp and exists(i, q + 1):
                                    m["back"](pe, i, q + 1)
                                if rows:
                                    pe.wait_ge(rows_ready, i * 4 + (q + 1))
                                else:
                                    pe.wait_ge(got[q], (i + 1) * (16 * G))
                                t0 = i * 16 + q * G
                                for u in range(G):
                                    pe.wait_ge(weighed if helped else hot_ready, t0 + (u + 1))
                                    wait(pe, added, t0 + (-G if shared else u + 1 - per))
                                    src = made[:, q % 2, u, :] if rows else gat[:, q, u, :]
                                    for k in range(nh):
                                        if banks == 1:
                                            o = slot(q, u)
                                        else:
                                            o = ps[:, u * 2 + k // 2, (k % 2) * ws:(k % 2) * ws + ws]
                                        ins = pe.matmul(o, lhsT=hot[:, q % 2, u, k, :],
                                                        rhs=src[:, k * ws:(k + 1) * ws], start=True, stop=True)
                                    ins.then_inc(summed, 1)
                        if mlp:
                            for q in range(3):
                                m["turn"](pe, 0, q)
                                if q < 2:
                                    m["front"](pe, 0, q)
                            m["back"](pe, 0, 0)
                        rolled(pe, body)

                    if helped:
                        @block.scalar
                        def _(act):
                            def weights(i, q):
                                t0 = i * 16 + q * G
                                wait(act, weighed, t0 - G)
                                act.copy(wgt_a[:, q % 2, :, 0:nh], weight[:, bass.ds(t0, G), 0:nh])\
                                    .then_inc(fetched, 1)

                            def body(i):
                                for q in range(4):
                                    t0 = i * 16 + q * G
                                    if exists(i, q + 1):
                                        weights(i, q + 1)
                                    act.wait_ge(fetched, i * 4 + (q + 1))
                                    act.wait_ge(hot_ready, i * 4 + (q + 1))
                                    for u in range(G):
                                        wait(act, summed, t0 + (u + 1 - 2 * G))
                                        for k in range(nh):
                                            ins = act.activation(hot[:, q % 2, u, k, :], plain[:, q % 2, u, :],
                                                                 ACT.Copy, scale=wgt_a[:, q % 2, u, k:k + 1])
                                        ins.then_inc(weighed, 1)
                            weights(0, 0)
                            rolled(act, body)

                    if mlp:
                        @block.scalar
                        def _(act):
                            m["scalar"](act)

                        @block.sync
                        def _(sp):
                            m["sync"](sp)

        W5 = NBU * P

        def node_stage(name, fill, kd, tensor, vector, n_vector, scalar, scratch, load=None, store=None,
                       n_scalar=0):
            with ExitStack() as st:
                stage = SB(st, name + "_stage", [P, NBU * kd, P])
                xt = SB(st, name + "_xt", [P, NBU * kd, P])
                nb = -(-NBU * kd // 4)
                ps_x = PS(st, name + "_ps_x", [P, 2, 4, P])
                staged, turned, copied = (sem(name + n) for n in ("_staged", "_turned", "_copied"))
                in_w, outs = sem(name + "_weights"), sem(name + "_stored")
                done_v, taken = sem(name + "_vdone"), sem(name + "_taken")
                s = scratch(st)
                with phase() as block:
                    @block.sync
                    def _(sp):
                        nl = load(sp, s, in_w) if load else 0
                        if store:
                            sp.wait_ge(done_v, 1)
                            ns = store(sp, s, outs)
                            sp.wait_ge(outs, 16 * ns)

                    @block.gpsimd
                    def _(pool):
                        c = Chain(pool, name + "_fill_step")
                        with c.loop(0, NBI, fill[1]) as i:
                            fill[0](pool, c.link, stage, i)
                            pool.sem_inc(staged, 1)
                            pool.wait_ge(turned, (i + 1) * nb)

                    @block.tensor
                    def _(pe):
                        with pe.Fori(0, NBI) as i:
                            pe.wait_ge(staged, i + 1)
                            for q in range(nb):
                                if q >= 2:
                                    pe.wait_ge(copied, i * nb + (q - 1))
                                c = min(4, NBU * kd - 4 * q)
                                for r in range(c):
                                    ins = pe.transpose(ps_x[:, q % 2, r, :], stage[:, 4 * q + r, :], ident[:])
                                ins.then_inc(turned, 1)
                            pe.wait_ge(copied, (i + 1) * nb)
                            pe.wait_ge(taken, i + 1)
                            tensor(pe, s, i, xt)

                    @block.scalar
                    def _(act):
                        steps = Chain(act, name + "_act_step")
                        with steps.loop(0, NBI, n_scalar) as i:
                            for q in range(nb):
                                act.wait_ge(turned, i * nb + (q + 1))
                                c = min(4, NBU * kd - 4 * q)
                                act.copy(xt[:, 4 * q:4 * q + c, :], ps_x[:, q % 2, 0:c, :]).then_inc(copied, 1)
                            scalar(act, steps.link, s, i)

                    @block.vector
                    def _(dve):
                        c = Chain(dve, name + "_step")
                        dve.sem_inc(taken, 1)
                        with c.loop(0, NBI, n_vector) as i:
                            vector(dve, c.link, s, i)
                            dve.sem_inc(taken, 1)
                        dve.sem_inc(done_v, 1)

        def blocks_of(data):
            flat = data[:].rearrange("p b d -> p (b d)") if len(data.shape) == 3 else data[:]

            def fill(pool, link, stage, i):
                link(pool.tensor_copy(stage[:].rearrange("p a d -> p (a d)"), flat[:, bass.ds(i * W5, W5)]))
            return fill, 1

        def nothing(*_):
            pass

        def add_norm(name, update, relu, last=False):
            with ExitStack() as st:
                sq = SB(st, name + "_sq", [P, NB, D])
                mean = SB(st, name + "_mean", [P, NB])
                var = SB(st, name + "_var", [P, NB])
                dev = SB(st, name + "_dev", [P, NB])
                v_ready, r_ready, o_ready, stored = (sem(name + n) for n in ("_var_r", "_dev_r", "_out_r", "_stored"))
                with phase() as block:
                    @block.vector
                    def _(dve):
                        link = Chain(dve, name + "_step").link
                        if relu:
                            link(dve.scalar_tensor_tensor(X[:], update, 0.0, X[:], ALU.max, ALU.add))
                        else:
                            link(dve.tensor_tensor(X[:], X[:], update, ALU.add))
                        link(dve.tensor_reduce(mean[:], X[:], AX.X, ALU.add))
                        link(dve.tensor_scalar(mean[:], mean[:], 1.0 / D, None, ALU.mult))
                        link(dve.tensor_tensor(X[:], X[:], mean[:].unsqueeze(2).to_broadcast([P, NB, D]), ALU.subtract))
                        link(dve.tensor_tensor(sq[:], X[:], X[:], ALU.mult))
                        link(dve.tensor_reduce(var[:], sq[:], AX.X, ALU.add))
                        link(dve.tensor_scalar(var[:], var[:], 1.0 / D, EPS, ALU.mult, ALU.add))
                        dve.sem_inc(v_ready, 1)
                        dve.wait_ge(r_ready, 1)
                        link(dve.reciprocal(dev[:], dev[:]))
                        link(dve.tensor_tensor(X[:], X[:], dev[:].unsqueeze(2).to_broadcast([P, NB, D]), ALU.mult))
                        dve.sem_inc(o_ready, 1)

                    @block.scalar
                    def _(act):
                        act.wait_ge(v_ready, 1)
                        act.activation(dev[:], var[:], ACT.Sqrt).then_inc(r_ready, 1)

                    if last:
                        @block.sync
                        def _(sp):
                            sp.wait_ge(o_ready, 1)
                            full = NB - 1
                            sp.dma_start(out[0:full * P, :].rearrange("(b p) d -> p b d", p=P), X[:, 0:full, :])\
                                .then_inc(stored, 16)
                            sp.dma_start(out[full * P:N_NODES, :], X[0:N_NODES - full * P, full, :])\
                                .then_inc(stored, 16)
                            sp.wait_ge(stored, 32)

        with ExitStack() as st:
            acc = SB(st, "l0_acc", [P, NB * D])

            def scratch(s_):
                return {"w": SB(s_, "l0_w", [P, 3 * D]), "hr": SB(s_, "l0_hr", [P, NB, 3 * D]),
                        "ps": PS(s_, "l0_ps", [P, NBU, 512]), "mm": sem("l0_mm")}

            def load(sp, s, in_w):
                sp.dma_start(s["w"][:].rearrange("p (r o) -> p r o", r=3),
                             a["L0_w"].rearrange("r i o -> i r o")).then_inc(in_w, 16)
                s["in_w"] = in_w
                return 1

            def tensor(pe, s, i, xt):
                pe.wait_ge(s["in_w"], 16)
                for u in range(NBU):
                    pe.matmul(s["ps"][:, u, 0:3 * D], lhsT=xt[:, u, :], rhs=s["w"][:], start=True, stop=True)\
                        .then_inc(s["mm"], 1)

            def vector(dve, link, s, i):
                for u in range(NBU):
                    dve.wait_ge(s["mm"], i * NBU + (u + 1))
                    link(move(dve, s["hr"][:, bass.ds(i * NBU + u, 1), :],
                                         s["ps"][:, u:u + 1, 0:3 * D]))

            def store(sp, s, outs):
                for r in range(3):
                    sp.dma_start(t_hr[r * NP:(r + 1) * NP, :].rearrange("(b p) d -> p b d", p=P),
                                 s["hr"][:, :, r * D:(r + 1) * D]).then_inc(outs, 16)
                return 3
            node_stage("l0n", blocks_of(X), 1, tensor, vector, NBU, nothing, scratch, load, store)
            edge_sums("l0e", t_hr, D, hr_i, dloc, blk_i, ew[:].unsqueeze(2), 1, D, acc, 1)
            add_norm("l0x", acc[:].rearrange("p (b d) -> p b d", b=NB), True)
        with ExitStack() as st:
            q_all = SB(st, "l1_q", [P, NB * D])
            w_all = SB(st, "l1_w", [P, 3 * D])
            b_row = SB(st, "l1_b", [1, 3 * D])
            rel = SB(st, "l1_rel", [P, D])
            with ExitStack() as s2:
                wv = SB(s2, "l1_wv", [P, D])
                bd = SB(s2, "l1_bd", [P, D])
                bv = SB(s2, "l1_bv", [P, 1])
                ps = PS(s2, "l1_ps_w", [P, 512])
                in_w, z_ready, mm = sem("l1_weights"), sem("l1_zeroed"), sem("l1_folded")
                with phase() as block:
                    @block.sync
                    def _(sp):
                        sp.dma_start(w_all[:, 0:D], a["L1_Wk"]).then_inc(in_w, 16)
                        sp.dma_start(w_all[:, D:2 * D], a["L1_Wq"]).then_inc(in_w, 16)
                        sp.dma_start(wv[:], a["L1_Wv"]).then_inc(in_w, 16)
                        sp.dma_start(b_row[:, 0:D], a["L1_bk"].unsqueeze(0)).then_inc(in_w, 16)
                        sp.dma_start(b_row[:, D:2 * D], a["L1_bq"].unsqueeze(0)).then_inc(in_w, 16)
                        sp.dma_start(bv[:], a["L1_bv"].unsqueeze(1)).then_inc(in_w, 16)
                        sp.dma_start(rel[:], a["L1_rel"].unsqueeze(0).to_broadcast([P, D])).then_inc(in_w, 16)
                        sp.wait_ge(z_ready, 1)
                        for h in range(H1):
                            sp.dma_start(bd[h * DK:(h + 1) * DK, h * DK:(h + 1) * DK], a["L1_rel_msg"][h])\
                                .then_inc(in_w, 16)
                        sp.wait_ge(in_w, 16 * (7 + H1))

                    @block.tensor
                    def _(pe):
                        pe.wait_ge(in_w, 16 * (7 + H1))
                        pe.matmul(ps[:, 0:D], lhsT=wv[:], rhs=bd[:], start=True, stop=True)
                        pe.matmul(ps[0:1, D:2 * D], lhsT=bv[:], rhs=bd[:], start=True, stop=True).then_inc(mm, 1)

                    @block.vector
                    def _(dve):
                        link = Chain(dve, "l1_prep_step").link
                        link(dve.memset(bd[:], 0.0))
                        dve.sem_inc(z_ready, 1)
                        dve.wait_ge(mm, 1)
                        link(dve.tensor_copy(w_all[:, 2 * D:3 * D], ps[:, 0:D]))
                        link(dve.tensor_copy(b_row[:, 2 * D:3 * D], ps[0:1, D:2 * D]))

            def scratch(s_):
                return {"k": SB(s_, "l1_k", [P, NB, D + H1]), "v": SB(s_, "l1_v", [P, NB, D]),
                        "t": SB(s_, "l1_t", [P, D]), "r": SB(s_, "l1_r", [P, H1]), "ps": PS(s_, "l1_ps", [P, NBU, 512]), "mm": sem("l1_mm")}

            def tensor(pe, s, i, xt):
                for u in range(NBU):
                    pe.matmul(s["ps"][:, u, 0:3 * D], lhsT=xt[:, u, :], rhs=w_all[:], start=True, stop=False)
                    pe.matmul(s["ps"][:, u, 0:3 * D], lhsT=ones[0:1, :], rhs=b_row[:], start=False, stop=True)\
                        .then_inc(s["mm"], 1)

            def vector(dve, link, s, i):
                for u in range(NBU):
                    dve.wait_ge(s["mm"], i * NBU + (u + 1))
                    b = i * NBU + u
                    kb = s["k"][:, bass.ds(b, 1), 0:D].rearrange("p b d -> p (b d)")
                    link(move(dve, kb, s["ps"][:, u, 0:D]))
                    link(move(dve, q_all[:, bass.ds(b * D, D)], s["ps"][:, u, D:2 * D]))
                    link(move(dve, s["v"][:, bass.ds(b, 1), :].rearrange("p b d -> p (b d)"),
                                         s["ps"][:, u, 2 * D:3 * D]))
                    link(dve.tensor_tensor(s["t"][:], kb, rel[:], ALU.mult))
                    link(dve.tensor_reduce(s["r"][:], s["t"][:].rearrange("p (h d) -> p h d", h=H1), AX.X, ALU.add))
                    link(move(dve, s["k"][:, bass.ds(b, 1), D:D + H1].rearrange("p b h -> p (b h)"), s["r"][:]))

            def store(sp, s, outs):
                sp.dma_start(t_k.rearrange("(b p) d -> p b d", p=P), s["k"][:]).then_inc(outs, 16)
                sp.dma_start(t_v.rearrange("(b p) d -> p b d", p=P), s["v"][:]).then_inc(outs, 16)
                return 2
            node_stage("l1n", blocks_of(X), 1, tensor, vector, 6 * NBU, nothing, scratch, store=store)

            def combine(dve, link, t0, rows, ps_q, prod, red, tmp):
                link(dve.tensor_tensor(prod[:], rows[:, :, 0:D], ps_q, ALU.mult))
                link(dve.tensor_reduce(red[:], prod[:].rearrange("p g (h d) -> p g h d", h=H1), AX.X, ALU.add))
                link(dve.tensor_tensor(tmp[:], rows[:, :, D:D + H1],
                                       ew[:, bass.ds(t0, G)].unsqueeze(2).to_broadcast([P, G, H1]), ALU.mult))
                link(dve.tensor_tensor(red[:], red[:], tmp[:], ALU.add))
                link(dve.tensor_scalar(att[:, bass.ds(t0, G), :], red[:], float(DK) ** -0.5, None, ALU.mult))
            edge_scores("l1s", t_k, D + H1, q_all, D, combine)
        segment_exp("l1x")

        with ExitStack() as st:
            acc = SB(st, "l1_acc", [P, NB * (D + H1)])
            upd = SB(st, "l1_upd", [P, NB, D])
            den = SB(st, "l1_den", [P, NB, H1])

            def rows(dve, n, b, t0, got, made, m):
                e = att[:, bass.ds(t0, G), :]
                dve.tensor_tensor(made[:, :, 0:D].rearrange("p g (h d) -> p g h d", h=H1),
                                  got.rearrange("p g (h d) -> p g h d", h=H1),
                                  e.unsqueeze(3).to_broadcast([P, G, H1, DK]), ALU.mult)
                return move(dve, made[:, :, D:D + H1], e)
            edge_sums("l1e", t_v, D, src_i, dloc, blk_i, None, 1, D + H1, acc, 1, rows)
            av = acc[:].rearrange("p (b d) -> p b d", b=NB)
            with phase() as block:
                @block.vector
                def _(dve):
                    link = Chain(dve, "l1_div_step").link
                    link(dve.tensor_scalar(den[:], av[:, :, D:D + H1], 1e-30, None, ALU.max))
                    link(dve.reciprocal(den[:], den[:]))
                    link(dve.tensor_tensor(upd[:].rearrange("p b (h d) -> p b h d", h=H1),
                                           av[:, :, 0:D].rearrange("p b (h d) -> p b h d", h=H1),
                                           den[:].unsqueeze(3).to_broadcast([P, NB, H1, DK]), ALU.mult))
            add_norm("l1x2", upd[:], True)

        def softplus_scalar(act, link, s, n, b, y):
            act.wait_ge(s["hid"], n + 1)
            wait(act, s["soft"], n + (1 - s["bufs"]))
            link(act.activation(s["l"][:, b, :], y, ACT.Abs, bias=s["bias"][:, 0:1]))
            act.sem_inc(s["abs_taken"], 1)
            link(act.activation(s["l"][:, b, :], s["l"][:, b, :], ACT.Exp, scale=-1.0))
            link(act.activation(s["l"][:, b, :], s["l"][:, b, :], ACT.Ln, bias=1.0))
            act.sem_inc(s["l_ready"], 1)

        def softplus_ramp(dve, s, n, b, y):
            dve.wait_ge(s["abs_taken"], n + 1)
            wait(dve, s["sp_used"], n + (1 - s["bufs"]))
            dve.tensor_scalar(s["sp"][:, b, :], y, s["bias"][:, 0:1], 0.0, ALU.add, ALU.max).then_inc(s["y_read"], 1)

        def softplus_sum(dve, s, n, b):
            dve.wait_ge(s["l_ready"], n + 1)
            dve.wait_ge(s["y_read"], n + 1)
            dve.tensor_tensor(s["sp"][:, b, :], s["sp"][:, b, :], s["l"][:, b, :], ALU.add).then_inc(s["soft"], 1)

        def softplus_scratch(s_, name, width, bias, bufs):
            s = {"bias": bias, "bufs": bufs}
            for k in ("l", "sp"):
                s[k] = SB(s_, f"{name}_{k}", [P, bufs, width])
            for k in ("hid", "abs_taken", "y_read", "l_ready", "soft", "sp_used"):
                s[k] = sem(f"{name}_{k}")
            return s

        with ExitStack() as st:
            w_in = SB(st, "l2_w_in", [P, D])
            wf1 = SB(st, "l2_wf1", [32, D])
            wf2 = SB(st, "l2_wf2", [P, D])
            wo1 = SB(st, "l2_wo1", [P, D])
            wo2 = SB(st, "l2_wo2", [P, D])
            bf1 = SB(st, "l2_bf1", [P, 1])
            bo1 = SB(st, "l2_bo1", [P, 1])
            rows2 = SB(st, "l2_rows", [1, 2, D])
            nlog2 = SB(st, "l2_nlog2", [P, 1])
            bias3 = SB(st, "l2_bias3", [3, 2, D], BF16)
            parts = SB(st, "l2_parts", [1, 3, 2, D], BF16)
            part_f = SB(st, "l2_part_f", [1, 2, D])
            acc = SB(st, "l2_acc", [P, NB * D])
            with ExitStack() as s2:
                ps = PS(s2, "l2_ps_b", [P, 512])
                in_w, set_, mm, split = (sem("l2_" + k) for k in ("weights", "set", "sums", "split"))
                with phase() as block:
                    @block.sync
                    def _(sp):
                        for d, k in ((w_in, "W_in"), (wf1, "Wf1"), (wf2, "Wf2"), (wo1, "Wo1"), (wo2, "Wo2")):
                            sp.dma_start(d[:], a["L2_" + k]).then_inc(in_w, 16)
                        sp.dma_start(bf1[:], a["L2_bf1"].unsqueeze(1)).then_inc(in_w, 16)
                        sp.dma_start(bo1[:], a["L2_bo1"].unsqueeze(1)).then_inc(in_w, 16)
                        sp.dma_start(rows2[:, 0, :], a["L2_bf2"].unsqueeze(0)).then_inc(in_w, 16)
                        sp.dma_start(rows2[:, 1, :], a["L2_bo2"].unsqueeze(0)).then_inc(in_w, 16)
                        sp.wait_ge(in_w, 16 * 9)
                        sp.wait_ge(split, 1)
                        for k in range(3):
                            sp.dma_start(bias3[k:k + 1, :, :], parts[:, k, :, :]).then_inc(in_w, 16)
                        sp.wait_ge(in_w, 16 * 12)

                    @block.tensor
                    def _(pe):
                        pe.wait_ge(set_, 1)
                        pe.wait_ge(in_w, 16 * 9)
                        pe.matmul(ps[0:1, 0:D], lhsT=nlog2[:], rhs=wf2[:], start=True, stop=True)
                        pe.matmul(ps[0:1, D:2 * D], lhsT=nlog2[:], rhs=wo2[:], start=True, stop=True).then_inc(mm, 1)

                    @block.vector
                    def _(dve):
                        link = Chain(dve, "l2_prep_step").link
                        link(dve.memset(nlog2[:], -LOG2))
                        dve.sem_inc(set_, 1)
                        dve.wait_ge(mm, 1)
                        link(dve.tensor_tensor(rows2[:], rows2[:], ps[0:1, 0:2 * D].rearrange("o (k d) -> o k d", k=2),
                                               ALU.add))
                        split3(dve, link, rows2[:], part_f[:], [parts[:, k, :, :] for k in range(3)])
                        dve.sem_inc(split, 1)

            def scratch(s_):
                return {"h": SB(s_, "l2_h", [P, NB, D]), "ps": PS(s_, "l2_ps", [P, NBU, 512]), "mm": sem("l2_mm")}

            def tensor(pe, s, i, xt):
                for u in range(NBU):
                    pe.matmul(s["ps"][:, u, 0:D], lhsT=xt[:, u, :], rhs=w_in[:], start=True, stop=True)\
                        .then_inc(s["mm"], 1)

            def vector(dve, link, s, i):
                for u in range(NBU):
                    dve.wait_ge(s["mm"], i * NBU + (u + 1))
                    link(move(dve, s["h"][:, bass.ds(i * NBU + u, 1), :], s["ps"][:, u:u + 1, 0:D]))

            def store(sp, s, outs):
                sp.dma_start(t_h.rearrange("(b p) d -> p b d", p=P), s["h"][:]).then_inc(outs, 16)
                return 1
            node_stage("l2n", blocks_of(X), 1, tensor, vector, NBU, nothing, scratch, store=store)

            def filters(s_, w_used):
                m = softplus_scratch(s_, "l2f", G * P, bf1, 2)
                rec = SB(s_, "l2f_rec", [P, 4, G, FR])
                ft = SB(s_, "l2f_ft", [32, 2, G * P])
                ps_f = PS(s_, "l2f_ps_f", [32, 2, G * P])
                ps_h = PS(s_, "l2f_ps_h", [P, 2, G * P])
                ps_w = PS(s_, "l2f_ps_w", [P, 2, G, P])
                turned, copied = (sem("l2f_" + k) for k in ("turned", "copied"))
                loaded_f = [sem(f"l2f_loaded{q}") for q in range(4)]
                view = rec_s.rearrange("(p t) f -> p (t f)", p=P)

                def sync(sp):
                    def body(i):
                        for q in range(4):
                            wait(sp, turned, i * 4 + (q - 3))
                            sp.dma_start(rec[:, q, :, :].rearrange("p g f -> p (g f)"),
                                         view[:, bass.ds((i * 16 + q * G) * FR, G * FR)]).then_inc(loaded_f[q], 16)
                    rolled(sp, body)
                    for q in range(4):
                        sp.wait_ge(loaded_f[q], 16 * STEPS)

                def turn(pe, i, q):
                    n, r, b = i * 4 + q, q % 4, q % 2
                    pe.wait_ge(loaded_f[r], (i + (q // 4 + 1)) * 16)
                    wait(pe, copied, n - 1)
                    for u in range(G):
                        ins = pe.transpose(ps_f[:, b, u * P:(u + 1) * P], rec[:, r, u, 0:32], ident[:])
                    ins.then_inc(turned, 1)

                def front(pe, i, q):
                    n, b = i * 4 + q, q % 2
                    pe.wait_ge(copied, n + 1)
                    wait(pe, m["y_read"], n - 1)
                    pe.matmul(ps_h[:, b, :], lhsT=wf1[:], rhs=ft[:, b, :], start=True, stop=True)\
                        .then_inc(m["hid"], 1)

                def back(pe, i, q):
                    n, b = i * 4 + q, q % 2
                    pe.wait_ge(m["soft"], n + 1)
                    wait(pe, w_used, n - 1)
                    for u in range(G):
                        pe.matmul(ps_w[:, b, u, :], lhsT=ones_bf[0:3, :], rhs=bias3[:, 0, :],
                                  start=True, stop=False)
                        ins = pe.matmul(ps_w[:, b, u, :], lhsT=m["sp"][:, b, u * P:(u + 1) * P], rhs=wf2[:],
                                        start=False, stop=True)
                    ins.then_inc(m["sp_used"], 1)

                def scalar(act):
                    act.preload_act_table_set("natural_log_exp_and_others")
                    c = Chain(act, "l2f_act_step")

                    def features(i, q):
                        act.wait_ge(turned, i * 4 + (q + 1))
                        wait(act, m["hid"], i * 4 + (q - 1))
                        act.copy(ft[:, q % 2, :], ps_f[:, q % 2, :]).then_inc(copied, 1)

                    def body(i):
                        for q in range(4):
                            if exists(i, q + 3):
                                features(i, q + 3)
                            if exists(i, q + 2):
                                softplus_scalar(act, c.link, m, i * 4 + (q + 2), q % 2, ps_h[:, q % 2, :])
                    for q in range(3):
                        features(0, q)
                        if q < 2:
                            softplus_scalar(act, c.link, m, q, q, ps_h[:, q, :])
                    c.mark = c.n
                    rolled(act, body, c)
                m.update(sync=sync, ps_h=ps_h, turn=turn, front=front, back=back, scalar=scalar, ps_w=ps_w)
                return m

            def rows(dve, n, b, t0, got, made, m):
                dve.wait_ge(m["sp_used"], n + 1)
                return dve.tensor_tensor(made, got, m["ps_w"][:, b, :, :], ALU.mult)
            edge_sums("l2e", t_h, D, dst2_i, rs4[:, :, 2], sblk_i, rs4[:, :, 0:1], 1, D, acc, 1, rows, filters)

            upd = SB(st, "l2_upd", [P, NB, D])

            def scratch(s_):
                s = softplus_scratch(s_, "l2o", W5, bo1, 1)
                s["ps_h"] = PS(s_, "l2o_ps_h", [P, 2, 512])
                s["ps_o"] = PS(s_, "l2o_ps_o", [P, NBU, P])
                return s

            def tensor(pe, s, i, xt):
                pe.matmul(s["ps_h"][:, 0, 0:512], lhsT=wo1[:], rhs=xt[:].rearrange("p a d -> p (a d)")[:, 0:512],
                          start=True, stop=True)
                pe.matmul(s["ps_h"][:, 1, 0:W5 - 512], lhsT=wo1[:], rhs=xt[:].rearrange("p a d -> p (a d)")[:, 512:W5],
                          start=True, stop=True).then_inc(s["hid"], 1)
                pe.wait_ge(s["soft"], i + 1)
                for u in range(NBU):
                    pe.matmul(s["ps_o"][:, u, :], lhsT=ones_bf[0:3, :], rhs=bias3[:, 1, :], start=True, stop=False)
                    ins = pe.matmul(s["ps_o"][:, u, :], lhsT=s["sp"][:, 0, u * P:(u + 1) * P], rhs=wo2[:],
                                    start=False, stop=True)
                ins.then_inc(s["sp_used"], 1)

            def scalar(act, link, s, i):
                softplus_scalar(act, link, s, i, 0, s["ps_h"][:].rearrange("p a d -> p (a d)")[:, 0:W5])

            def vector(dve, link, s, i):
                softplus_ramp(dve, s, i, 0, s["ps_h"][:].rearrange("p a d -> p (a d)")[:, 0:W5])
                softplus_sum(dve, s, i, 0)
                dve.wait_ge(s["sp_used"], i + 1)
                link(move(dve, upd[:, bass.ds(i * NBU, NBU), :], s["ps_o"][:]))
            node_stage("l2o", blocks_of(acc), 1, tensor, vector, 1, scalar, scratch, n_scalar=3)
            add_norm("l2x", upd[:], False)

        def leaky(dve, link, dst, src, tmp):
            link(dve.tensor_scalar(tmp, src, 0.01, None, ALU.mult))
            link(dve.tensor_tensor(dst, tmp, src, ALU.max))

        def gat_scores(name, heads, table, a_src, a_dst, ew_, mw_):
            near_scores(name, table, a_src, src_local, src_block, a_dst, heads)
            with ExitStack() as s2:
                t = SB(s2, name + "_t", [P, T, heads])
                with phase() as block:
                    @block.vector
                    def _(dve):
                        link = Chain(dve, name + "_lin_step").link
                        v = att[:, :, 0:heads]
                        link(dve.tensor_tensor(t[:], v, ew1[:].unsqueeze(2).to_broadcast([P, T, heads]), ALU.mult))
                        link(dve.tensor_tensor(t[:], t[:], ew_.unsqueeze(1).to_broadcast([P, T, heads]), ALU.mult))
                        link(dve.scalar_tensor_tensor(t[:], t[:], 0.01, t[:], ALU.mult, ALU.max))
                        link(dve.memset(att[:], 0.0))
                        link(dve.tensor_tensor(v, t[:], mw_.unsqueeze(1).to_broadcast([P, T, heads]), ALU.mult))
            segment_exp(name + "x")

        with ExitStack() as st:
            acc = SB(st, "l3_acc", [P, NB * H3 * ZW])
            acc4 = acc[:].rearrange("p (b h d) -> p b h d", b=NB, h=H3)
            a_src = SB(st, "l3_a_src", [P, NB, H3])
            ao_src = SB(st, "l3_ao_src", [P, NB, H3])
            src_local = SB(st, "l3_src_local", [P, T])
            src_block = SB(st, "l3_src_block", [P, T])
            src_part = SB(st, "l3_src_part", [P, T], I32)
            a_dst = SB(st, "l3_a_dst", [P, NB * H3])
            ao_dst = SB(st, "l3_ao_dst", [P, NB])
            coef = SB(st, "l3_coef", [P, 10])
            with ExitStack() as s2:
                fc = SB(s2, "l3_fc", [P, H3 * D])
                at = SB(s2, "l3_at", [P, 2, H3 * D])
                in_w = sem("l3_weights")
                with phase() as block:
                    @block.sync
                    def _(sp):
                        sp.dma_start(fc[:], a["L3_fc"]).then_inc(in_w, 16)
                        sp.dma_start(at[:].rearrange("p k d -> p (k d)"),
                                     a["L3_at"].unsqueeze(0).to_broadcast([P, 2 * H3 * D])).then_inc(in_w, 16)
                        for k, (n, o) in {"ew": (4, 0), "mw": (4, 4), "oew": (1, 8), "omw": (1, 9)}.items():
                            sp.dma_start(coef[:, o:o + n], a["L3_" + k].unsqueeze(0).to_broadcast([P, n]))\
                                .then_inc(in_w, 16)
                        sp.wait_ge(in_w, 16 * 6)

                    @block.vector
                    def _(dve):
                        link = Chain(dve, "l3_prep_step").link
                        link(dve.memset(acc[:], 1.0))
                        link(dve.tensor_scalar(src_part[:], src_i[:], P - 1, None, ALU.bitwise_and))
                        link(dve.tensor_copy(src_local[:], src_part[:]))
                        link(dve.tensor_scalar(src_part[:], src_i[:], 7, None, ALU.arith_shift_right))
                        link(dve.tensor_copy(src_block[:], src_part[:]))

                def scratch(s_):
                    return {"ps": PS(s_, "l3_ps", [P, NBU, 512]), "mm": sem("l3_mm"),
                            "t": SB(s_, "l3_t", [P, H3, D]), "r": SB(s_, "l3_r", [P, H3])}

                def tensor(pe, s, i, xt):
                    for u in range(NBU):
                        pe.matmul(s["ps"][:, u, :], lhsT=xt[:, u, :], rhs=fc[:], start=True, stop=True)\
                            .then_inc(s["mm"], 1)

                def vector(dve, link, s, i):
                    for u in range(NBU):
                        b = i * NBU + u
                        dve.wait_ge(s["mm"], i * NBU + (u + 1))
                        z = acc4[:, bass.ds(b, 1), :, 0:D].rearrange("p b h d -> p (b h) d")
                        leaky(dve, link, z, s["ps"][:, u, :].rearrange("p (h d) -> p h d", h=H3), s["t"][:])
                        for k, o in ((0, a_src[:, bass.ds(b, 1), :].rearrange("p b h -> p (b h)")),
                                     (1, a_dst[:, bass.ds(b * H3, H3)])):
                            link(dve.tensor_tensor(s["t"][:], z, at[:, k, :].rearrange("p (h d) -> p h d", h=H3),
                                                   ALU.mult))
                            link(dve.tensor_reduce(s["r"][:], s["t"][:], AX.X, ALU.add))
                            link(move(dve, o, s["r"][:]))

                def store(sp, s, outs):
                    sp.dma_start(t_z.rearrange("(b p) d -> p b d", p=P),
                                 acc[:].rearrange("p (b d) -> p b d", b=NB)).then_inc(outs, 16)
                    sp.dma_start(t_as.rearrange("(b p) d -> p b d", p=P), a_src[:]).then_inc(outs, 16)
                    return 2
                node_stage("l3n", blocks_of(X), 1, tensor, vector, 8 * NBU, nothing, scratch, store=store)
            gat_scores("l3s", H3, t_as, a_src, a_dst, coef[:, 0:4], coef[:, 4:8])
            edge_sums("l3e", t_z, H3 * ZW, src_i, dloc, blk_i, att, H3, ZW, acc, 2)

            def divide(name, view, heads):
                with ExitStack() as s2:
                    den = SB(s2, name + "_den", [P, NB, heads])
                    with phase() as block:
                        @block.vector
                        def _(dve):
                            link = Chain(dve, name + "_step").link
                            link(dve.tensor_scalar(den[:].unsqueeze(3), view[:, :, :, D:ZW], 1e-30, None, ALU.max))
                            link(dve.reciprocal(den[:], den[:]))
                            for h in range(heads):
                                z = view[:, :, h, 0:D]
                                link(dve.tensor_tensor(z, z, den[:, :, h:h + 1].to_broadcast([P, NB, D]), ALU.mult))
                                link(dve.scalar_tensor_tensor(z, z, 0.01, z, ALU.mult, ALU.max))
            divide("l3d", acc4, H3)

            zo = SB(st, "l3_zo", [P, NB, ZW])
            with ExitStack() as s2:
                ofc = SB(s2, "l3_ofc", [P, H3, D])
                oat = SB(s2, "l3_oat", [P, 2, D])
                in_w = sem("l3_out_weights")
                with phase() as block:
                    @block.sync
                    def _(sp):
                        sp.dma_start(ofc[:], a["L3_ofc"]).then_inc(in_w, 16)
                        sp.dma_start(oat[:].rearrange("p k d -> p (k d)"),
                                     a["L3_oat"].unsqueeze(0).to_broadcast([P, 2 * D])).then_inc(in_w, 16)
                        sp.wait_ge(in_w, 32)

                    @block.vector
                    def _(dve):
                        link = Chain(dve, "l3_oprep_step").link
                        link(dve.memset(zo[:], 1.0))
                        link(dve.memset(ao_src[:], 0.0))

                def scratch(s_):
                    return {"ps": PS(s_, "l3o_ps", [P, NBU, 512]), "mm": sem("l3o_mm"),
                            "t": SB(s_, "l3o_t", [P, D]), "r": SB(s_, "l3o_r", [P, 1])}

                def fill(pool, link, stage, i):
                    for h in range(H3):
                        link(pool.tensor_copy(stage[:].rearrange("p (b h) d -> p b h d", h=H3)[:, :, h, :],
                                              acc4[:, bass.ds(i * NBU, NBU), h, 0:D]))

                def tensor(pe, s, i, xt):
                    for u in range(NBU):
                        for k in range(H3):
                            ins = pe.matmul(s["ps"][:, u, 0:D], lhsT=xt[:, u * H3 + k, :], rhs=ofc[:, k, :],
                                            start=k == 0, stop=k == H3 - 1)
                        ins.then_inc(s["mm"], 1)

                def vector(dve, link, s, i):
                    for u in range(NBU):
                        b = i * NBU + u
                        dve.wait_ge(s["mm"], i * NBU + (u + 1))
                        z = zo[:, bass.ds(b, 1), 0:D].rearrange("p b d -> p (b d)")
                        leaky(dve, link, z, s["ps"][:, u, 0:D], s["t"][:])
                        for k, o in ((0, ao_src[:, bass.ds(b, 1), 0]), (1, ao_dst[:, bass.ds(b, 1)])):
                            link(dve.tensor_tensor(s["t"][:], z, oat[:, k, :], ALU.mult))
                            link(dve.tensor_reduce(s["r"][:], s["t"][:], AX.X, ALU.add))
                            link(move(dve, o, s["r"][:]))

                def store(sp, s, outs):
                    sp.dma_start(t_zo.rearrange("(b p) d -> p b d", p=P), zo[:]).then_inc(outs, 16)
                    sp.dma_start(t_ao.rearrange("(b p) d -> p b d", p=P), ao_src[:]).then_inc(outs, 16)
                    return 2
                node_stage("l3o", (fill, H3), H3, tensor, vector, 8 * NBU, nothing, scratch, store=store)
            gat_scores("l3t", 1, t_ao, ao_src, ao_dst, coef[:, 8:9], coef[:, 9:10])
            oacc = zo[:].rearrange("p b d -> p (b d)")
            edge_sums("l3f", t_zo, ZW, src_i, dloc, blk_i, att, 1, ZW, oacc, 1)
            divide("l3g", zo[:].unsqueeze(2), 1)

            upd = acc[:, 0:NB * D].rearrange("p (b d) -> p b d", b=NB)
            with ExitStack() as s2:
                wih = SB(s2, "gru_wih", [P, 3 * D])
                whh = SB(s2, "gru_whh", [P, 3 * D])
                gb = SB(s2, "gru_b", [1, 2, 3 * D])
                gb_f = SB(s2, "gru_b_f", [1, 2, 3 * D])
                gb_parts = SB(s2, "gru_b_parts", [1, 3, 2, 3 * D], BF16)
                gb3 = SB(s2, "gru_b3", [3, 2, 3 * D], BF16)
                in_w, split = sem("gru_in"), sem("gru_split")
                with phase() as block:
                    @block.sync
                    def _(sp):
                        sp.dma_start(wih[:], a["L3_wih"]).then_inc(in_w, 16)
                        sp.dma_start(whh[:], a["L3_whh"]).then_inc(in_w, 16)
                        sp.dma_start(gb[:, 0, :], a["L3_bih"].unsqueeze(0)).then_inc(in_w, 16)
                        sp.dma_start(gb[:, 1, :], a["L3_bhh"].unsqueeze(0)).then_inc(in_w, 16)
                        sp.wait_ge(in_w, 64)
                        sp.wait_ge(split, 1)
                        for k in range(3):
                            sp.dma_start(gb3[k:k + 1, :, :], gb_parts[:, k, :, :]).then_inc(in_w, 16)
                        sp.wait_ge(in_w, 64 + 48)

                    @block.vector
                    def _(dve):
                        dve.wait_ge(in_w, 64)
                        split3(dve, Chain(dve, "gru_split_step").link, gb[:], gb_f[:],
                               [gb_parts[:, k, :, :] for k in range(3)])
                        dve.sem_inc(split, 1)

                def scratch(s_):
                    s = {"ps": PS(s_, "gru_ps", [P, NBU, 512]), "rz": SB(s_, "gru_rz", [P, NBU, 2 * D]),
                         "n": SB(s_, "gru_n", [P, NBU, D]), "d": SB(s_, "gru_d", [P, NBU, D])}
                    for k in ("mm", "gates", "pre", "new"):
                        s[k] = sem("gru_" + k)
                    return s

                def fill(pool, link, stage, i):
                    link(pool.tensor_copy(stage[:, 0:NBU, :], zo[:, bass.ds(i * NBU, NBU), 0:D]))
                    link(pool.tensor_copy(stage[:, NBU:2 * NBU, :], X[:, bass.ds(i * NBU, NBU), :]))

                def tensor(pe, s, i, xt):
                    for u in range(NBU):
                        o = s["ps"][:, u, :]
                        pe.matmul(o[:, 0:256], lhsT=ones_bf[0:3, :], rhs=gb3[:, 0, 0:256], start=True, stop=False)
                        pe.matmul(o[:, 0:256], lhsT=ones_bf[0:3, :], rhs=gb3[:, 1, 0:256], start=False, stop=False)
                        pe.matmul(o[:, 0:256], lhsT=xt[:, u, :], rhs=wih[:, 0:256], start=False, stop=False)
                        pe.matmul(o[:, 0:256], lhsT=xt[:, NBU + u, :], rhs=whh[:, 0:256], start=False, stop=True)
                        for k, (w, x0) in enumerate(((wih, 0), (whh, NBU))):
                            v = o[:, 256 + k * D:256 + (k + 1) * D]
                            pe.matmul(v, lhsT=ones_bf[0:3, :], rhs=gb3[:, k, 256:384], start=True, stop=False)
                            ins = pe.matmul(v, lhsT=xt[:, x0 + u, :], rhs=w[:, 256:384], start=False, stop=True)
                    ins.then_inc(s["mm"], 1)

                def scalar(act, link, s, i):
                    act.wait_ge(s["mm"], i + 1)
                    link(act.activation(s["rz"][:], s["ps"][:, :, 0:256], ACT.Sigmoid))
                    act.sem_inc(s["gates"], 1)
                    act.wait_ge(s["pre"], i + 1)
                    link(act.activation(s["n"][:], s["d"][:], ACT.Tanh))
                    act.sem_inc(s["new"], 1)

                def vector(dve, link, s, i):
                    dve.wait_ge(s["gates"], i + 1)
                    link(dve.tensor_tensor(s["d"][:], s["rz"][:, :, 0:D], s["ps"][:, :, 384:512], ALU.mult))
                    link(dve.tensor_tensor(s["d"][:], s["d"][:], s["ps"][:, :, 256:384], ALU.add))
                    dve.sem_inc(s["pre"], 1)
                    dve.wait_ge(s["new"], i + 1)
                    x = X[:, bass.ds(i * NBU, NBU), :]
                    link(dve.tensor_tensor(s["d"][:], x, s["n"][:], ALU.subtract))
                    link(dve.tensor_tensor(s["d"][:], s["d"][:], s["rz"][:, :, D:2 * D], ALU.mult))
                    link(dve.tensor_tensor(s["d"][:], s["d"][:], s["n"][:], ALU.add))
                    link(dve.scalar_tensor_tensor(upd[:, bass.ds(i * NBU, NBU), :], s["d"][:], 0.01, s["d"][:],
                                                  ALU.mult, ALU.max))
                node_stage("gru", (fill, 2), 2, tensor, vector, 6, scalar, scratch, n_scalar=2)
            add_norm("l3y", upd, False, last=True)



def kernel(**inputs):
    import numpy as np
    import concourse.bacc as _bacc
    from concourse import mybir as _mybir
    from concourse.bass_utils import run_bass_kernel_spmd as _run

    i = {k: np.asarray(v) for k, v in inputs.items()}
    pad = TR * P - N_EDGES

    def tiled(v, fill):
        v = np.pad(v, [(0, pad)] + [(0, 0)] * (v.ndim - 1), constant_values=fill)
        return np.ascontiguousarray(np.swapaxes(v.reshape((TR, P) + v.shape[1:]), 0, 1))

    line = np.pad(i["dst"], (0, pad + 1), constant_values=NP)
    arrays = {
        "x": np.pad(i["x"], [(0, NP - N_NODES), (0, 0)]),
        "src": tiled(i["src"], -1), "dst": tiled(i["dst"], -1), "typ": tiled(i["edge_type_3"], 0),
        "w": tiled(i["edge_weight"], 0), "w1": tiled(i["edge_weight1"][:, 0], 0),
        "f": tiled(i["edge_attr3_1x32"][:, 0, :], 0),
        "dst_line": np.ascontiguousarray(np.stack([line[p * TR:(p + 1) * TR + 1] for p in range(P)])),
        "L0_w": i["L0_gnn_weight"],
    }
    for k in ("Wk", "Wq"):
        arrays["L1_" + k] = np.ascontiguousarray(i["L1_gnn_" + k].T)
    for k in ("Wv", "bk", "bq", "bv", "rel_msg"):
        arrays["L1_" + k] = i["L1_gnn_" + k]
    arrays["L1_rel"] = i["L1_gnn_rel_att"].reshape(D)
    for k in ("W_in", "Wf1", "bf1", "Wf2", "bf2", "Wo1", "bo1", "Wo2", "bo2"):
        arrays["L2_" + k] = i["L2_gnn_" + k]
    arrays["L3_fc"] = np.ascontiguousarray(i["L3_gnn_fc_W"].transpose(2, 0, 1).reshape(D, H3 * D))
    arrays["L3_at"] = np.ascontiguousarray(i["L3_gnn_attn_W"].reshape(H3, 2, D).transpose(1, 0, 2).reshape(2 * H3 * D))
    arrays["L3_ew"] = i["L3_gnn_edge_w"].reshape(H3)
    arrays["L3_mw"] = i["L3_gnn_m_w"].reshape(H3)
    arrays["L3_ofc"] = np.ascontiguousarray(i["L3_gnn_out_fc_W"].T.reshape(H3, D, D).transpose(1, 0, 2))
    arrays["L3_oat"] = i["L3_gnn_out_attn_W"].reshape(2 * D)
    arrays["L3_oew"] = i["L3_gnn_out_edge_w"].reshape(1)
    arrays["L3_omw"] = i["L3_gnn_out_m_w"].reshape(1)
    arrays["L3_wih"] = np.ascontiguousarray(i["L3_gnn_gru_Wih"].T)
    arrays["L3_whh"] = np.ascontiguousarray(i["L3_gnn_gru_Whh"].T)
    arrays["L3_bih"] = i["L3_gnn_gru_bih"]
    arrays["L3_bhh"] = i["L3_gnn_gru_bhh"]

    nc = _bacc.Bacc("TRN2", target_bir_lowering=False, num_devices=1)
    aps, feeds = {}, {}
    for k, v in arrays.items():
        feeds["in_" + k] = np.ascontiguousarray(v)
        aps[k] = nc.dram_tensor("in_" + k, v.shape, _mybir.dt.from_np(v.dtype), kind="ExternalInput").ap()
    out = nc.dram_tensor("out_0", (N_NODES, D), _mybir.dt.float32, kind="ExternalOutput").ap()
    gnn_program(nc, aps, out)
    return _run(nc, [feeds], core_ids=[0]).results[0]["out_0"]
```
